# Optimizing a Trainium2 kernel written in Bass

```python
import numpy as np
import jax
import jax.numpy as jnp

def _softmax(x, axis=-1):
    return jax.nn.softmax(x, axis=axis)

def _gelu(x):
    return jax.nn.gelu(x, approximate=True)

def _silu(x):
    return jax.nn.silu(x)

def _sigmoid(x):
    return jax.nn.sigmoid(x)

def _layernorm(x, axis=-1, eps=1e-05):
    m = jnp.mean(x, axis=axis, keepdims=True)
    v = jnp.var(x, axis=axis, keepdims=True)
    return (x - m) / jnp.sqrt(v + eps)

def _scatter_add(tgt, idx, src, axis=0):
    return tgt.at[idx].add(src)

def _segment_sum(src, seg, n):
    return jax.ops.segment_sum(src, seg, n)
kernel_name = 'mk_gnn_ffn_d2_gnn_r32_d45c2d'

def setup_inputs(seed: int=0):
    np.random.seed(seed)
    _w = jnp.asarray

    def _rec_inputs():
        import jax
        import jax.numpy as jnp
        _gk = jax.random.key(seed)
        x = -0.0002928 + 1 * jax.random.normal(jax.random.fold_in(_gk, 1), (256, 512), jnp.float32)
        _s = jax.random.randint(jax.random.fold_in(_gk, 2), (2048,), 0, 256, jnp.int32)
        _d = jax.random.randint(jax.random.fold_in(_gk, 3), (2048,), 0, 256, jnp.int32)
        _loop = jnp.arange(256, dtype=jnp.int32)
        src = jnp.concatenate([_s, _d, _loop])
        dst = jnp.concatenate([_d, _s, _loop])
        _o = jnp.argsort(dst, stable=True)
        src = src[_o]
        dst = dst[_o]
        edge_type_32 = jax.random.randint(jax.random.fold_in(_gk, 13), (4352,), 0, 32, jnp.int32)
        edge_weight1 = jax.random.uniform(jax.random.fold_in(_gk, 14), (4352, 1), jnp.float32, 0.0, 0.999996)
        return (x, src, dst, edge_type_32, edge_weight1)
    x, src, dst, edge_type_32, edge_weight1 = _rec_inputs()

    def _L0_gnn_setup():
        import jax, jax.numpy as jnp
        import numpy as np
        N_NODES = 256
        N_EDGES = 8192
        D_IN = 512
        D_OUT = 512
        key = jax.random.key(seed)
        k1, k2, k3 = jax.random.split(key, 3)
        x = jax.random.normal(k1, (N_NODES, D_IN), dtype=jnp.float32)
        edge_index = jax.random.randint(k2, (2, N_EDGES), 0, N_NODES, dtype=jnp.int64)
        weight = jax.random.normal(k3, (D_IN, D_OUT), dtype=jnp.float32)
        bias = jnp.zeros((D_OUT,), dtype=jnp.float32)
        return {'x': x, 'edge_index': edge_index, 'weight': weight, 'bias': bias}
    _L0_gnn_all = _L0_gnn_setup()
    _L0_gnn_in = {k: v for k, v in _L0_gnn_all.items() if k in ('weight', 'bias')}
    del _L0_gnn_all

    def _L0_ffn_setup():
        import jax, jax.numpy as jnp
        import numpy as np
        DIM = 512
        MOE_DIM = 256
        E = 64
        G = 8
        TOPK_G = 4
        K = 8
        SCALE = 2.5
        CAP = 1024

        def _gate(x2, gate_w, gate_b):
            T = x2.shape[0]
            scores = jax.nn.sigmoid(x2 @ gate_w.T)
            s = (scores + gate_b).reshape(T, G, E // G)
            group_scores = jax.lax.top_k(s, 2)[0].sum(-1)
            top_groups = jax.lax.top_k(group_scores, TOPK_G)[1]
            gmask = jnp.zeros((T, G), bool).at[jnp.arange(T)[:, None], top_groups].set(True)
            s = jnp.where(gmask[..., None], s, -jnp.inf).reshape(T, E)
            idx = jax.lax.top_k(s, K)[1]
            w = jnp.take_along_axis(scores, idx, axis=1)
            w = w / w.sum(-1, keepdims=True) * SCALE
            return (w, idx)

        def _moe_forward(x, gate_w, gate_b, w1, w3, w2):
            shape = x.shape
            x2 = x.reshape(-1, DIM)
            T = x2.shape[0]
            w, idx = _gate(x2, gate_w, gate_b)
            flat_e = idx.reshape(-1)
            oh = (flat_e[:, None] == jnp.arange(E)[None, :]).astype(jnp.int32)
            pos = (jnp.cumsum(oh, axis=0) * oh).sum(-1) - 1
            x_rep = jnp.repeat(x2, K, axis=0)
            xb = jnp.zeros((E, CAP, DIM), x2.dtype).at[flat_e, pos].set(x_rep, mode='drop')
            h = jax.nn.silu(jnp.einsum('ecd,edm->ecm', xb, w1)) * jnp.einsum('ecd,edm->ecm', xb, w3)
            yb = jnp.einsum('ecm,emd->ecd', h, w2)
            y = yb.at[flat_e, pos].get(mode='fill', fill_value=0.0) * w.reshape(-1)[:, None]
            return y.reshape(T, K, DIM).sum(1).reshape(shape)
        key = jax.random.key(seed)
        ks = jax.random.split(key, 6)
        x = jax.random.normal(ks[0], (4, 512, DIM), jnp.float32)
        gate_w = jax.random.normal(ks[1], (E, DIM), jnp.float32) / np.sqrt(DIM).astype(np.float32)
        gate_b = jax.random.normal(ks[2], (E,), jnp.float32) * 0.01
        w1 = jax.random.normal(ks[3], (E, DIM, MOE_DIM), jnp.float32) / np.sqrt(DIM).astype(np.float32)
        w3 = jax.random.normal(ks[4], (E, DIM, MOE_DIM), jnp.float32) / np.sqrt(DIM).astype(np.float32)
        w2 = jax.random.normal(ks[5], (E, MOE_DIM, DIM), jnp.float32) / np.sqrt(MOE_DIM).astype(np.float32)
        return {'x': x, 'gate_w': gate_w, 'gate_b': gate_b, 'w1': w1, 'w3': w3, 'w2': w2}
    _L0_ffn_all = _L0_ffn_setup()
    _L0_ffn_in = {k: v for k, v in _L0_ffn_all.items() if k in ('gate_w', 'gate_b', 'w1', 'w3', 'w2')}
    del _L0_ffn_all

    def _L1_gnn_setup():
        import jax, jax.numpy as jnp
        import numpy as np
        N_NODES = 625
        N_EDGES = 10000
        IN_FEAT = 512
        OUT_FEAT = 512
        NUM_RELS = 32
        NUM_BASES = 8
        key = jax.random.key(seed)
        ks = jax.random.split(key, 8)
        x = jax.random.normal(ks[0], (N_NODES, IN_FEAT), dtype=jnp.float32)
        bases = jax.random.normal(ks[1], (NUM_BASES, IN_FEAT, OUT_FEAT), dtype=jnp.float32) * (1.0 / np.sqrt(IN_FEAT))
        w_comp = jax.random.normal(ks[2], (NUM_RELS, NUM_BASES), dtype=jnp.float32) * (1.0 / np.sqrt(NUM_BASES))
        h_bias = jnp.zeros((OUT_FEAT,), dtype=jnp.float32)
        norm = jax.random.uniform(ks[3], (N_EDGES, 1), dtype=jnp.float32)
        src = jax.random.randint(ks[4], (N_EDGES,), 0, N_NODES, dtype=jnp.int32)
        dst = jax.random.randint(ks[5], (N_EDGES,), 0, N_NODES, dtype=jnp.int32)
        etype = jnp.sort(jax.random.randint(ks[6], (N_EDGES,), 0, NUM_RELS, dtype=jnp.int32))
        return {'x': x, 'bases': bases, 'w_comp': w_comp, 'h_bias': h_bias, 'norm': norm, 'src': src, 'dst': dst, 'etype': etype}
    _L1_gnn_all = _L1_gnn_setup()
    _L1_gnn_in = {k: v for k, v in _L1_gnn_all.items() if k in ('bases', 'w_comp', 'h_bias')}
    del _L1_gnn_all

    def _L1_ffn_setup():
        import jax, jax.numpy as jnp
        import numpy as np
        BINS = jnp.array([-1.5, -1.0, -0.5, 0.0, 0.5, 1.0, 1.5], dtype=jnp.float32)
        N_BINS = BINS.shape[0] + 1
        INDEX = 0
        key = jax.random.key(seed)
        k1, k2 = jax.random.split(key)
        x = jax.random.normal(k1, (8, 128, 512), dtype=jnp.float32)
        W = jax.random.normal(k2, (N_BINS, 512, 512), dtype=jnp.float32) * 0.02
        return {'x': x, 'W': W}
    _L1_ffn_all = _L1_ffn_setup()
    _L1_ffn_in = {k: v for k, v in _L1_ffn_all.items() if k in ('W',)}
    del _L1_ffn_all
    return {'x': x, 'src': src, 'dst': dst, 'edge_type_32': edge_type_32, 'edge_weight1': edge_weight1, 'L0_gnn_weight': _L0_gnn_in['weight'], 'L0_gnn_bias': _L0_gnn_in['bias'], 'L0_ffn_gate_w': _L0_ffn_in['gate_w'], 'L0_ffn_gate_b': _L0_ffn_in['gate_b'], 'L0_ffn_w1': _L0_ffn_in['w1'], 'L0_ffn_w3': _L0_ffn_in['w3'], 'L0_ffn_w2': _L0_ffn_in['w2'], 'L1_gnn_bases': _L1_gnn_in['bases'], 'L1_gnn_w_comp': _L1_gnn_in['w_comp'], 'L1_gnn_h_bias': _L1_gnn_in['h_bias'], 'L1_ffn_W': _L1_ffn_in['W']}

def reference(x, src, dst, edge_type_32, edge_weight1, L0_gnn_weight, L0_gnn_bias, L0_ffn_gate_w, L0_ffn_gate_b, L0_ffn_w1, L0_ffn_w3, L0_ffn_w2, L1_gnn_bases, L1_gnn_w_comp, L1_gnn_h_bias, L1_ffn_W):
    import jax
    import jax.numpy as jnp

    def _L0_gnn_ref(x, edge_index, weight, bias):
        import jax, jax.numpy as jnp
        import numpy as np
        N_NODES = 256
        N_EDGES = 8192
        D_IN = 512
        D_OUT = 512
        n = x.shape[0]
        adj = jnp.zeros((n, n), dtype=x.dtype)
        adj = adj.at[edge_index[0], edge_index[1]].set(1.0)
        adj = adj.at[edge_index[1], edge_index[0]].set(1.0)
        adj = adj + jnp.eye(n, dtype=x.dtype)
        deg = jnp.sum(adj, axis=1)
        dinv = 1.0 / jnp.sqrt(deg)
        adj = adj * dinv[:, None] * dinv[None, :]
        return adj @ (x @ weight) + bias

    def _L0_ffn_ref(x, gate_w, gate_b, w1, w3, w2):
        import jax, jax.numpy as jnp
        import numpy as np
        DIM = 512
        MOE_DIM = 256
        E = 64
        G = 8
        TOPK_G = 4
        K = 8
        SCALE = 2.5
        CAP = 1024

        def _gate(x2, gate_w, gate_b):
            T = x2.shape[0]
            scores = jax.nn.sigmoid(x2 @ gate_w.T)
            s = (scores + gate_b).reshape(T, G, E // G)
            group_scores = jax.lax.top_k(s, 2)[0].sum(-1)
            top_groups = jax.lax.top_k(group_scores, TOPK_G)[1]
            gmask = jnp.zeros((T, G), bool).at[jnp.arange(T)[:, None], top_groups].set(True)
            s = jnp.where(gmask[..., None], s, -jnp.inf).reshape(T, E)
            idx = jax.lax.top_k(s, K)[1]
            w = jnp.take_along_axis(scores, idx, axis=1)
            w = w / w.sum(-1, keepdims=True) * SCALE
            return (w, idx)

        def _moe_forward(x, gate_w, gate_b, w1, w3, w2):
            shape = x.shape
            x2 = x.reshape(-1, DIM)
            T = x2.shape[0]
            w, idx = _gate(x2, gate_w, gate_b)
            flat_e = idx.reshape(-1)
            oh = (flat_e[:, None] == jnp.arange(E)[None, :]).astype(jnp.int32)
            pos = (jnp.cumsum(oh, axis=0) * oh).sum(-1) - 1
            x_rep = jnp.repeat(x2, K, axis=0)
            xb = jnp.zeros((E, CAP, DIM), x2.dtype).at[flat_e, pos].set(x_rep, mode='drop')
            h = jax.nn.silu(jnp.einsum('ecd,edm->ecm', xb, w1)) * jnp.einsum('ecd,edm->ecm', xb, w3)
            yb = jnp.einsum('ecm,emd->ecd', h, w2)
            y = yb.at[flat_e, pos].get(mode='fill', fill_value=0.0) * w.reshape(-1)[:, None]
            return y.reshape(T, K, DIM).sum(1).reshape(shape)
        return _moe_forward(x, gate_w, gate_b, w1, w3, w2)

    def _L1_gnn_ref(x, bases, w_comp, h_bias, norm, src, dst, etype):
        import jax, jax.numpy as jnp
        import numpy as np
        N_NODES = 625
        N_EDGES = 10000
        IN_FEAT = 512
        OUT_FEAT = 512
        NUM_RELS = 32
        NUM_BASES = 8
        n_nodes = x.shape[0]
        weight = jnp.einsum('rb,bio->rio', w_comp, bases)
        h_rel = jnp.einsum('ni,rio->rno', x, weight)
        msg = h_rel[etype, src] * norm
        out = jax.ops.segment_sum(msg, dst, num_segments=n_nodes)
        out = out + h_bias
        return out

    def _L1_ffn_ref(x, W):
        import jax, jax.numpy as jnp
        import numpy as np
        BINS = jnp.array([-1.5, -1.0, -0.5, 0.0, 0.5, 1.0, 1.5], dtype=jnp.float32)
        N_BINS = BINS.shape[0] + 1
        INDEX = 0
        y = x[..., INDEX]
        mem = jnp.sum(y[..., None] > BINS, axis=-1)
        B, T, D = x.shape
        xf = x.reshape(B * T, D)
        memf = mem.reshape(B * T)
        out = jnp.zeros((B * T, W.shape[-1]), dtype=x.dtype)
        for k in range(N_BINS):
            sel = (memf == k)[:, None].astype(x.dtype)
            out = out + sel * (xf @ W[k])
        return out.reshape(B, T, W.shape[-1])
    edge_index = jnp.stack([src, dst])
    x = x + _L0_gnn_ref(_layernorm(x, axis=-1), edge_index, L0_gnn_weight, L0_gnn_bias)
    x = x + _L0_ffn_ref(_layernorm(x, axis=-1)[None], L0_ffn_gate_w, L0_ffn_gate_b, L0_ffn_w1, L0_ffn_w3, L0_ffn_w2)[0]
    x = x + _L1_gnn_ref(_layernorm(x, axis=-1), L1_gnn_bases, L1_gnn_w_comp, L1_gnn_h_bias, edge_weight1, src, dst, edge_type_32)
    x = x + _L1_ffn_ref(_layernorm(x, axis=-1)[None], L1_ffn_W)[0]
    return x

_drawn_inputs = setup_inputs


def setup_inputs(seed=0):
    import zlib

    import numpy as np

    out = dict(_drawn_inputs(seed))
    spreads = {'L0_gnn_bias': (0.0, 0.284), 'L1_gnn_h_bias': (0.0, 0.296)}
    factors = {}
    for name, (base, spread) in spreads.items():
        noise = np.random.default_rng([zlib.crc32(name.encode()), seed]).standard_normal(out[name].shape)
        drawn = base * np.exp(spread * noise) if base else spread * noise
        out[name] = jnp.asarray(drawn.astype(out[name].dtype))
    for name, factor in factors.items():
        out[name] = (out[name] * factor).astype(out[name].dtype)
    return out
```

```python
import concourse.bass as bass
from concourse import mybir
from contextlib import ExitStack


def build(nc, x, src, dst, etype, ew, w0, bias0, gate_w, gate_b, w1, w3, w2, bases, w_comp, bias1, wf, out):
    fp32, bf16, i32, u32 = mybir.dt.float32, mybir.dt.bfloat16, mybir.dt.int32, mybir.dt.uint32
    ALU = mybir.AluOpType
    ACT = mybir.ActivationFunctionType
    AX = mybir.AxisListType.X

    P = 128
    N, D = x.shape
    T = N // P
    K = D // P
    EDGES = src.shape[0]
    EC = EDGES // P
    E, _, M = w1.shape
    MC = M // P
    R, B = w_comp.shape
    NBIN = wf.shape[0]
    G, TOPG, TOPK, SCALE = 8, 4, 8, 2.5
    GE = E // G
    EPS = 1e-5
    BINS = [-1.5, -1.0, -0.5, 0.0, 0.5, 1.0, 1.5]
    W = 64
    NRING = 8
    PR = NRING // 2
    ROUNDS = E // NRING
    EDGE_ROUND = 3
    NP = E // 2
    NOVMAX = 32
    NEG, TAKEN = -1.0e30, -3.0e30
    CELLS = N * N
    ROWS = CELLS + P

    table = nc.dram_tensor("cell_table", [ROWS, B], fp32, kind="Internal").ap()

    ctx = ExitStack()
    with ctx:
        def sb(name, shape, dt=fp32):
            return ctx.enter_context(nc.sbuf_tensor(name, shape, dt))

        def sem(name):
            return ctx.enter_context(nc.semaphore(name))

        ring = sb("ring", [P, NRING, 3 * 1024])
        extra = sb("extra", [P, EC * N])
        zreg = sb("zreg", [P, EDGES])
        areg = sb("areg", [P, EDGES])
        pa = sb("pair_arena", [P, 5632])
        xcur = sb("xcur", [P, T, D])
        h = sb("h", [P, T, D])
        bias1_sb = sb("bias1_sb", [P, D])
        ident = sb("ident", [P, P])
        before = sb("before", [P, P])
        onesb = sb("onesb", [P, 1], bf16)
        ones = sb("ones", [P, P])
        iota_n = sb("iota_n", [P, N], bf16)
        iota_w = sb("iota_w", [P, W])
        spare = sb("spare", [P, 1])
        src_i = sb("src_i", [P, EC], i32)
        dst_i = sb("dst_i", [P, EC], i32)
        srcf = sb("srcf", [P, EC])
        dstf = sb("dstf", [P, EC])
        key = sb("key", [P, EC])
        ew_sb = sb("ew_sb", [P, EC])
        wc_sb = sb("wc_sb", [R, B])
        coef = sb("coef", [P, EC, B])
        csum = coef
        dup = sb("dup", [P, EC])
        isdup = sb("isdup", [P, EC])
        idxf = sb("idxf", [P, EC])
        idx = sb("idx", [P, EC], u32)
        relid = sb("relid", [R, 1])
        gateb_sb = sb("gateb_sb", [P, E])
        gT = sb("gT", [P, K, E])
        sel = sb("sel", [P, T, E])
        gw = sb("gw", [P, T, E])
        rankm = sb("rankm", [P, T, E])
        gsc = sb("gsc", [P, T, 16])
        v8 = sb("v8", [P, T, 8])
        grep = sb("grep", [P, T, 16])
        gmask = sb("gmask", [P, T, G])
        gpen = sb("gpen", [P, T, G])
        den = sb("den", [P, T])
        stats = sb("stats", [P, T, 6])
        mv = sb("mv", [P, T, 2])
        rstd = sb("rstd", [P, T])
        nw_v = sb("newton_v", [P, T])
        nw_i = sb("newton_i", [P, T], i32)
        nw_t = sb("newton_t", [P, T])
        deg = sb("deg", [P, T])
        dinv = sb("dinv", [P, T])
        hscale = sb("hscale", [P, T])
        cnt = sb("cnt", [P, E])
        ovc = sb("ovc", [P, E])
        oincl = sb("oincl", [P, E])
        viota = sb("viota", [P, NOVMAX])
        ov_e = sb("ov_e", [P, NOVMAX])
        ov_k = sb("ov_k", [P, NOVMAX])
        ov_i = sb("ov_i", [P, NOVMAX + 1], i32)
        bins = sb("bins", [P, NBIN + 1])
        above = sb("above", [P, T, NBIN + 1])
        binm = sb("binm", [P, T, NBIN])

        oneh = extra[:, :].bitcast(bf16)
        S1 = oneh[:, 0:EC * N].rearrange("p (c n) -> p c n", n=N)
        D1 = oneh[:, EC * N:2 * EC * N].rearrange("p (c n) -> p c n", n=N)
        ov_tmp = extra[:, 0:NOVMAX * E].rearrange("p (v e) -> p v e", e=E)
        eqb = oneh[:, 2 * NOVMAX * E:2 * NOVMAX * E + EDGES].rearrange("p (c q) -> p c q", q=P)
        rel_i = zreg[0:R, :].bitcast(i32)
        relh = zreg[0:R, :]
        relh_c = relh.rearrange("r (p c) -> r c p", c=EC)
        keyrow = areg[:, :].rearrange("p (c q) -> p c q", q=P)
        atab = areg[:, 0:T * N * B].rearrange("p (t r) -> p t r", t=T)
        zbuf = zreg[:, 0:K * B * P].rearrange("p (k b d) -> p k b d", k=K, b=B)
        zero = pa[:, 0:ROWS * B // P // 4]
        Pb = pa[:, 0:512].rearrange("p (u t s) -> p u t s", u=2, t=T)
        Pw = pa[:, 512:1024].rearrange("p (u t s) -> p u t s", u=2, t=T)
        PT = pa[:, 1024:1536].rearrange("p (u t s) -> p u t s", u=2, t=T)
        xg = pa[:, 1536:2560].rearrange("p (u k s) -> p u k s", u=2, k=K)
        hh = pa[:, 2560:3072].rearrange("p (u i m s) -> p u i m s", u=2, i=2, m=MC)
        sg = pa[:, 3072:3328].rearrange("p (i m s) -> p i m s", i=2, m=MC)
        yT = pa[:, 3584:4608].rearrange("p (u j s) -> p u j s", u=2, j=K)
        yy = pa[:, 4608:5632].rearrange("p (u d) -> p u d", u=2)
        hT = pa[:, 1536:2560].rearrange("p (k n) -> p k n", k=K)
        adj = pa[:, 2560:3072].rearrange("p (t n) -> p t n", t=T)
        gate_sb = pa[0:E, 2048:2560]
        s = pa[:, 2560:2688].rearrange("p (t e) -> p t e", t=T)
        rep = pa[:, 2688:2816].rearrange("p (t e) -> p t e", t=T)
        m8 = pa[:, 2816:2944].rearrange("p (g i) -> p g i", i=8)
        scores = pa[:, 2944:3072].rearrange("p (t e) -> p t e", t=T)
        w0_sb = pa[:, 3584:5632].rearrange("p (k o) -> p k o", k=K)
        bias0_sb = pa[:, 3072:3584]
        hm = pa[:, 3584:5632].rearrange("p (u k n) -> p u k n", u=2, k=K)

        def basis(b):
            flat = extra[:, b * 2048:(b + 1) * 2048] if b < 4 else ring[:, b - 4, 0:2048]
            return flat.rearrange("p (k o) -> p k o", k=K)

        def wf_half(b, half):
            if b < 4:
                return ring[:, 4 + b, half * 1024:(half + 1) * 1024].rearrange("p (k o) -> p k o", k=2)
            return ring[:, 2 * (b - 4) + half, 2048:3072].rearrange("p (k o) -> p k o", k=2)

        ps = ctx.enter_context(nc.psum_tensor("ps", [P, 8, 512], fp32))

        s_x, s_w0, s_edges, s_ew, s_wc, s_rel = (sem(n) for n in (
            "x_loaded", "w0_loaded", "edges_loaded", "ew_loaded", "wcomp_loaded", "relations_loaded"))
        s_gate, s_gateb, s_b0, s_b1 = (sem(n) for n in ("gate_loaded", "gateb_loaded", "bias0_loaded", "bias1_loaded"))
        s_slot = [sem(f"slot{i}_loaded") for i in range(NRING)]
        s_base = [sem(f"basis{b}_loaded") for b in range(B)]
        s_wf = [sem(f"binmat{b}_loaded") for b in range(NBIN)]
        s_zeroset, s_zeroed, s_cellsum, s_scat, s_atab = (sem(n) for n in (
            "zero_set", "table_zeroed", "cell_sums_made", "scattered", "table_loaded"))
        s_const, s_dve, s_pool = sem("constants_made"), sem("dve_chain"), sem("pool_chain")
        s_key, s_onehot, s_keyrow, s_keyrow_sb, s_eq, s_relh = (sem(n) for n in (
            "key_made", "onehots_made", "keyrow_done", "keyrow_copied", "equalities_made", "relation_onehot_made"))
        s_coefps, s_coef, s_csps = sem("coef_product"), sem("coef_made"), sem("cellsum_product")
        s_C, s_adj, s_T0, s_T0sb, s_o0, s_h1, s_hT, s_hTsb = (sem(n) for n in (
            "links_counted", "adj_made", "adj_h_product", "adj_h_copied", "gcn_product", "h1_made", "hT_done", "hT_copied"))
        s_gT, s_gTsb, s_logit, s_score, s_sel, s_rank, s_route, s_ovtab = (sem(n) for n in (
            "gateT_done", "gateT_copied", "logits_done", "scores_made", "selected", "ranks_done", "routed", "overflow_listed"))
        s_P, s_Pw, s_PTp, s_xgp, s_PT, s_xg = (sem(n) for n in (
            "onehot_made", "weighted_made", "transposed_done", "gather_done", "transposed_copied", "gathered_copied"))
        s_up, s_silu, s_hh, s_yT, s_yTp, s_y, s_comb = (sem(n) for n in (
            "up_done", "silu_made", "hidden_made", "yT_copied", "y_transposed", "y_copied", "combined"))
        s_used = sem("experts_used")
        o_w, o_P, o_PTp, o_xgp, o_PT, o_xg, o_up, o_silu, o_hh, o_down, o_yT, o_yTp, o_y, o_done = (
            sem("over_" + n) for n in ("loaded", "onehot", "transposed", "gather", "PT_copied", "xg_copied", "up",
                                       "silu", "hidden", "down", "yT_copied", "y_transposed", "y_copied", "done"))
        s_h2, s_zp, s_zuse, s_h3, s_h3T, s_h3Tsb = (sem(n) for n in (
            "h2_made", "ah_product", "ah_used", "h3_made",
            "h3T_done", "h3T_copied"))
        s_mb, s_hm, s_mrow, s_fp, s_fin, s_out = (sem(n) for n in (
            "mask_rows_done", "masked_made", "mask_row_done", "binned_product", "result_made", "result_stored"))
        s_z = [sem("ah_copied_by_vector"), sem("ah_copied_by_scalar")]

        block = ctx.enter_context(nc.Block())

        @block.sync
        def _(sp):
            sp.dma_start(xcur[:, :, :], x.rearrange("(t p) d -> p t d", p=P)).then_inc(s_x, 16)
            sp.dma_start(w0_sb, w0.rearrange("(p k) o -> p k o", k=K)).then_inc(s_w0, 16)

            def load_expert(slot, e, done):
                s0 = ring[:, slot, :]
                one = bass.ds(e, 1)
                sp.dma_start(s0[:, 0:1024], w1[one].rearrange("a (p k) m -> p (a k m)", k=K)).then_inc(done, 16)
                sp.dma_start(s0[:, 1024:2048], w3[one].rearrange("a (p k) m -> p (a k m)", k=K)).then_inc(done, 16)
                sp.dma_start(s0[:, 2048:3072], w2[one].rearrange("a (p k) m -> p (a k m)", k=MC)).then_inc(done, 16)

            for slot in range(NRING):
                load_expert(slot, slot, s_slot[slot])
            with sp.Fori(1, ROUNDS) as r:
                for slot in range(NRING):
                    sp.wait_ge(s_used, NRING * (r - 1) + slot + 1)
                    load_expert(slot, r * NRING + slot, s_slot[slot])

            sp.wait_ge(s_ovtab, 1)
            nov = sp.value_load(ov_i[0:1, NOVMAX:NOVMAX + 1], min_val=0, max_val=NOVMAX - 1)
            sp.wait_ge(s_used, E - NRING + 1)
            with sp.If(nov > 0):
                with sp.Fori(0, nov) as v:
                    e = sp.value_load(ov_i[0:1, bass.ds(v, 1)], min_val=0, max_val=E - 1)
                    sp.wait_ge(o_done, v + 1)
                    load_expert(0, e, o_w)
            basis_v = bases.rearrange("b (p k) o -> b p k o", k=K)
            wf_v = wf.rearrange("b (p k) o -> b p k o", k=K)
            for b in range(4):
                sp.dma_start(basis(b), basis_v[b]).then_inc(s_base[b], 16)
            sp.wait_ge(o_done, nov + 1)
            for b in range(4, B):
                sp.wait_ge(s_used, E - NRING + (b - 4) + 1)
                sp.dma_start(basis(b), basis_v[b]).then_inc(s_base[b], 16)
            for b in range(NBIN):
                if b < 4:
                    sp.wait_ge(s_used, E - NRING + 4 + b + 1)
                for half in range(2):
                    sp.dma_start(wf_half(b, half), wf_v[b][:, 2 * half:2 * half + 2, :]).then_inc(s_wf[b], 16)
            for t in range(T):
                sp.wait_ge(s_fin, t + 1)
                sp.dma_start(out[t * P:(t + 1) * P, :], xcur[:, t, :]).then_inc(s_out, 16)
            sp.wait_ge(s_out, 16 * T)

        @block.gpsimd
        def _(pool):
            gp = nc.gpsimd
            chain = [0]

            def link(ins):
                chain[0] += 1
                ins.then_inc(s_pool, 1)
                pool.wait_ge(s_pool, chain[0])

            gp.iota(iota_n[:, :], [[1, N]], base=0, channel_multiplier=0, allow_small_or_imprecise_dtypes=True)
            gp.iota(iota_w[:, :], [[1, W]], base=0, channel_multiplier=0, allow_small_or_imprecise_dtypes=True)
            gp.iota(spare[:, :], [[1, 1]], base=CELLS, channel_multiplier=1, allow_small_or_imprecise_dtypes=True)
            gp.iota(relid[:, :], [[1, 1]], base=0, channel_multiplier=1, allow_small_or_imprecise_dtypes=True)
            gp.iota(viota[:, :], [[1, NOVMAX]], base=0, channel_multiplier=0, allow_small_or_imprecise_dtypes=True)
            gp.memset(gsc[:, :, :], NEG)
            for i, edge in enumerate(BINS):
                gp.memset(bins[:, i + 1:i + 2], edge)
            link(gp.memset(ones[:, :], 1.0))
            gp.memset(onesb[:, :], 1.0)
            gp.affine_select(out=ident[:, :], in_=ones[:, :], compare_op=ALU.is_equal, fill=0.0, base=0,
                             pattern=[[-1, P]], channel_multiplier=1)
            gp.affine_select(out=before[:, :], in_=ones[:, :], compare_op=ALU.is_gt, fill=0.0, base=0,
                             pattern=[[1, P]], channel_multiplier=-1).then_inc(s_const, 1)
            gp.memset(zero, 0.0).then_inc(s_zeroset, 1)
            pool.wait_ge(s_rel, 16)
            pool.wait_ge(s_const, 1)
            gp.tensor_scalar(relh, rel_i, relid[:, 0:1], None, ALU.is_equal).then_inc(s_relh, 1)
            pool.wait_ge(s_key, 1)
            for c in range(EC):
                if c % 4 == 0:
                    pool.wait_ge(s_keyrow_sb, c // 4 + 1)
                last = gp.tensor_scalar(keyrow[:, c, :], keyrow[:, c, :], key[:, c:c + 1], None, ALU.is_equal)
            link(last)
            pool.wait_ge(s_C, 1)
            gp.tensor_tensor(eqb, keyrow, before[:, :].unsqueeze(1).to_broadcast([P, EC, P]),
                             ALU.mult).then_inc(s_eq, 1)
            pool.wait_ge(s_zeroed, 64)
            pool.wait_ge(s_cellsum, 1)
            link(gp.tensor_scalar(isdup[:, :], dup[:, :], 0.0, None, ALU.is_gt))
            link(gp.tensor_scalar(idxf[:, :], key[:, :], spare[:, 0:1], None, ALU.subtract))
            link(gp.tensor_tensor(idxf[:, :], idxf[:, :], isdup[:, :], ALU.mult))
            link(gp.tensor_tensor(idxf[:, :], key[:, :], idxf[:, :], ALU.subtract))
            link(gp.tensor_copy(idx[:, :], idxf[:, :]))
            for c in range(EC):
                gp.indirect_dma_start(out=table, out_offset=bass.IndirectOffsetOnAxis(ap=idx[:, c:c + 1], axis=0),
                                      in_=csum[:, c, :], in_offset=None, compute_op=ALU.add).then_inc(s_scat, 16)
                pool.wait_ge(s_scat, 16 * (c + 1))
            pool.dma_start(atab, table[0:CELLS, :].rearrange("(t p d) b -> p t (d b)", t=T, p=P)).then_inc(s_atab, 16)

        @block.scalar
        def _(act):
            sc = nc.scalar
            ints = "(p c) -> p c"
            act.dma_start(src_i[:, :], src.rearrange(ints, c=EC)).then_inc(s_edges, 16)
            act.dma_start(dst_i[:, :], dst.rearrange(ints, c=EC)).then_inc(s_edges, 16)
            act.dma_start(rel_i, etype.rearrange("(a e) -> a e", a=1).broadcast_to([R, EDGES])).then_inc(s_rel, 16)
            act.dma_start(wc_sb[:, :], w_comp).then_inc(s_wc, 16)
            act.dma_start(ew_sb[:, :], ew.rearrange("(p c) a -> p (c a)", c=EC)).then_inc(s_ew, 16)
            act.dma_start(gate_sb, gate_w).then_inc(s_gate, 16)
            act.dma_start(gateb_sb[:, :], gate_b.rearrange("(a e) -> a e", a=1).broadcast_to([P, E])).then_inc(s_gateb, 16)
            act.dma_start(bias0_sb, bias0.rearrange("(a e) -> a e", a=1).broadcast_to([P, D])).then_inc(s_b0, 16)
            act.dma_start(bias1_sb[:, :], bias1.rearrange("(a e) -> a e", a=1).broadcast_to([P, D])).then_inc(s_b1, 16)
            act.wait_ge(s_zeroset, 1)
            tz = table.rearrange("(p r) b -> p (r b)", p=P)
            q = ROWS * B // P // 4
            for i in range(4):
                act.dma_start(tz[:, i * q:(i + 1) * q], zero).then_inc(s_zeroed, 16)
            for g in range((EC + 3) // 4):
                n = min(4, EC - 4 * g)
                act.wait_ge(s_keyrow, g + 1)
                sc.copy(areg[:, g * 512:g * 512 + n * P], ps[:, g % 2, 0:n * P]).then_inc(s_keyrow_sb, 1)
            act.wait_ge(s_T0, 1)
            sc.copy(hT[:, 0:2, :], ps[:, 2, :].rearrange("p (k n) -> p k n", k=2)).then_inc(s_T0sb, 1)
            act.wait_ge(s_gT, 1)
            sc.copy(gT[:, :, :], ps[:, 4, 0:K * E].rearrange("p (k e) -> p k e", k=K)).then_inc(s_gTsb, 1)
            act.wait_ge(s_hT, 1)
            sc.copy(hT[:, 0:2, :], ps[:, 2, :].rearrange("p (k n) -> p k n", k=2)).then_inc(s_hTsb, 1)
            act.wait_ge(s_logit, 1)
            sc.activation(scores[:, :, :], ps[:, 4, 0:T * E].rearrange("p (t e) -> p t e", t=T),
                          ACT.Sigmoid).then_inc(s_score, 1)

            def early(p, n):
                return isinstance(p, int) and p < n

            def copy_gathered(p, u):
                act.wait_ge(s_xgp, p + 1)
                if not early(p, 2):
                    act.wait_ge(s_up, 2 * (p - 1))
                sc.copy(xg[:, u], ps[:, 0, :].rearrange("p (k s) -> p k s", k=K)).then_inc(s_xg, 1)

            def copy_weights(p, u):
                act.wait_ge(s_PTp, p + 1)
                if not early(p, 2):
                    act.wait_ge(s_comb, p - 1)
                sc.copy(PT[:, u], ps[:, 1, 0:T * P].rearrange("p (t s) -> p t s", t=T)).then_inc(s_PT, 1)

            def silu(p, i):
                act.wait_ge(s_up, 2 * p + i + 1)
                if not early(p, 1):
                    act.wait_ge(s_hh, 2 * (p - 1) + i + 1)
                sc.activation(sg[:, i], ps[:, 2 + i, 0:MC * W].rearrange("p (m s) -> p m s", m=MC),
                              ACT.Silu).then_inc(s_silu, 1)

            def round_(r, last=False):
                for j in range(PR):
                    p = r * PR + j
                    u = j % 2
                    more = not (last and j == PR - 1)
                    silu(p, 0)
                    if more:
                        copy_gathered(p + 1, 1 - u)
                    silu(p, 1)
                    if more:
                        copy_weights(p + 1, 1 - u)
                    act.wait_ge(s_used, 2 * p + 2)
                    if not early(p, 2):
                        act.wait_ge(s_yTp, p - 1)
                    sc.copy(yT[:, u], ps[:, 4, :].rearrange("p (j s) -> p j s", j=K)).then_inc(s_yT, 1)

            copy_weights(0, 0)
            copy_gathered(0, 0)
            round_(0)
            with act.Fori(1, ROUNDS - 1) as r:
                round_(r)
            round_(ROUNDS - 1, last=True)

            act.wait_ge(s_ovtab, 1)
            nov = act.value_load(ov_i[0:1, NOVMAX:NOVMAX + 1], min_val=0, max_val=NOVMAX - 1)
            act.wait_ge(s_comb, NP)
            with act.If(nov > 0):
                with act.Fori(0, nov) as v:
                    act.wait_ge(o_PTp, v + 1)
                    sc.copy(PT[0:W, 0], ps[0:W, 1, 0:T * P].rearrange("p (t s) -> p t s", t=T)).then_inc(o_PT, 1)
                    act.wait_ge(o_xgp, v + 1)
                    sc.copy(xg[:, 0, :, 0:W], ps[:, 0, 0:K * W].rearrange("p (k s) -> p k s", k=K)).then_inc(o_xg, 1)
                    act.wait_ge(o_up, v + 1)
                    sc.activation(sg[:, 0], ps[:, 2, 0:MC * W].rearrange("p (m s) -> p m s", m=MC),
                                  ACT.Silu).then_inc(o_silu, 1)
                    act.wait_ge(o_down, v + 1)
                    sc.copy(yT[:, 0, :, 0:W], ps[:, 4, 0:K * W].rearrange("p (k s) -> p k s", k=K)).then_inc(o_yT, 1)

            for g in range(1, T * K * 2, 2):
                t, k = g // (2 * K), (g // 2) % K
                act.wait_ge(s_zp, g + 1)
                if t > 0:
                    act.wait_ge(s_zuse, t)
                sc.copy(zbuf[:, k, :, 64:128], ps[:, g % 4, :].rearrange("p (d b) -> p b d", b=B)).then_inc(s_z[1], 1)
            act.wait_ge(s_h3T, 1)
            sc.copy(hT[:, 0:2, :], ps[:, 4, :].rearrange("p (k n) -> p k n", k=2)).then_inc(s_h3Tsb, 1)

        @block.vector
        def _(dve):
            v_ = nc.vector
            chain = [0]

            def link(ins):
                chain[0] += 1
                ins.then_inc(s_dve, 1)
                dve.wait_ge(s_dve, chain[0])

            dve.wait_ge(s_edges, 32)
            v_.tensor_copy(dstf[:, :], dst_i[:, :])
            link(v_.tensor_copy(srcf[:, :], src_i[:, :]))
            v_.scalar_tensor_tensor(out=key[:, :], in0=srcf[:, :], scalar=float(N), in1=dstf[:, :],
                                    op0=ALU.mult, op1=ALU.add).then_inc(s_key, 1)
            dve.wait_ge(s_const, 1)
            with dve.Fori(0, EC) as c:
                one = bass.ds(c, 1)
                v_.tensor_scalar(S1[:, one, :], iota_n[:, :], srcf[:, one], None, ALU.is_equal)
                v_.tensor_scalar(D1[:, one, :], iota_n[:, :], dstf[:, one], None, ALU.is_equal).then_inc(s_onehot, 1)

            def rsqrt(out_, in_, add):
                link(v_.tensor_scalar(nw_v[:, :], in_, add, None, ALU.add))
                link(v_.tensor_scalar(nw_i[:, :], nw_v[:, :].bitcast(i32), 1, None, ALU.logical_shift_right))
                link(v_.tensor_scalar(out_.bitcast(i32), nw_i[:, :], -1.0, float(0x5F3759DF), ALU.mult, ALU.add))
                for _ in range(3):
                    link(v_.scalar_tensor_tensor(out=nw_t[:, :], in0=out_, scalar=-0.5, in1=nw_v[:, :],
                                                 op0=ALU.mult, op1=ALU.mult))
                    link(v_.tensor_tensor(nw_t[:, :], nw_t[:, :], out_, ALU.mult))
                    link(v_.scalar_tensor_tensor(out=out_, in0=nw_t[:, :], scalar=1.5, in1=out_,
                                                 op0=ALU.add, op1=ALU.mult))

            def norm_stats():
                for t in range(T):
                    link(v_.bn_stats(stats[:, t, :], xcur[:, t, :]))
                for t in range(T):
                    link(v_.bn_aggr(mv[:, t, :], stats[:, t, :]))
                rsqrt(rstd[:, :], mv[:, :, 1], EPS)

            dve.wait_ge(s_x, 16)
            norm_stats()
            dve.wait_ge(s_C, 1)
            for t in range(T):
                link(v_.tensor_scalar(adj[:, t, :], ps[:, 2 + t, 0:N], 1.0, 0.0, ALU.min, ALU.add,
                                      accum_out=deg[:, t:t + 1]))
            for t in range(T):
                blk = adj[:, t, t * P:(t + 1) * P]
                v_.tensor_tensor(blk, blk, ident[:, :], ALU.add)
            rsqrt(dinv[:, :], deg[:, :], 1.0)
            link(v_.tensor_tensor(hscale[:, :], rstd[:, :], dinv[:, :], ALU.mult))
            for t in range(T):
                last = v_.tensor_scalar(h[:, t, :], xcur[:, t, :], mv[:, t, 0:1], hscale[:, t:t + 1],
                                        ALU.subtract, ALU.mult)
            last.then_inc(s_adj, 1)
            dve.wait_ge(s_adj, 1)
            dve.wait_ge(s_b0, 16)
            for t in range(T):
                link(v_.tensor_tensor(xcur[:, t, :], xcur[:, t, :], bias0_sb, ALU.add))
            dve.wait_ge(s_T0, 1)
            v_.tensor_copy(hT[:, 2:4, :], ps[:, 3, :].rearrange("p (k n) -> p k n", k=2)).then_inc(s_T0sb, 1)
            for t in range(T):
                dve.wait_ge(s_o0, t + 1)
                link(v_.scalar_tensor_tensor(out=xcur[:, t, :], in0=ps[:, 5 + t, :], scalar=dinv[:, t:t + 1],
                                             in1=xcur[:, t, :], op0=ALU.mult, op1=ALU.add))
            norm_stats()
            for t in range(T):
                last = v_.tensor_scalar(h[:, t, :], xcur[:, t, :], mv[:, t, 0:1], rstd[:, t:t + 1],
                                        ALU.subtract, ALU.mult)
            last.then_inc(s_h1, 1)
            dve.wait_ge(s_hT, 1)
            v_.tensor_copy(hT[:, 2:4, :], ps[:, 3, :].rearrange("p (k n) -> p k n", k=2)).then_inc(s_hTsb, 1)

            dve.wait_ge(s_score, 1)
            dve.wait_ge(s_gateb, 16)
            for t in range(T):
                link(v_.tensor_tensor(s[:, t, :], scores[:, t, :], gateb_sb[:, :], ALU.add))
            for t in range(T):
                for g in range(G):
                    last = v_.max(m8[:, t * G + g, :], s[:, t, g * GE:(g + 1) * GE])
            link(last)
            link(v_.tensor_tensor(gsc[:, :, 0:G], m8[:, :, 0].rearrange("p (t g) -> p t g", t=T),
                                  m8[:, :, 1].rearrange("p (t g) -> p t g", t=T), ALU.add))
            for t in range(T):
                link(v_.max(v8[:, t, :], gsc[:, t, 0:G]))
            link(v_.memset(v8[:, :, TOPG:8], NEG))
            for t in range(T):
                link(v_.match_replace(out=grep[:, t, :], in_to_replace=v8[:, t, :], in_values=gsc[:, t, :],
                                      imm_value=TAKEN))
            link(v_.tensor_scalar(gmask[:, :, :], grep[:, :, 0:G], 2 * NEG, None, ALU.is_lt))
            link(v_.tensor_scalar(gpen[:, :, :], gmask[:, :, :], 1.0, -NEG, ALU.subtract, ALU.mult))
            sv = s[:, :, :].rearrange("p t (g e) -> p (t g) e", g=G)
            gmv = gmask[:, :, :].rearrange("p t g -> p (t g)").unsqueeze(2).to_broadcast([P, T * G, GE])
            gpv = gpen[:, :, :].rearrange("p t g -> p (t g)").unsqueeze(2).to_broadcast([P, T * G, GE])
            link(v_.tensor_tensor(sv, sv, gmv, ALU.mult))
            link(v_.tensor_tensor(sv, sv, gpv, ALU.add))
            for t in range(T):
                link(v_.max(v8[:, t, :], s[:, t, :]))
                link(v_.match_replace(out=rep[:, t, :], in_to_replace=v8[:, t, :], in_values=s[:, t, :],
                                      imm_value=TAKEN))
            v_.tensor_scalar(sel[:, :, :], rep[:, :, :], 2 * NEG, None, ALU.is_lt).then_inc(s_sel, 1)
            dve.wait_ge(s_sel, 1)
            link(v_.tensor_tensor(gw[:, :, :], scores[:, :, :], sel[:, :, :], ALU.mult))
            link(v_.tensor_reduce(den[:, :], gw[:, :, :], AX, ALU.add))
            link(v_.reciprocal(den[:, :], den[:, :]))
            for t in range(T):
                link(v_.tensor_scalar(gw[:, t, :], gw[:, t, :], den[:, t:t + 1], SCALE, ALU.mult, ALU.mult))
            dve.wait_ge(s_rank, 1)
            link(v_.scalar_tensor_tensor(out=rankm[:, :, :], in0=ps[:, 5, 0:T * E].rearrange("p (t e) -> p t e", t=T),
                                         scalar=1.0, in1=sel[:, :, :], op0=ALU.add, op1=ALU.mult))
            link(v_.tensor_scalar(rankm[:, :, :], rankm[:, :, :], -1.0, None, ALU.add))
            link(v_.tensor_copy(cnt[:, :], ps[:, 5, T * E:T * E + E]))

            iota_b = iota_w[:, :].unsqueeze(1).to_broadcast([P, 2, W])

            def early(p, n):
                return isinstance(p, int) and p < n

            def make_onehots(p, u):
                if not early(p, 2):
                    dve.wait_ge(s_xgp, p - 1)
                for t in range(T):
                    ranks = rankm[:, t, bass.ds(2 * p, 2)].unsqueeze(2).to_broadcast([P, 2, W])
                    last = v_.tensor_tensor(Pb[:, u, t].rearrange("p (i s) -> p i s", i=2), iota_b, ranks, ALU.is_equal)
                last.then_inc(s_P, 1)
                dve.wait_ge(s_P, p + 1)
                for t in range(T):
                    weights = gw[:, t, bass.ds(2 * p, 2)].unsqueeze(2).to_broadcast([P, 2, W])
                    last = v_.tensor_tensor(Pw[:, u, t].rearrange("p (i s) -> p i s", i=2),
                                            Pb[:, u, t].rearrange("p (i s) -> p i s", i=2), weights, ALU.mult)
                last.then_inc(s_Pw, 1)

            def hidden(p, u, i):
                dve.wait_ge(s_silu, 2 * p + i + 1)
                if not early(p, 2):
                    dve.wait_ge(s_used, 2 * (p - 1))
                v_.tensor_tensor(hh[:, u, i], sg[:, i],
                                 ps[:, 2 + i, 128:128 + MC * W].rearrange("p (m s) -> p m s", m=MC),
                                 ALU.mult).then_inc(s_hh, 1)

            def copy_y(p, u):
                dve.wait_ge(s_yTp, p + 1)
                if not early(p, 2):
                    dve.wait_ge(s_comb, p - 1)
                v_.tensor_copy(yy[:, u, :], ps[:, 5, :]).then_inc(s_y, 1)

            def round_(r, last=False):
                for j in range(PR):
                    p = r * PR + j
                    u = j % 2
                    if not (last and j >= PR - 2):
                        make_onehots(p + 2, u)
                    for i in range(2):
                        hidden(p, u, i)
                    if not early(p, 1):
                        copy_y(p - 1, 1 - u)

            dve.wait_ge(s_zeroed, 64)
            make_onehots(0, 0)
            make_onehots(1, 1)
            round_(0)
            dve.wait_ge(s_coefps, 1)
            dve.wait_ge(s_ew, 16)
            v_.tensor_tensor(coef[:, :, :], ps[:, 5, 0:EC * B].rearrange("p (c b) -> p c b", b=B),
                             ew_sb[:, :].unsqueeze(2).to_broadcast([P, EC, B]), ALU.mult).then_inc(s_coef, 1)
            link(v_.tensor_scalar(ovc[:, :], cnt[:, :], float(W), None, ALU.is_gt))
            for q in range(2, N // W):
                link(v_.scalar_tensor_tensor(out=ovc[:, :], in0=cnt[:, :], scalar=float(W * q), in1=ovc[:, :],
                                             op0=ALU.is_gt, op1=ALU.add))
            link(v_.tensor_tensor_scan(out=oincl[:, :], data0=ones[:, 0:E], data1=ovc[:, :], initial=0.0,
                                       op0=ALU.mult, op1=ALU.add))
            incl_b = oincl[:, :].unsqueeze(1).to_broadcast([P, NOVMAX, E])
            v_b = viota[:, :].unsqueeze(2).to_broadcast([P, NOVMAX, E])
            dve.wait_ge(s_C, 1)
            link(v_.tensor_tensor(ov_tmp, incl_b, v_b, ALU.is_le))
            link(v_.tensor_reduce(ov_e[:, :], ov_tmp, AX, ALU.add))
            link(v_.tensor_tensor(ov_tmp, ov_tmp, ovc[:, :].unsqueeze(1).to_broadcast([P, NOVMAX, E]), ALU.mult))
            link(v_.tensor_reduce(ov_k[:, :], ov_tmp, AX, ALU.add))
            link(v_.tensor_tensor(ov_k[:, :], viota[:, :], ov_k[:, :], ALU.subtract))
            link(v_.tensor_scalar(ov_k[:, :], ov_k[:, :], 1.0, float(W), ALU.add, ALU.mult))
            v_.tensor_copy(ov_i[:, 0:NOVMAX], ov_e[:, :]).then_inc(o_done, 1)
            v_.tensor_copy(ov_i[:, NOVMAX:NOVMAX + 1], oincl[:, E - 1:E]).then_inc(s_ovtab, 1)
            with dve.Fori(1, EDGE_ROUND) as r:
                round_(r)
            dve.wait_ge(s_csps, 1)
            v_.tensor_copy(dup[:, :], ps[:, 5, EC * B:EC * (B + 1)])
            v_.tensor_copy(csum[:, :, :], ps[:, 5, 0:EC * B].rearrange("p (c b) -> p c b", b=B)).then_inc(s_cellsum, 1)
            with dve.Fori(EDGE_ROUND, ROUNDS - 1) as r:
                round_(r)
            round_(ROUNDS - 1, last=True)
            copy_y(NP - 1, (NP - 1) % 2)

            dve.wait_ge(s_ovtab, 1)
            nov = dve.value_load(ov_i[0:1, NOVMAX:NOVMAX + 1], min_val=0, max_val=NOVMAX - 1)
            dve.wait_ge(s_comb, NP)
            with dve.If(nov > 0):
                with dve.Fori(0, nov) as v:
                    e = dve.value_load(ov_i[0:1, bass.ds(v, 1)], min_val=0, max_val=E - 1)
                    for t in range(T):
                        last = v_.scalar_tensor_tensor(
                            out=Pb[:, 0, t, 0:W], in0=rankm[:, t, bass.ds(e, 1)].to_broadcast([P, W]),
                            scalar=ov_k[:, bass.ds(v, 1)], in1=iota_w[:, :], op0=ALU.subtract, op1=ALU.is_equal)
                    last.then_inc(o_P, 1)
                    dve.wait_ge(o_P, 2 * v + 1)
                    for t in range(T):
                        last = v_.tensor_scalar(Pw[:, 0, t, 0:W], Pb[:, 0, t, 0:W], gw[:, t, bass.ds(e, 1)], None, ALU.mult)
                    last.then_inc(o_P, 1)
                    dve.wait_ge(o_silu, v + 1)
                    v_.tensor_tensor(hh[:, 0, 0], sg[:, 0],
                                     ps[:, 2, 128:128 + MC * W].rearrange("p (m s) -> p m s", m=MC),
                                     ALU.mult).then_inc(o_hh, 1)
                    dve.wait_ge(o_yTp, v + 1)
                    v_.tensor_copy(yy[0:W, 0, :], ps[0:W, 5, :]).then_inc(o_y, 1)
                    dve.wait_ge(o_done, v + 2)

            dve.wait_ge(s_comb, NP)
            for t in range(T):
                link(v_.tensor_tensor(xcur[:, t, :], xcur[:, t, :], ps[:, 6 + t, :], ALU.add))
            norm_stats()
            for t in range(T):
                last = v_.tensor_scalar(h[:, t, :], xcur[:, t, :], mv[:, t, 0:1], rstd[:, t:t + 1],
                                        ALU.subtract, ALU.mult)
            last.then_inc(s_h2, 1)
            dve.wait_ge(s_b1, 16)
            for t in range(T):
                link(v_.tensor_tensor(xcur[:, t, :], xcur[:, t, :], bias1_sb[:, :], ALU.add))
            for g in range(0, T * K * 2, 2):
                t, k = g // (2 * K), (g // 2) % K
                dve.wait_ge(s_zp, g + 1)
                if t > 0:
                    dve.wait_ge(s_zuse, t)
                v_.tensor_copy(zbuf[:, k, :, 0:64], ps[:, g % 4, :].rearrange("p (d b) -> p b d", b=B)).then_inc(s_z[0], 1)
            for t in range(T):
                dve.wait_ge(s_zuse, t + 1)
                link(v_.tensor_tensor(xcur[:, t, :], xcur[:, t, :], ps[:, 4 + t, :], ALU.add))
            norm_stats()
            for t in range(T):
                last = v_.tensor_scalar(h[:, t, :], xcur[:, t, :], mv[:, t, 0:1], rstd[:, t:t + 1],
                                        ALU.subtract, ALU.mult)
            last.then_inc(s_h3, 1)
            dve.wait_ge(s_h3, 1)
            link(v_.memset(above[:, :, 0:1], 1.0))
            link(v_.memset(above[:, :, NBIN:NBIN + 1], 0.0))
            for t in range(T):
                link(v_.tensor_scalar(above[:, t, 1:NBIN], bins[:, 1:NBIN], h[:, t, 0:1], None, ALU.is_lt))
            link(v_.tensor_tensor(binm[:, :, :], above[:, :, 0:NBIN], above[:, :, 1:NBIN + 1], ALU.subtract))
            for b in range(NBIN):
                for t in range(T):
                    last = v_.tensor_scalar(areg[:, (b * T + t) * P:(b * T + t + 1) * P], ident[:, :],
                                            binm[:, t, b:b + 1], None, ALU.mult)
            last.then_inc(s_mb, 1)
            dve.wait_ge(s_h3T, 1)
            v_.tensor_copy(hT[:, 2:4, :], ps[:, 5, :].rearrange("p (k n) -> p k n", k=2)).then_inc(s_h3Tsb, 1)
            dve.wait_ge(s_h3Tsb, 2)
            for b in range(NBIN):
                dve.wait_ge(s_mrow, 2 * (b // 2) + 2)
                if b >= 2:
                    dve.wait_ge(s_fp, b - 1)
                v_.tensor_tensor(hm[:, b % 2], hT[:, :, :], ps[:, b // 2, (b % 2) * N:(b % 2 + 1) * N].unsqueeze(1)
                                 .to_broadcast([P, K, N]), ALU.mult).then_inc(s_hm, 1)
            dve.wait_ge(s_fp, NBIN)
            for t in range(T):
                v_.tensor_tensor(xcur[:, t, :], xcur[:, t, :], ps[:, 6 + t, :], ALU.add).then_inc(s_fin, 1)

        @block.tensor
        def _(pe):
            mm = nc.tensor.matmul
            tr = nc.tensor.transpose

            pe.wait_ge(s_key, 1)
            pe.wait_ge(s_const, 1)
            for c in range(EC):
                g = c // 4
                if c % 4 == 0 and g >= 2:
                    pe.wait_ge(s_keyrow_sb, g - 1)
                last = mm(ps[:, g % 2, (c % 4) * P:(c % 4 + 1) * P], key[:, c:c + 1].to_broadcast([P, P]),
                          ident[:, :], start=True, stop=True)
                if c % 4 == 3 or c == EC - 1:
                    last.then_inc(s_keyrow, 1)
            def count(c, one, start, stop):
                pe.wait_ge(s_onehot, c + 1)
                for t in range(T):
                    half = slice(t * P, (t + 1) * P)
                    mm(ps[:, 2 + t, 0:N], S1[:, one, half], D1[:, one, :], start=start, stop=False)
                    last = mm(ps[:, 2 + t, 0:N], D1[:, one, half], S1[:, one, :], start=False, stop=stop)
                return last

            count(0, 0, True, False)
            with pe.Fori(1, EC - 1) as c:
                count(c, bass.ds(c, 1), False, False)
            count(EC - 1, EC - 1, False, True).then_inc(s_C, 1)
            pe.wait_ge(s_gate, 16)
            for k in range(K):
                last = tr(ps[:, 4, k * E:(k + 1) * E], gate_sb[:, k::K], ident[0:E, 0:E])
            last.then_inc(s_gT, 1)
            pe.wait_ge(s_adj, 1)
            for k in range(K):
                for t in range(T):
                    last = mm(ps[:, 2 + k // 2, (k % 2) * N:(k % 2 + 1) * N], h[:, t, k::K], adj[:, t, :],
                              start=t == 0, stop=t == T - 1)
            last.then_inc(s_T0, 1)
            pe.wait_ge(s_T0sb, 2)
            pe.wait_ge(s_w0, 16)
            for t in range(T):
                for k in range(K):
                    last = mm(ps[:, 5 + t, :], hT[:, k, t * P:(t + 1) * P], w0_sb[:, k, :],
                              start=k == 0, stop=k == K - 1)
                last.then_inc(s_o0, 1)

            def transpose_h(bank, done):
                for k in range(K):
                    for t in range(T):
                        o = (k % 2) * N + t * P
                        last = tr(ps[:, bank + k // 2, o:o + P], h[:, t, k::K], ident[:, :])
                last.then_inc(done, 1)

            pe.wait_ge(s_h1, 1)
            transpose_h(2, s_hT)
            pe.wait_ge(s_hTsb, 2)
            pe.wait_ge(s_gTsb, 1)
            for t in range(T):
                for k in range(K):
                    last = mm(ps[:, 4, t * E:(t + 1) * E], hT[:, k, t * P:(t + 1) * P], gT[:, k, :],
                              start=k == 0, stop=k == K - 1)
            last.then_inc(s_logit, 1)
            pe.wait_ge(s_sel, 1)
            mm(ps[:, 5, 0:E], before[:, :], sel[:, 0, :], start=True, stop=True)
            mm(ps[:, 5, E:2 * E], before[:, :], sel[:, 1, :], start=True, stop=False)
            mm(ps[:, 5, E:2 * E], ones[:, :], sel[:, 0, :], start=False, stop=True)
            mm(ps[:, 5, 2 * E:3 * E], ones[:, :], sel[:, 0, :], start=True, stop=False)
            mm(ps[:, 5, 2 * E:3 * E], ones[:, :], sel[:, 1, :], start=False, stop=True).then_inc(s_rank, 1)

            def gather(p, u):
                pe.wait_ge(s_Pw, p + 1)
                pe.wait_ge(s_PT, p)
                for t in range(T):
                    last = tr(ps[:, 1, t * P:(t + 1) * P], Pw[:, u, t, :], ident[:, :])
                last.then_inc(s_PTp, 1)
                for k in range(K):
                    for t in range(T):
                        last = mm(ps[:, 0, k * P:(k + 1) * P], h[:, t, k::K], Pb[:, u, t, :],
                                  start=t == 0, stop=t == T - 1)
                last.then_inc(s_xgp, 1)

            def up(w, tokens, bank):
                for mat in range(2):
                    wv = ring[:, w, mat * 1024:(mat + 1) * 1024].rearrange("p (k q m) -> p k q m", k=K, m=MC)
                    for m in range(MC):
                        o = mat * 128 + m * W
                        for k in range(K):
                            last = mm(ps[:, bank, o:o + W], wv[:, k, :, m], tokens[:, k, :],
                                      start=k == 0, stop=k == K - 1)
                return last

            def down(w, hidden, off, width):
                wv = ring[:, w, 2048:3072].rearrange("p (m d) -> p m d", m=MC)
                for j in range(K):
                    for m in range(MC):
                        o = j * width + off
                        last = mm(ps[:, 4, o:o + W], wv[:, m, j * P:(j + 1) * P], hidden[:, m, :],
                                  start=m == 0, stop=m == MC - 1)
                return last

            def transpose_y(p, u):
                pe.wait_ge(s_yT, p + 1)
                for j in range(K):
                    last = tr(ps[:, 5, j * P:(j + 1) * P], yT[:, u, j, :], ident[:, :])
                last.then_inc(s_yTp, 1)

            def combine(p, u, start):
                pe.wait_ge(s_y, p + 1)
                for t in range(T):
                    last = mm(ps[:, 6 + t, :], PT[:, u, t, :], yy[:, u, :], start=start, stop=True,
                              skip_group_check=True)
                last.then_inc(s_comb, 1)

            def round_(r, last=False):
                for j in range(PR):
                    p = r * PR + j
                    u = j % 2
                    start = isinstance(p, int) and p == 0
                    for i in range(2):
                        w = 2 * j + i
                        pe.wait_ge(s_slot[w], 48 * (r + 1))
                        if i == 0:
                            pe.wait_ge(s_xg, p + 1)
                        up(w, xg[:, u, :, i * W:(i + 1) * W], 2 + i).then_inc(s_up, 1)
                        if i == 0 and not (last and j == PR - 1):
                            gather(p + 1, 1 - u)
                    if not start:
                        transpose_y(p - 1, 1 - u)
                    for i in range(2):
                        w = 2 * j + i
                        pe.wait_ge(s_hh, 2 * p + i + 1)
                        down(w, hh[:, u, i], i * W, 2 * W).then_inc(s_used, 1)
                        if i == 0 and not start:
                            combine(p - 1, 1 - u, isinstance(p, int) and p == 1)

            gather(0, 0)
            round_(0)
            pe.wait_ge(s_relh, 1)
            pe.wait_ge(s_wc, 16)
            for c in range(EC):
                last = mm(ps[:, 5, c * B:(c + 1) * B], relh_c[:, c, :], wc_sb[:, :], start=True, stop=True)
            last.then_inc(s_coefps, 1)
            pe.wait_ge(s_coef, 1)
            with pe.Fori(1, EDGE_ROUND) as r:
                round_(r)
            pe.wait_ge(s_eq, 1)
            for c in range(EC):
                last = mm(ps[:, 5, c * B:(c + 1) * B], keyrow[:, c, :], coef[:, c, :], start=True, stop=True)
            for c in range(EC):
                last = mm(ps[:, 5, EC * B + c:EC * B + c + 1], eqb[:, c, :], onesb[:, :], start=True, stop=True)
            last.then_inc(s_csps, 1)
            pe.wait_ge(s_cellsum, 1)
            with pe.Fori(EDGE_ROUND, ROUNDS - 1) as r:
                round_(r)
            round_(ROUNDS - 1, last=True)
            transpose_y(NP - 1, (NP - 1) % 2)
            combine(NP - 1, (NP - 1) % 2, False)

            pe.wait_ge(s_ovtab, 1)
            nov = pe.value_load(ov_i[0:1, NOVMAX:NOVMAX + 1], min_val=0, max_val=NOVMAX - 1)
            with pe.If(nov > 0):
                with pe.Fori(0, nov) as v:
                    pe.wait_ge(o_P, 2 * v + 2)
                    for t in range(T):
                        last = tr(ps[:, 1, t * P:(t + 1) * P], Pw[:, 0, t, :], ident[:, :])
                    last.then_inc(o_PTp, 1)
                    for k in range(K):
                        for t in range(T):
                            last = mm(ps[:, 0, k * W:(k + 1) * W], h[:, t, k::K], Pb[:, 0, t, 0:W],
                                      start=t == 0, stop=t == T - 1)
                    last.then_inc(o_xgp, 1)
                    pe.wait_ge(o_w, 48 * (v + 1))
                    pe.wait_ge(o_xg, v + 1)
                    up(0, xg[:, 0, :, 0:W], 2).then_inc(o_up, 1)
                    pe.wait_ge(o_hh, v + 1)
                    down(0, hh[:, 0, 0], 0, W).then_inc(o_down, 1)
                    pe.wait_ge(o_yT, v + 1)
                    for j in range(K):
                        last = tr(ps[:, 5, j * P:(j + 1) * P], yT[:, 0, j, :], ident[:, :])
                    last.then_inc(o_yTp, 1)
                    pe.wait_ge(o_y, v + 1)
                    pe.wait_ge(o_PT, v + 1)
                    for t in range(T):
                        last = mm(ps[:, 6 + t, :], PT[0:W, 0, t, :], yy[0:W, 0, :], start=False, stop=True,
                                  skip_group_check=True)
                    last.then_inc(o_done, 1)

            pe.wait_ge(s_h2, 1)
            pe.wait_ge(s_atab, 16)
            for t in range(T):
                for k in range(K):
                    for half in range(2):
                        g = t * 2 * K + 2 * k + half
                        if g >= 4:
                            pe.wait_ge(s_z[half], g // 2 - 1)
                        for st in range(T):
                            o = t * P * B + half * 512
                            last = mm(ps[:, g % 4, :], h[:, st, k::K], atab[:, st, o:o + 512],
                                      start=st == 0, stop=st == T - 1)
                        last.then_inc(s_zp, 1)
                pe.wait_ge(s_z[0], K * (t + 1))
                pe.wait_ge(s_z[1], K * (t + 1))
                for b in range(B):
                    pe.wait_ge(s_base[b], 16)
                    for k in range(K):
                        last = mm(ps[:, 4 + t, :], zbuf[:, k, b, :], basis(b)[:, k, :],
                                  start=b == 0 and k == 0, stop=b == B - 1 and k == K - 1)
                last.then_inc(s_zuse, 1)

            pe.wait_ge(s_h3, 1)
            transpose_h(4, s_h3T)
            pe.wait_ge(s_mb, 1)
            for b in range(NBIN):
                for t in range(T):
                    last = mm(ps[:, b // 2, (b % 2) * N + t * P:(b % 2) * N + (t + 1) * P], ones[:, :],
                              areg[:, (b * T + t) * P:(b * T + t + 1) * P], start=True, stop=True)
                last.then_inc(s_mrow, 1)
            for b in range(NBIN):
                pe.wait_ge(s_hm, b + 1)
                pe.wait_ge(s_wf[b], 32)
                for t in range(T):
                    for k in range(K):
                        last = mm(ps[:, 6 + t, :], hm[:, b % 2, k, t * P:(t + 1) * P], wf_half(b, k // 2)[:, k % 2, :],
                                  start=b == 0 and k == 0, stop=b == NBIN - 1 and k == K - 1)
                last.then_inc(s_fp, 1)


_INS = ["x", "src", "dst", "edge_type_32", "edge_weight1", "L0_gnn_weight", "L0_gnn_bias", "L0_ffn_gate_w",
        "L0_ffn_gate_b", "L0_ffn_w1", "L0_ffn_w3", "L0_ffn_w2", "L1_gnn_bases", "L1_gnn_w_comp",
        "L1_gnn_h_bias", "L1_ffn_W"]


def kernel(**inputs):
    import numpy as _np
    import concourse.bacc as _bacc
    from concourse import mybir as _mybir
    from concourse.bass_utils import run_bass_kernel_spmd as _run

    nc = _bacc.Bacc("TRN2", target_bir_lowering=False, num_devices=1)
    arrays, args = {}, []
    for name in _INS:
        a = _np.ascontiguousarray(inputs[name])
        arrays[f"in_{name}_dram"] = a
        args.append(nc.dram_tensor(f"in_{name}_dram", a.shape, _mybir.dt.from_np(a.dtype), kind="ExternalInput").ap())
    n, d = arrays["in_x_dram"].shape
    res = nc.dram_tensor("out_0_dram", (n, d), _mybir.dt.float32, kind="ExternalOutput").ap()
    build(nc, *args, res)
    r = _run(nc, [arrays], core_ids=[0])
    return r.results[0]["out_0_dram"]
```

```python
import concourse.bass as bass
from concourse import mybir
from contextlib import ExitStack


def build(nc, x, src, dst, etype, ew, w0, bias0, gate_w, gate_b, w1, w3, w2, bases, w_comp, bias1, wf, out):
    fp32, bf16, i32, u32 = mybir.dt.float32, mybir.dt.bfloat16, mybir.dt.int32, mybir.dt.uint32
    f32r = mybir.dt.float32r
    ALU = mybir.AluOpType
    ACT = mybir.ActivationFunctionType
    AX = mybir.AxisListType.X

    P = 128
    N, D = x.shape
    T = N // P
    K = D // P
    EDGES = src.shape[0]
    EC = EDGES // P
    E, _, M = w1.shape
    MC = M // P
    R, B = w_comp.shape
    NBIN = wf.shape[0]
    G, TOPG, TOPK, SCALE = 8, 4, 8, 2.5
    GE = E // G
    EPS = 1e-5
    BINS = [-1.5, -1.0, -0.5, 0.0, 0.5, 1.0, 1.5]
    W = 64
    NRING = 4
    PR = 4
    ROUNDS = E // 2 // PR
    EDGE_ROUND = 2
    U = K * D
    NP = E // 2
    NOVMAX = 32
    NEG, TAKEN = -1.0e30, -3.0e30
    CELLS = N * N
    ROWS = CELLS + P

    table = nc.dram_tensor("cell_table", [ROWS, B], fp32, kind="Internal").ap()

    ctx = ExitStack()
    with ctx:
        def sb(name, shape, dt=fp32):
            return ctx.enter_context(nc.sbuf_tensor(name, shape, dt))

        def sem(name):
            return ctx.enter_context(nc.semaphore(name))

        raw = sb("raw", [P, NRING, U])
        raw2 = sb("raw2", [P, NRING, M * D // P])
        whi = sb("whi", [P, 2, U + M * D // P], f32r)
        wlo = sb("wlo", [P, 2, U + M * D // P], f32r)
        fr = sb("split_arena", [P, 6144], f32r)
        extra = sb("extra", [P, EDGES])
        areg = sb("areg", [P, EDGES])
        pa = sb("pair_arena", [P, 5121 + 1024])
        xcur = sb("xcur", [P, T, D])
        h = sb("h", [P, T, D])
        bias1_sb = sb("bias1_sb", [P, D])
        ident = sb("ident", [P, P])
        before = sb("before", [P, P])
        onesb = sb("onesb", [P, 1], bf16)
        ones = sb("ones", [P, P])
        iota_n = sb("iota_n", [P, N], bf16)
        iota_w = sb("iota_w", [P, W])
        identb = sb("identb", [P, P], bf16)
        pidx = sb("pidx", [P, 1])
        gwb = sb("gw_thirds", [P, T, E, 3], bf16)
        gw_r = sb("gw_rest", [P, T, E])
        gs = sb("slot_weight", [P, 1])
        osel = sb("osel", [P, E])
        ov_d = sb("ov_d", [P, 2 * NOVMAX])
        spare = sb("spare", [P, 1])
        src_i = sb("src_i", [P, EC], i32)
        dst_i = sb("dst_i", [P, EC], i32)
        srcf = sb("srcf", [P, EC])
        dstf = sb("dstf", [P, EC])
        key = sb("key", [P, EC])
        ew_sb = sb("ew_sb", [P, EC])
        wc_sb = sb("wc_sb", [R, B])
        coef = sb("coef", [P, EC, B])
        csum = coef
        dup = sb("dup", [P, EC])
        isdup = sb("isdup", [P, EC])
        idxf = sb("idxf", [P, EC])
        idx = sb("idx", [P, EC], u32)
        gateb_sb = sb("gateb_sb", [P, E])
        gT = sb("gT", [P, K, E])
        sel = sb("sel", [P, T, E])
        gw = sb("gw", [P, T, E])
        rankm = sb("rankm", [P, T, E])
        gsc = sb("gsc", [P, T, 16])
        v8 = sb("v8", [P, T, 8])
        grep = sb("grep", [P, T, 16])
        gmask = sb("gmask", [P, T, G])
        gpen = sb("gpen", [P, T, G])
        den = sb("den", [P, T])
        stats = sb("stats", [P, T, 6])
        mv = sb("mv", [P, T, 2])
        rstd = sb("rstd", [P, T])
        nw_v = sb("newton_v", [P, T])
        nw_i = sb("newton_i", [P, T], i32)
        nw_t = sb("newton_t", [P, T])
        deg = sb("deg", [P, T])
        dinv = sb("dinv", [P, T])
        hscale = sb("hscale", [P, T])
        cnt = sb("cnt", [P, E])
        ovc = sb("ovc", [P, E])
        oincl = sb("oincl", [P, E])
        ov_e = sb("ov_e", [P, 1])
        ov_m = sb("ov_m", [P, 1])
        ov_k = sb("ov_k", [P, NOVMAX])
        ov_i = sb("ov_i", [P, NOVMAX + 1], i32)
        bins = sb("bins", [P, NBIN + 1])
        above = sb("above", [P, T, NBIN + 1])
        binm = sb("binm", [P, T, NBIN])

        NH = EC // 2
        oneh = extra[:, 0:NH * N].bitcast(bf16)
        S1 = oneh[:, 0:NH * N].rearrange("p (c n) -> p c n", n=N)
        D1 = oneh[:, NH * N:2 * NH * N].rearrange("p (c n) -> p c n", n=N)
        eqb = extra[:, 2048:2048 + EDGES // 2].bitcast(bf16).rearrange("p (c q) -> p c q", q=P)
        rel_v = raw[:, 1:4, :].rearrange("p a b -> p (a b)")[0:R, 0:EDGES]
        rel_i = rel_v.bitcast(i32)
        relh = rel_v
        relh_c = relh.rearrange("r (p c) -> r c p", c=EC)
        keyrow = areg[:, :].rearrange("p (c q) -> p c q", q=P)
        atab = areg[:, 0:T * N * B].rearrange("p (t d b) -> p t d b", t=T, b=B)
        zero = pa[:, 0:ROWS * B // P // 8]
        hT = pa[:, 1537:2561].rearrange("p (k n) -> p k n", k=K)
        adj = pa[:, 2561:3073].rearrange("p (t n) -> p t n", t=T)
        links = pa[:, 513:1025].rearrange("p (t n) -> p t n", t=T)
        gate_sb = pa[0:E, 5121:5121 + D]
        y0 = pa[:, 5121:5121 + T * D].rearrange("p (t o) -> p t o", t=T)
        s = pa[:, 2561:2689].rearrange("p (t e) -> p t e", t=T)
        rep = pa[:, 2689:2817].rearrange("p (t e) -> p t e", t=T)
        m8 = pa[:, 2817:2945].rearrange("p (g i) -> p g i", i=8)
        scores = pa[:, 2945:3073].rearrange("p (t e) -> p t e", t=T)
        w0_sb = pa[:, 3073:5121].rearrange("p (k o) -> p k o", k=K)
        bias0_sb = pa[:, 1025:1537]
        Pb = pa[:, 0:256].bitcast(bf16).rearrange("p (u t s) -> p u t s", u=2, t=T)
        sg = pa[:, 256:512]
        hid = pa[:, 512:768]
        hb = pa[:, 3073:4609].bitcast(bf16).rearrange("p (i t d) -> p i t d", i=3, t=T)
        h_r = extra[:, 0:T * D].rearrange("p (t d) -> p t d", t=T)
        xw = pa[:, 1792:2048].rearrange("p (k s) -> p k s", k=K)
        hw = pa[:, 2048:2176].rearrange("p (m s) -> p m s", m=MC)
        PTw = pa[:, 2304:2560]
        yw = pa[:, 2560:3072]
        xg = fr[:, 0:3072].rearrange("p (u h k s) -> p u h k s", u=2, h=2, k=K)
        hiT = fr[:, 3072:3840].rearrange("p (h m s) -> p h m s", h=2, m=MC)
        PT = fr[:, 3840:4352].rearrange("p (u t s) -> p u t s", u=2, t=T)
        yy = fr[:, 4352:5376].rearrange("p (h d) -> p h d", h=2)
        zz = fr[:, 0:4096].rearrange("p (u h k n) -> p u h k n", u=2, h=2, k=K)
        mrow = extra[:, 0:NBIN * N].rearrange("p (b n) -> p b n", b=NBIN)
        hT3 = fr[:, 4096:6144].rearrange("p (h k n) -> p h k n", h=2, k=K)

        def own_slots(blocks):
            return blocks.rearrange("p a (j s) -> p a j s", j=3)[:, :, 0::2, :]

        ps = ctx.enter_context(nc.psum_tensor("ps", [P, 8, 512], fp32))

        s_x, s_w0, s_edges, s_ew, s_wc, s_rel = (sem(n) for n in (
            "x_loaded", "w0_loaded", "edges_loaded", "ew_loaded", "wcomp_loaded", "relations_loaded"))
        s_gate, s_gateb, s_b0, s_b1 = (sem(n) for n in ("gate_loaded", "gateb_loaded", "bias0_loaded", "bias1_loaded"))
        s_unit = [sem(f"unit{i}_loaded") for i in range(NRING)]
        s_two = [sem(f"w2_{i}_loaded") for i in range(NRING)]
        s_zeroset, s_zeroed, s_cellsum, s_scat, s_atab = (sem(n) for n in (
            "zero_set", "table_zeroed", "cell_sums_made", "scattered", "table_loaded"))
        s_const, s_dve, s_pool = sem("constants_made"), sem("dve_chain"), sem("pool_chain")
        s_key, s_onehot, s_keyrow, s_keyrow_sb, s_eq, s_relh = (sem(n) for n in (
            "key_made", "onehots_made", "keyrow_done", "keyrow_copied", "equalities_made", "relation_onehot_made"))
        s_coefps, s_coef, s_csps = sem("coef_product"), sem("coef_made"), sem("cellsum_product")
        s_adj, s_T0, s_T0sb, s_o0, s_h1, s_hT, s_hTsb = (sem(n) for n in (
            "adj_made", "adj_h_product", "adj_h_copied", "gcn_product", "h1_made", "hT_done", "hT_copied"))
        s_gT, s_gTsb, s_logit, s_score, s_sel, s_rank, s_route, s_ovtab = (sem(n) for n in (
            "gateT_done", "gateT_copied", "logits_done", "scores_made", "selected", "ranks_done", "routed", "overflow_listed"))
        s_P, s_xgp, s_xgh, s_xgl, s_PTp, s_PT = (sem(n) for n in (
            "onehot_made", "gather_done", "gathered_hi", "gathered_lo", "PT_product", "PT_copied"))
        s_uhi, s_ulo, s_uused, s_2hi, s_2lo, s_used = (sem(n) for n in (
            "unit_hi", "unit_lo", "units_used", "w2_hi", "w2_lo", "experts_used"))
        s_sg, s_hid, s_T, s_Th, s_Tl, s_gsp, s_gs = (sem(n) for n in (
            "silu_made", "hidden_made", "hidden_transposed", "hiddenT_hi", "hiddenT_lo", "slot_weight_product", "slot_weight"))
        s_yh, s_yl, s_comb, s_padded, s_h1st, s_rest, s_hb, s_ovd = (sem(n) for n in (
            "y_hi", "y_lo", "combined", "padding_zeroed", "thirds_act", "rests_pool", "h_thirds_made", "overflow_diag"))
        s_mrow_sb, s_hml, s_h0 = sem("mask_rows_copied"), sem("masked_lo_made"), sem("h0_made")
        s_ohread, s_y0, s_y0sb, s_lk, s_lkT, s_y0d = (sem(n) for n in (
            "onehots_read", "xw_product", "xw_copied", "links_copied", "links_transposed", "xw_scaled"))
        o_w, o_P, o_xgp, o_xg, o_gs, o_PT, o_up, o_silu, o_hh, o_T, o_Tc, o_down, o_y, o_done = (
            sem("over_" + n) for n in ("loaded", "onehot", "gather", "xg_copied", "slot_weight", "PT_copied", "up",
                                       "silu", "hidden", "transposed", "hiddenT_copied", "down", "y_copied", "done"))
        s_h2, s_zp, s_zhi, s_zlo, s_h3, s_h3T, s_h3Tsb = (sem(n) for n in (
            "h2_made", "ah_product", "ah_hi", "ah_lo", "h3_made",
            "h3T_done", "h3T_copied"))
        s_mb, s_hm, s_mrow, s_fin, s_out = (sem(n) for n in (
            "mask_rows_done", "masked_made", "mask_row_done", "result_made", "result_stored"))

        block = ctx.enter_context(nc.Block())

        @block.sync
        def _(sp):
            sp.dma_start(xcur[:, :, :], x.rearrange("(t p) d -> p t d", p=P)).then_inc(s_x, 16)
            sp.dma_start(w0_sb, w0.rearrange("(p k) o -> p k o", k=K)).then_inc(s_w0, 16)

            def load_unit(slot, e):
                one = bass.ds(e, 1)
                sp.dma_start(raw[:, slot, 0:U // 2], w1[one].rearrange("a (p k) m -> p (a k m)", k=K)).then_inc(s_unit[slot], 16)
                sp.dma_start(raw[:, slot, U // 2:U], w3[one].rearrange("a (p k) m -> p (a k m)", k=K)).then_inc(s_unit[slot], 16)

            def load_two(slot, e):
                sp.dma_start(raw2[:, slot, :], w2[bass.ds(e, 1)].rearrange("a (p k) m -> p (a k m)", k=MC)).then_inc(s_two[slot], 16)

            load_unit(0, 0)
            load_two(0, 0)
            load_two(1, 1)
            load_two(2, 2)
            load_two(3, 3)
            sp.wait_ge(s_coefps, 1)
            for slot in range(1, NRING):
                load_unit(slot, slot)
            with sp.Fori(1, E // NRING) as r:
                for half in range(2):
                    for slot in (2 * half, 2 * half + 1):
                        sp.wait_ge(s_ulo, 2 * (NRING * (r - 1) + slot) + 2)
                        load_unit(slot, r * NRING + slot)
                    for slot in (2 * half, 2 * half + 1):
                        sp.wait_ge(s_2lo, NRING * (r - 1) + slot + 1)
                        load_two(slot, r * NRING + slot)

            sp.wait_ge(s_ovtab, 1)
            nov = sp.value_load(ov_i[0:1, NOVMAX:NOVMAX + 1], min_val=0, max_val=NOVMAX - 1)
            with sp.If(nov > 0):
                with sp.Fori(0, nov) as v:
                    one = bass.ds(sp.value_load(ov_i[0:1, bass.ds(v, 1)], min_val=0, max_val=E - 1), 1)
                    sp.wait_ge(o_done, v + 1)
                    sp.dma_start(extra[:, 0:1024], w1[one].rearrange("a (p k) m -> p (a k m)", k=K)).then_inc(o_w, 16)
                    sp.dma_start(extra[:, 1024:2048], w3[one].rearrange("a (p k) m -> p (a k m)", k=K)).then_inc(o_w, 16)
                    sp.dma_start(extra[:, 2048:3072], w2[one].rearrange("a (p k) m -> p (a k m)", k=MC)).then_inc(o_w, 16)
            for b in range(B + NBIN):
                e = E + b
                of = bases[b] if b < B else wf[b - B]
                sp.wait_ge(s_ulo, 2 * (e - NRING) + 2)
                for half in range(2):
                    cols = slice(half * U // 2, (half + 1) * U // 2)
                    sp.dma_start(raw[:, e % NRING, cols],
                                 of.rearrange("(p k) o -> p (k o)", k=K)[:, cols]).then_inc(s_unit[e % NRING], 16)
            for t in range(T):
                sp.wait_ge(s_fin, t + 1)
                sp.dma_start(out[t * P:(t + 1) * P, :], xcur[:, t, :]).then_inc(s_out, 16)
            sp.wait_ge(s_out, 16 * T)

        @block.gpsimd
        def _(pool):
            gp = nc.gpsimd
            chain = [0]

            def link(ins):
                chain[0] += 1
                ins.then_inc(s_pool, 1)
                pool.wait_ge(s_pool, chain[0])

            gp.iota(iota_n[:, :], [[1, N]], base=0, channel_multiplier=0, allow_small_or_imprecise_dtypes=True)
            gp.iota(iota_w[:, :], [[1, W]], base=0, channel_multiplier=0, allow_small_or_imprecise_dtypes=True)
            gp.iota(spare[:, :], [[1, 1]], base=CELLS, channel_multiplier=1, allow_small_or_imprecise_dtypes=True)
            gp.iota(pidx[:, :], [[1, 1]], base=0, channel_multiplier=1, allow_small_or_imprecise_dtypes=True)
            gp.memset(gsc[:, :, :], NEG)
            for i, edge in enumerate(BINS):
                gp.memset(bins[:, i + 1:i + 2], edge)
            link(gp.memset(ones[:, :], 1.0))
            gp.memset(onesb[:, :], 1.0)
            gp.affine_select(out=ident[:, :], in_=ones[:, :], compare_op=ALU.is_equal, fill=0.0, base=0,
                             pattern=[[-1, P]], channel_multiplier=1)
            gp.affine_select(out=before[:, :], in_=ones[:, :], compare_op=ALU.is_gt, fill=0.0, base=0,
                             pattern=[[1, P]], channel_multiplier=-1).then_inc(s_const, 1)
            pool.wait_ge(s_const, 1)
            gp.tensor_copy(identb[:, :], ident[:, :]).then_inc(s_const, 1)
            gp.memset(zero, 0.0).then_inc(s_zeroset, 1)
            gp.memset(fr[:, 0:3840].bitcast(fp32), 0.0).then_inc(s_padded, 1)
            pool.wait_ge(s_rel, 16)
            pool.wait_ge(s_const, 1)
            gp.tensor_scalar(relh, rel_i, pidx[0:R, 0:1], None, ALU.is_equal).then_inc(s_relh, 1)
            pool.wait_ge(s_key, 1)
            for c in range(EC):
                if c % 4 == 0:
                    pool.wait_ge(s_keyrow_sb, c // 4 + 1)
                last = gp.tensor_scalar(keyrow[:, c, :], keyrow[:, c, :], key[:, c:c + 1], None, ALU.is_equal)
            link(last)
            pool.wait_ge(s_ohread, EC)
            pool.wait_ge(s_h1, 1)
            pool.wait_ge(s_h1st, 1)
            gp.tensor_tensor(h_r, h[:, :, :], hb[:, 0], ALU.subtract).then_inc(s_rest, 1)
            pool.wait_ge(s_h1st, 2)
            gp.tensor_tensor(h_r, h_r, hb[:, 1], ALU.subtract).then_inc(s_rest, 1)
            gp.tensor_tensor(eqb, keyrow, before[:, :].unsqueeze(1).to_broadcast([P, EC, P]),
                             ALU.mult).then_inc(s_eq, 1)
            pool.wait_ge(s_zeroed, 128)
            pool.wait_ge(s_cellsum, 1)
            link(gp.tensor_scalar(isdup[:, :], dup[:, :], 0.0, None, ALU.is_gt))
            link(gp.tensor_scalar(idxf[:, :], key[:, :], spare[:, 0:1], None, ALU.subtract))
            link(gp.tensor_tensor(idxf[:, :], idxf[:, :], isdup[:, :], ALU.mult))
            link(gp.tensor_tensor(idxf[:, :], key[:, :], idxf[:, :], ALU.subtract))
            link(gp.tensor_copy(idx[:, :], idxf[:, :]))
            for c in range(EC):
                gp.indirect_dma_start(out=table, out_offset=bass.IndirectOffsetOnAxis(ap=idx[:, c:c + 1], axis=0),
                                      in_=csum[:, c, :], in_offset=None, compute_op=ALU.add).then_inc(s_scat, 16)
                pool.wait_ge(s_scat, 16 * (c + 1))
            pool.dma_start(atab, table[0:CELLS, :].rearrange("(t p d) b -> p t (d b)", t=T, p=P)).then_inc(s_atab, 16)

            pool.wait_ge(s_h3Tsb, 2)
            for b in range(NBIN):
                pool.wait_ge(s_mrow_sb, b // 2 + 1)
                if b >= 2:
                    pool.wait_ge(s_uused, E + B + b - 1)
                gp.tensor_tensor(zz[:, b % 2, 1], hT3[:, 1].bitcast(fp32),
                                 mrow[:, b, :].unsqueeze(1).to_broadcast([P, K, N]), ALU.mult).then_inc(s_hml, 1)

        @block.scalar
        def _(act):
            sc = nc.scalar
            ints = "(p c) -> p c"
            act.dma_start(src_i[:, :], src.rearrange(ints, c=EC)).then_inc(s_edges, 16)
            act.dma_start(dst_i[:, :], dst.rearrange(ints, c=EC)).then_inc(s_edges, 16)
            act.dma_start(rel_i, etype.rearrange("(a e) -> a e", a=1).broadcast_to([R, EDGES])).then_inc(s_rel, 16)
            act.dma_start(wc_sb[:, :], w_comp).then_inc(s_wc, 16)
            act.dma_start(ew_sb[:, :], ew.rearrange("(p c) a -> p (c a)", c=EC)).then_inc(s_ew, 16)
            act.dma_start(gate_sb, gate_w).then_inc(s_gate, 16)
            act.dma_start(gateb_sb[:, :], gate_b.rearrange("(a e) -> a e", a=1).broadcast_to([P, E])).then_inc(s_gateb, 16)
            act.dma_start(bias0_sb, bias0.rearrange("(a e) -> a e", a=1).broadcast_to([P, D])).then_inc(s_b0, 16)
            act.dma_start(bias1_sb[:, :], bias1.rearrange("(a e) -> a e", a=1).broadcast_to([P, D])).then_inc(s_b1, 16)
            act.wait_ge(s_zeroset, 1)
            tz = table.rearrange("(p r) b -> p (r b)", p=P)
            q = ROWS * B // P // 8
            for i in range(8):
                act.dma_start(tz[:, i * q:(i + 1) * q], zero).then_inc(s_zeroed, 16)
            act.wait_ge(s_T0, 1)
            sc.copy(hT[:, :, :], ps[:, 6:8, :].rearrange("p a (k n) -> p (a k) n", k=2)).then_inc(s_T0sb, 1)
            act.wait_ge(s_gT, 1)
            sc.copy(gT[:, :, :], ps[:, 4, 0:K * E].rearrange("p (k e) -> p k e", k=K)).then_inc(s_gTsb, 1)
            act.wait_ge(s_gTsb, 1)
            for t in range(T):
                act.wait_ge(s_y0, t + 1)
                sc.copy(y0[:, t, :], ps[:, t, :]).then_inc(s_y0sb, 1)
            for g in range((EC + 3) // 4):
                n = min(4, EC - 4 * g)
                act.wait_ge(s_keyrow, g + 1)
                sc.copy(areg[:, g * 512:g * 512 + n * P], ps[:, g % 2, 0:n * P]).then_inc(s_keyrow_sb, 1)
            for e in range(2):
                act.wait_ge(s_unit[e], 32)
                for half in range(2):
                    c = slice(half * U // 2, (half + 1) * U // 2)
                    sc.copy(whi[:, e, c], raw[:, e, c]).then_inc(s_uhi, 1)
            act.wait_ge(s_h1, 1)
            sc.copy(hb[:, 0], h[:, :, :]).then_inc(s_h1st, 1)
            act.wait_ge(s_hT, 1)
            sc.copy(hT[:, 0:2, :], ps[:, 2, :].rearrange("p (k n) -> p k n", k=2)).then_inc(s_hTsb, 1)
            act.wait_ge(s_rest, 1)
            sc.copy(hb[:, 1], h_r).then_inc(s_h1st, 1)
            act.wait_ge(s_logit, 1)
            sc.activation(scores[:, :, :], ps[:, 4, 0:T * E].rearrange("p (t e) -> p t e", t=T),
                          ACT.Sigmoid).then_inc(s_score, 1)
            act.wait_ge(s_rest, 2)
            sc.copy(hb[:, 2], h_r).then_inc(s_hb, 1)

            def early(p, n):
                return isinstance(p, int) and p < n

            def times(e, slot):
                return e // NRING + 1 if isinstance(e, int) else (e - slot) // NRING + 1

            def unit_hi(e, b, slot, fill, half):
                if half == 0:
                    act.wait_ge(s_unit[slot], 32 * (fill + 1))
                    if not early(e, 2):
                        act.wait_ge(s_uused, e - 1)
                c = slice(half * U // 2, (half + 1) * U // 2)
                sc.copy(whi[:, b, c], raw[:, slot, c]).then_inc(s_uhi, 1)

            def two_hi(e, b, slot, fill):
                act.wait_ge(s_two[slot], 16 * (fill + 1))
                if not early(e, 2):
                    act.wait_ge(s_used, e - 1)
                sc.copy(whi[:, b, U:], raw2[:, slot, :]).then_inc(s_2hi, 1)

            def gathered_hi(p, u):
                act.wait_ge(s_xgp, p + 1)
                sc.copy(own_slots(xg[:, u, 0]), ps[:, 0, :].rearrange("p (k i s) -> p k i s", k=K, i=2)).then_inc(s_xgh, 1)

            def y_hi(p):
                act.wait_ge(s_used, 2 * p + 2)
                sc.copy(yy[:, 0, :], ps[:, 4, :]).then_inc(s_yh, 1)

            def pair(p, j, r, last=False):
                u = j % 2
                at, nxt = 2 * u, 2 * (1 - u)
                fill = r * (PR // 2) + j // 2
                nfill = fill + u
                if not early(p, 1):
                    y_hi(p - 1)
                for i in range(2):
                    two_hi(2 * p + i, i, at + i, fill)
                for half in range(2):
                    unit_hi(2 * p + 2, 0, nxt, nfill, half)
                act.wait_ge(s_uused, 2 * p + 2)
                sc.activation(sg, ps[:, 2 + u, 0:M], ACT.Silu).then_inc(s_sg, 1)
                unit_hi(2 * p + 3, 1, nxt + 1, nfill, 0)
                if not last:
                    gathered_hi(p + 1, 1 - u)
                act.wait_ge(s_T, p + 1)
                sc.copy(own_slots(hiT[:, 0]), ps[:, 1, 0:MC * P].rearrange("p (m i s) -> p m i s", m=MC, i=2)).then_inc(s_Th, 1)
                act.wait_ge(s_PTp, p + 1)
                sc.copy(PT[:, u], ps[:, 5, 0:T * P].rearrange("p (t s) -> p t s", t=T)).then_inc(s_PT, 1)
                unit_hi(2 * p + 3, 1, nxt + 1, nfill, 1)

            def round_(r, last=False):
                for j in range(PR):
                    pair(r * PR + j, j, r, last and j == PR - 1)

            act.wait_ge(s_padded, 1)
            gathered_hi(0, 0)
            round_(0)
            with act.Fori(1, ROUNDS - 1) as r:
                round_(r)
            round_(ROUNDS - 1, last=True)
            y_hi(NP - 1)

            act.wait_ge(s_ovtab, 1)
            nov = act.value_load(ov_i[0:1, NOVMAX:NOVMAX + 1], min_val=0, max_val=NOVMAX - 1)
            act.wait_ge(s_comb, NP)
            with act.If(nov > 0):
                with act.Fori(0, nov) as v:
                    act.wait_ge(o_xgp, v + 1)
                    sc.copy(xw, ps[:, 0, 0:K * W].rearrange("p (k s) -> p k s", k=K)).then_inc(o_xg, 1)
                    sc.copy(PTw[0:W, :], ps[0:W, 5, 0:T * P]).then_inc(o_PT, 1)
                    act.wait_ge(o_up, v + 1)
                    sc.activation(sg[0:W, :], ps[0:W, 2, 0:M], ACT.Silu).then_inc(o_silu, 1)
                    act.wait_ge(o_T, v + 1)
                    sc.copy(hw, ps[:, 1, 0:MC * P].rearrange("p (m s) -> p m s", m=MC)[:, :, 0:W]).then_inc(o_Tc, 1)

            def split_next(b):
                e = E + b + 2
                if b + 2 < B + NBIN:
                    for half in range(2):
                        unit_hi(e, b % 2, e % NRING, e // NRING, half)

            def links_hi(b):
                act.wait_ge(s_zp, b + 1)
                if b >= 2:
                    act.wait_ge(s_uused, E + b - 1)
                sc.copy(zz[:, b % 2, 0], ps[:, 2 * (b % 2):2 * (b % 2) + 2, :].rearrange("p a (k n) -> p (a k) n", k=2)).then_inc(s_zhi, 1)

            links_hi(0)
            for b in range(B):
                if b + 1 < B:
                    links_hi(b + 1)
                split_next(b)
            act.wait_ge(s_h3T, 1)
            sc.copy(hT3[:, 0], ps[:, 4:6, :].rearrange("p a (k n) -> p (a k) n", k=2)).then_inc(s_h3Tsb, 1)
            for g in range(NBIN // 2):
                act.wait_ge(s_mrow, 2 * g + 2)
                sc.copy(mrow[:, 2 * g:2 * g + 2, :], ps[:, g, :].rearrange("p (b n) -> p b n", b=2)).then_inc(s_mrow_sb, 1)
            for b in range(B, B + NBIN):
                split_next(b)

        @block.vector
        def _(dve):
            v_ = nc.vector
            chain = [0]

            def link(ins):
                chain[0] += 1
                ins.then_inc(s_dve, 1)
                dve.wait_ge(s_dve, chain[0])

            def unit_lo(e, b, slot, half):
                c = slice(half * U // 2, (half + 1) * U // 2)
                dve.wait_ge(s_uhi, 2 * e + half + 1)
                v_.tensor_tensor(wlo[:, b, c], raw[:, slot, c], whi[:, b, c].bitcast(fp32), ALU.subtract).then_inc(s_ulo, 1)

            def rsqrt(out_, in_, add):
                link(v_.tensor_scalar(nw_v[:, :], in_, add, None, ALU.add))
                link(v_.tensor_scalar(nw_i[:, :], nw_v[:, :].bitcast(i32), 1, None, ALU.logical_shift_right))
                link(v_.tensor_scalar(out_.bitcast(i32), nw_i[:, :], -1.0, float(0x5F3759DF), ALU.mult, ALU.add))
                for _ in range(3):
                    link(v_.scalar_tensor_tensor(out=nw_t[:, :], in0=out_, scalar=-0.5, in1=nw_v[:, :],
                                                 op0=ALU.mult, op1=ALU.mult))
                    link(v_.tensor_tensor(nw_t[:, :], nw_t[:, :], out_, ALU.mult))
                    link(v_.scalar_tensor_tensor(out=out_, in0=nw_t[:, :], scalar=1.5, in1=out_,
                                                 op0=ALU.add, op1=ALU.mult))

            def norm_stats():
                for t in range(T):
                    link(v_.bn_stats(stats[:, t, :], xcur[:, t, :]))
                for t in range(T):
                    link(v_.bn_aggr(mv[:, t, :], stats[:, t, :]))
                rsqrt(rstd[:, :], mv[:, :, 1], EPS)

            dve.wait_ge(s_x, 16)
            norm_stats()
            for t in range(T):
                last = v_.tensor_scalar(h[:, t, :], xcur[:, t, :], mv[:, t, 0:1], rstd[:, t:t + 1],
                                        ALU.subtract, ALU.mult)
            last.then_inc(s_h0, 1)
            dve.wait_ge(s_edges, 32)
            v_.tensor_copy(dstf[:, :], dst_i[:, :])
            link(v_.tensor_copy(srcf[:, :], src_i[:, :]))
            v_.scalar_tensor_tensor(out=key[:, :], in0=srcf[:, :], scalar=float(N), in1=dstf[:, :],
                                    op0=ALU.mult, op1=ALU.add).then_inc(s_key, 1)
            dve.wait_ge(s_const, 1)
            def onehots(c, one, j, first=False):
                if not first:
                    dve.wait_ge(s_ohread, c - NH + 1)
                v_.tensor_scalar(S1[:, j, :], iota_n[:, :], srcf[:, one], None, ALU.is_equal)
                v_.tensor_scalar(D1[:, j, :], iota_n[:, :], dstf[:, one], None, ALU.is_equal).then_inc(s_onehot, 1)

            for j in range(NH):
                onehots(j, slice(j, j + 1), j, first=True)
            for j in range(NH):
                onehots(NH + j, slice(NH + j, NH + j + 1), j)

            dve.wait_ge(s_b0, 16)
            for t in range(T):
                link(v_.tensor_tensor(xcur[:, t, :], xcur[:, t, :], bias0_sb, ALU.add))
            dve.wait_ge(s_ohread, EC)
            v_.tensor_copy(links[:, :, :], ps[:, 2:4, 0:N]).then_inc(s_lk, 1)
            dve.wait_ge(s_lk, 1)
            dve.wait_ge(s_lkT, 1)
            link(v_.tensor_tensor(links[:, :, :], links[:, :, :], ps[:, 6, :].rearrange("p (t n) -> p t n", t=T), ALU.add))
            for t in range(T):
                link(v_.tensor_scalar(adj[:, t, :], links[:, t, :], 1.0, 0.0, ALU.min, ALU.add,
                                      accum_out=deg[:, t:t + 1]))
            for t in range(T):
                blk = adj[:, t, t * P:(t + 1) * P]
                last = v_.tensor_tensor(blk, blk, ident[:, :], ALU.add)
            last.then_inc(s_adj, 1)
            rsqrt(dinv[:, :], deg[:, :], 1.0)
            dve.wait_ge(s_y0sb, T)
            for t in range(T):
                v_.tensor_scalar(y0[:, t, :], y0[:, t, :], dinv[:, t:t + 1], None, ALU.mult).then_inc(s_y0d, 1)
            unit_lo(0, 0, 0, 0)
            for t in range(T):
                dve.wait_ge(s_o0, t + 1)
                link(v_.scalar_tensor_tensor(out=xcur[:, t, :], in0=ps[:, 6 + t, :], scalar=dinv[:, t:t + 1],
                                             in1=xcur[:, t, :], op0=ALU.mult, op1=ALU.add))
            norm_stats()
            for t in range(T):
                last = v_.tensor_scalar(h[:, t, :], xcur[:, t, :], mv[:, t, 0:1], rstd[:, t:t + 1],
                                        ALU.subtract, ALU.mult)
            last.then_inc(s_h1, 1)
            unit_lo(0, 0, 0, 1)
            dve.wait_ge(s_hT, 1)
            v_.tensor_copy(hT[:, 2:4, :], ps[:, 3, :].rearrange("p (k n) -> p k n", k=2)).then_inc(s_hTsb, 1)
            unit_lo(1, 1, 1, 0)
            dve.wait_ge(s_coefps, 1)
            dve.wait_ge(s_ew, 16)
            v_.tensor_tensor(coef[:, :, :], ps[:, 5, 0:EC * B].rearrange("p (c b) -> p c b", b=B),
                             ew_sb[:, :].unsqueeze(2).to_broadcast([P, EC, B]), ALU.mult).then_inc(s_coef, 1)

            dve.wait_ge(s_score, 1)
            dve.wait_ge(s_gateb, 16)
            for t in range(T):
                link(v_.tensor_tensor(s[:, t, :], scores[:, t, :], gateb_sb[:, :], ALU.add))
            for t in range(T):
                for g in range(G):
                    last = v_.max(m8[:, t * G + g, :], s[:, t, g * GE:(g + 1) * GE])
            link(last)
            link(v_.tensor_tensor(gsc[:, :, 0:G], m8[:, :, 0].rearrange("p (t g) -> p t g", t=T),
                                  m8[:, :, 1].rearrange("p (t g) -> p t g", t=T), ALU.add))
            for t in range(T):
                link(v_.max(v8[:, t, :], gsc[:, t, 0:G]))
            link(v_.memset(v8[:, :, TOPG:8], NEG))
            for t in range(T):
                link(v_.match_replace(out=grep[:, t, :], in_to_replace=v8[:, t, :], in_values=gsc[:, t, :],
                                      imm_value=TAKEN))
            link(v_.tensor_scalar(gmask[:, :, :], grep[:, :, 0:G], 2 * NEG, None, ALU.is_lt))
            link(v_.tensor_scalar(gpen[:, :, :], gmask[:, :, :], 1.0, -NEG, ALU.subtract, ALU.mult))
            sv = s[:, :, :].rearrange("p t (g e) -> p (t g) e", g=G)
            gmv = gmask[:, :, :].rearrange("p t g -> p (t g)").unsqueeze(2).to_broadcast([P, T * G, GE])
            gpv = gpen[:, :, :].rearrange("p t g -> p (t g)").unsqueeze(2).to_broadcast([P, T * G, GE])
            link(v_.tensor_tensor(sv, sv, gmv, ALU.mult))
            link(v_.tensor_tensor(sv, sv, gpv, ALU.add))
            for t in range(T):
                link(v_.max(v8[:, t, :], s[:, t, :]))
                link(v_.match_replace(out=rep[:, t, :], in_to_replace=v8[:, t, :], in_values=s[:, t, :],
                                      imm_value=TAKEN))
            v_.tensor_scalar(sel[:, :, :], rep[:, :, :], 2 * NEG, None, ALU.is_lt).then_inc(s_sel, 1)
            dve.wait_ge(s_sel, 1)
            link(v_.tensor_tensor(gw[:, :, :], scores[:, :, :], sel[:, :, :], ALU.mult))
            link(v_.tensor_reduce(den[:, :], gw[:, :, :], AX, ALU.add))
            link(v_.reciprocal(den[:, :], den[:, :]))
            for t in range(T):
                link(v_.tensor_scalar(gw[:, t, :], gw[:, t, :], den[:, t:t + 1], SCALE, ALU.mult, ALU.mult))
            dve.wait_ge(s_rank, 1)
            link(v_.scalar_tensor_tensor(out=rankm[:, :, :], in0=ps[:, 5, 0:T * E].rearrange("p (t e) -> p t e", t=T),
                                         scalar=1.0, in1=sel[:, :, :], op0=ALU.add, op1=ALU.mult))
            link(v_.tensor_scalar(rankm[:, :, :], rankm[:, :, :], -1.0, None, ALU.add))

            def early(p, n):
                return isinstance(p, int) and p < n

            iota_b = iota_w[:, :].unsqueeze(1).to_broadcast([P, 2, W])

            def make_onehots(p, u):
                if not early(p, 2):
                    dve.wait_ge(s_PTp, p - 1)
                for t in range(T):
                    ranks = rankm[:, t, bass.ds(2 * p, 2)].unsqueeze(2).to_broadcast([P, 2, W])
                    last = v_.tensor_tensor(Pb[:, u, t].rearrange("p (i s) -> p i s", i=2), iota_b, ranks, ALU.is_equal)
                last.then_inc(s_P, 1)

            dve.wait_ge(s_zeroed, 128)
            make_onehots(0, 0)
            make_onehots(1, 1)
            unit_lo(1, 1, 1, 1)
            link(v_.tensor_copy(gwb[:, :, :, 0], gw[:, :, :]))
            link(v_.tensor_tensor(gw_r[:, :, :], gw[:, :, :], gwb[:, :, :, 0], ALU.subtract))
            link(v_.tensor_copy(gwb[:, :, :, 1], gw_r[:, :, :]))
            link(v_.tensor_tensor(gw_r[:, :, :], gw_r[:, :, :], gwb[:, :, :, 1], ALU.subtract))
            v_.tensor_copy(gwb[:, :, :, 2], gw_r[:, :, :]).then_inc(s_route, 1)
            v_.tensor_copy(cnt[:, :], ps[:, 5, T * E:T * E + E]).then_inc(s_sel, 1)

            def two_lo(e, b, slot):
                dve.wait_ge(s_2hi, e + 1)
                v_.tensor_tensor(wlo[:, b, U:], raw2[:, slot, :], whi[:, b, U:].bitcast(fp32), ALU.subtract).then_inc(s_2lo, 1)

            def gathered_lo(p, u):
                dve.wait_ge(s_xgh, p + 1)
                v_.tensor_tensor(own_slots(xg[:, u, 1]), ps[:, 0, :].rearrange("p (k i s) -> p k i s", k=K, i=2),
                                 own_slots(xg[:, u, 0]).bitcast(fp32), ALU.subtract).then_inc(s_xgl, 1)

            def slot_weights(p):
                dve.wait_ge(s_gsp, p + 1)
                for i in range(2):
                    rows = slice(i * W, (i + 1) * W)
                    last = v_.tensor_reduce(gs[rows, :], ps[rows, 1, MC * P + 3 * i:MC * P + 3 * i + 3], AX, ALU.add)
                last.then_inc(s_gs, 1)

            def y_lo(p):
                dve.wait_ge(s_yh, p + 1)
                v_.tensor_tensor(yy[:, 1, :], ps[:, 4, :], yy[:, 0, :].bitcast(fp32), ALU.subtract).then_inc(s_yl, 1)

            def pair(p, j, last=False):
                u = j % 2
                at, nxt = 2 * u, 2 * (1 - u)
                if not early(p, 1):
                    y_lo(p - 1)
                for i in range(2):
                    two_lo(2 * p + i, i, at + i)
                for half in range(2):
                    unit_lo(2 * p + 2, 0, nxt, half)
                dve.wait_ge(s_gs, p + 1)
                dve.wait_ge(s_sg, p + 1)
                v_.scalar_tensor_tensor(out=hid, in0=ps[:, 2 + u, M:2 * M], scalar=gs[:, 0:1], in1=sg,
                                        op0=ALU.mult, op1=ALU.mult).then_inc(s_hid, 1)
                unit_lo(2 * p + 3, 1, nxt + 1, 0)
                dve.wait_ge(s_Th, p + 1)
                v_.tensor_tensor(own_slots(hiT[:, 1]), ps[:, 1, 0:MC * P].rearrange("p (m i s) -> p m i s", m=MC, i=2),
                                 own_slots(hiT[:, 0]).bitcast(fp32), ALU.subtract).then_inc(s_Tl, 1)
                if not last:
                    slot_weights(p + 1)
                    gathered_lo(p + 1, 1 - u)
                unit_lo(2 * p + 3, 1, nxt + 1, 1)

            def round_(r, last=False):
                for j in range(PR):
                    p = r * PR + j
                    pair(p, j, last and j == PR - 1)
                    if not (last and j >= PR - 2):
                        make_onehots(p + 2, j % 2)

            slot_weights(0)
            gathered_lo(0, 0)
            round_(0)
            dve.wait_ge(s_sel, 2)
            link(v_.tensor_scalar(ovc[:, :], cnt[:, :], float(W), None, ALU.is_gt))
            for q in range(2, N // W):
                link(v_.scalar_tensor_tensor(out=ovc[:, :], in0=cnt[:, :], scalar=float(W * q), in1=ovc[:, :],
                                             op0=ALU.is_gt, op1=ALU.add))
            link(v_.tensor_tensor_scan(out=oincl[:, :], data0=ones[:, 0:E], data1=ovc[:, :], initial=0.0,
                                       op0=ALU.mult, op1=ALU.add))
            link(v_.tensor_scalar(osel[:, :], oincl[:, :], pidx[:, 0:1], None, ALU.is_le))
            link(v_.tensor_reduce(ov_e[:, :], osel[:, :], AX, ALU.add))
            link(v_.tensor_tensor(osel[:, :], osel[:, :], ovc[:, :], ALU.mult))
            link(v_.tensor_reduce(ov_m[:, :], osel[:, :], AX, ALU.add))
            link(v_.tensor_tensor(ov_m[:, :], pidx[:, :], ov_m[:, :], ALU.subtract))
            link(v_.tensor_scalar(ov_m[:, :], ov_m[:, :], 1.0, float(W), ALU.add, ALU.mult))
            v_.tensor_scalar(ov_d[:, 0:NOVMAX], ident[:, 0:NOVMAX], ov_e[:, 0:1], None, ALU.mult)
            v_.tensor_scalar(ov_d[:, NOVMAX:], ident[:, 0:NOVMAX], ov_m[:, 0:1], None, ALU.mult).then_inc(s_ovd, 1)
            with dve.Fori(1, EDGE_ROUND) as r:
                round_(r)
            dve.wait_ge(s_csps, 1)
            v_.tensor_copy(dup[:, :], ps[:, 5, EC * B:EC * (B + 1)])
            v_.tensor_copy(csum[:, :, :], ps[:, 5, 0:EC * B].rearrange("p (c b) -> p c b", b=B)).then_inc(s_cellsum, 1)
            o = EC * (B + 1)
            v_.tensor_copy(ov_i[:, 0:NOVMAX], ps[:, 5, o:o + NOVMAX])
            v_.tensor_copy(ov_k[:, :], ps[:, 5, o + NOVMAX:o + 2 * NOVMAX]).then_inc(o_done, 1)
            v_.tensor_copy(ov_i[:, NOVMAX:NOVMAX + 1], oincl[:, E - 1:E]).then_inc(s_ovtab, 1)
            with dve.Fori(EDGE_ROUND, ROUNDS - 1) as r:
                round_(r)
            round_(ROUNDS - 1, last=True)
            y_lo(NP - 1)

            dve.wait_ge(s_ovtab, 1)
            nov = dve.value_load(ov_i[0:1, NOVMAX:NOVMAX + 1], min_val=0, max_val=NOVMAX - 1)
            dve.wait_ge(s_comb, NP)
            with dve.If(nov > 0):
                with dve.Fori(0, nov) as v:
                    e = dve.value_load(ov_i[0:1, bass.ds(v, 1)], min_val=0, max_val=E - 1)
                    for t in range(T):
                        last = v_.scalar_tensor_tensor(
                            out=Pb[:, 0, t, 0:W], in0=rankm[:, t, bass.ds(e, 1)].to_broadcast([P, W]),
                            scalar=ov_k[:, bass.ds(v, 1)], in1=iota_w[:, :], op0=ALU.subtract, op1=ALU.is_equal)
                    last.then_inc(o_P, 1)
                    dve.wait_ge(o_xgp, v + 1)
                    v_.tensor_reduce(gs[0:W, :], ps[0:W, 1, MC * P:MC * P + 3], AX, ALU.add).then_inc(o_gs, 1)
                    dve.wait_ge(o_gs, v + 1)
                    dve.wait_ge(o_silu, v + 1)
                    v_.scalar_tensor_tensor(out=hid[0:W, :], in0=ps[0:W, 2, M:2 * M], scalar=gs[0:W, 0:1], in1=sg[0:W, :],
                                            op0=ALU.mult, op1=ALU.mult).then_inc(o_hh, 1)
                    dve.wait_ge(o_down, v + 1)
                    v_.tensor_copy(yw[0:W, :], ps[0:W, 4, :]).then_inc(o_y, 1)
                    dve.wait_ge(o_done, v + 2)

            dve.wait_ge(s_comb, NP)
            for t in range(T):
                link(v_.tensor_tensor(xcur[:, t, :], xcur[:, t, :], ps[:, 6 + t, :], ALU.add))
            norm_stats()
            for t in range(T):
                last = v_.tensor_scalar(h[:, t, :], xcur[:, t, :], mv[:, t, 0:1], rstd[:, t:t + 1],
                                        ALU.subtract, ALU.mult)
            last.then_inc(s_h2, 1)
            dve.wait_ge(s_b1, 16)
            for t in range(T):
                link(v_.tensor_tensor(xcur[:, t, :], xcur[:, t, :], bias1_sb[:, :], ALU.add))
            def split_next(b):
                if b + 2 < B + NBIN:
                    for half in range(2):
                        unit_lo(E + b + 2, b % 2, (E + b + 2) % NRING, half)

            def links_lo(b):
                dve.wait_ge(s_zhi, b + 1)
                v_.tensor_tensor(zz[:, b % 2, 1], ps[:, 2 * (b % 2):2 * (b % 2) + 2, :].rearrange("p a (k n) -> p (a k) n", k=2),
                                 zz[:, b % 2, 0].bitcast(fp32), ALU.subtract).then_inc(s_zlo, 1)

            links_lo(0)
            for b in range(B):
                if b + 1 < B:
                    links_lo(b + 1)
                split_next(b)
            dve.wait_ge(s_uused, E + B)
            for t in range(T):
                link(v_.tensor_tensor(xcur[:, t, :], xcur[:, t, :], ps[:, 4 + t, :], ALU.add))
            norm_stats()
            for t in range(T):
                last = v_.tensor_scalar(h[:, t, :], xcur[:, t, :], mv[:, t, 0:1], rstd[:, t:t + 1],
                                        ALU.subtract, ALU.mult)
            last.then_inc(s_h3, 1)
            dve.wait_ge(s_h3, 1)
            link(v_.memset(above[:, :, 0:1], 1.0))
            link(v_.memset(above[:, :, NBIN:NBIN + 1], 0.0))
            for t in range(T):
                link(v_.tensor_scalar(above[:, t, 1:NBIN], bins[:, 1:NBIN], h[:, t, 0:1], None, ALU.is_lt))
            link(v_.tensor_tensor(binm[:, :, :], above[:, :, 0:NBIN], above[:, :, 1:NBIN + 1], ALU.subtract))
            for b in range(NBIN):
                for t in range(T):
                    last = v_.tensor_scalar(areg[:, (b * T + t) * P:(b * T + t + 1) * P], ident[:, :],
                                            binm[:, t, b:b + 1], None, ALU.mult)
            last.then_inc(s_mb, 1)
            dve.wait_ge(s_h3T, 1)
            dve.wait_ge(s_h3Tsb, 1)
            v_.tensor_tensor(hT3[:, 1], ps[:, 4:6, :].rearrange("p a (k n) -> p (a k) n", k=2),
                             hT3[:, 0].bitcast(fp32), ALU.subtract).then_inc(s_h3Tsb, 1)
            dve.wait_ge(s_h3Tsb, 2)
            def masked(b, eng, ns, part, done):
                eng.wait_ge(s_mrow_sb, b // 2 + 1)
                if b >= 2:
                    eng.wait_ge(s_uused, E + B + b - 1)
                ns.tensor_tensor(zz[:, b % 2, part], hT3[:, part].bitcast(fp32),
                                 mrow[:, b, :].unsqueeze(1).to_broadcast([P, K, N]), ALU.mult).then_inc(done, 1)

            masked(0, dve, v_, 0, s_hm)
            for b in range(NBIN):
                if b + 1 < NBIN:
                    masked(b + 1, dve, v_, 0, s_hm)
                split_next(B + b)
            dve.wait_ge(s_uused, E + B + NBIN)
            for t in range(T):
                v_.tensor_tensor(xcur[:, t, :], xcur[:, t, :], ps[:, 6 + t, :], ALU.add).then_inc(s_fin, 1)

        @block.tensor
        def _(pe):
            mm = nc.tensor.matmul
            tr = nc.tensor.transpose

            def transpose_h(bank, done):
                for k in range(K):
                    for t in range(T):
                        o = (k % 2) * N + t * P
                        last = tr(ps[:, bank + k // 2, o:o + P], h[:, t, k::K], ident[:, :])
                last.then_inc(done, 1)

            pe.wait_ge(s_const, 1)
            pe.wait_ge(s_gate, 16)
            for k in range(K):
                last = tr(ps[:, 4, k * E:(k + 1) * E], gate_sb[:, k::K], ident[0:E, 0:E])
            last.then_inc(s_gT, 1)
            pe.wait_ge(s_h0, 1)
            transpose_h(6, s_T0)
            pe.wait_ge(s_T0sb, 1)
            pe.wait_ge(s_w0, 16)
            for t in range(T):
                for k in range(K):
                    last = mm(ps[:, t, :], hT[:, k, t * P:(t + 1) * P], w0_sb[:, k, :],
                              start=k == 0, stop=k == K - 1)
                last.then_inc(s_y0, 1)
            for c in range(EC):
                pe.wait_ge(s_onehot, c + 1)
                for t in range(T):
                    last = mm(ps[:, 2 + t, 0:N], S1[:, c % NH, t * P:(t + 1) * P], D1[:, c % NH, :],
                              start=c == 0, stop=c == EC - 1)
                last.then_inc(s_ohread, 1)
            pe.wait_ge(s_lk, 1)
            for t in range(T):
                for st in range(T):
                    last = tr(ps[:, 6, t * N + st * P:t * N + (st + 1) * P], links[:, st, t * P:(t + 1) * P], ident[:, :])
            last.then_inc(s_lkT, 1)
            pe.wait_ge(s_relh, 1)
            pe.wait_ge(s_wc, 16)
            for c in range(EC):
                last = mm(ps[:, 5, c * B:(c + 1) * B], relh_c[:, c, :], wc_sb[:, :], start=True, stop=True)
            last.then_inc(s_coefps, 1)
            pe.wait_ge(s_adj, 1)
            for t in range(T):
                for st in range(T):
                    pe.wait_ge(s_y0d, st + 1)
                    last = mm(ps[:, 6 + t, :], adj[:, st, t * P:(t + 1) * P], y0[:, st, :],
                              start=st == 0, stop=st == T - 1)
                last.then_inc(s_o0, 1)
            pe.wait_ge(s_key, 1)
            pe.wait_ge(s_y0sb, T)
            for c in range(EC):
                g = c // 4
                if c % 4 == 0 and g >= 2:
                    pe.wait_ge(s_keyrow_sb, g - 1)
                last = mm(ps[:, g % 2, (c % 4) * P:(c % 4 + 1) * P], key[:, c:c + 1].to_broadcast([P, P]),
                          ident[:, :], start=True, stop=True)
                if c % 4 == 3 or c == EC - 1:
                    last.then_inc(s_keyrow, 1)
            pe.wait_ge(s_h1, 1)
            transpose_h(2, s_hT)
            pe.wait_ge(s_hTsb, 2)
            pe.wait_ge(s_gTsb, 1)
            for t in range(T):
                for k in range(K):
                    last = mm(ps[:, 4, t * E:(t + 1) * E], hT[:, k, t * P:(t + 1) * P], gT[:, k, :],
                              start=k == 0, stop=k == K - 1)
            last.then_inc(s_logit, 1)
            pe.wait_ge(s_sel, 1)
            pe.wait_ge(s_coef, 1)
            mm(ps[:, 5, 0:E], before[:, :], sel[:, 0, :], start=True, stop=True)
            mm(ps[:, 5, E:2 * E], before[:, :], sel[:, 1, :], start=True, stop=False)
            mm(ps[:, 5, E:2 * E], ones[:, :], sel[:, 0, :], start=False, stop=True)
            mm(ps[:, 5, 2 * E:3 * E], ones[:, :], sel[:, 0, :], start=True, stop=False)
            mm(ps[:, 5, 2 * E:3 * E], ones[:, :], sel[:, 1, :], start=False, stop=True).then_inc(s_rank, 1)

            def split_product(out_, pairs, n, start=True, stop=True):
                for k in range(n):
                    (xh, xl), (wh, wl) = pairs(k)
                    mm(out_, xh, wh, start=start and k == 0, stop=False, skip_group_check=True)
                    mm(out_, xh, wl, start=False, stop=False, skip_group_check=True)
                    last = mm(out_, xl, wh, start=False, stop=stop and k == n - 1, skip_group_check=True)
                return last

            def gather(p, u):
                pe.wait_ge(s_P, p + 1)
                for k in range(K):
                    for i in range(3):
                        for t in range(T):
                            last = mm(ps[:, 0, k * P:(k + 1) * P], hb[:, i, t, k::K], Pb[:, u, t, :],
                                      start=i == 0 and t == 0, stop=i == 2 and t == T - 1)
                last.then_inc(s_xgp, 1)

            def weights(p, u):
                for t in range(T):
                    last = mm(ps[:, 1, MC * P:MC * P + 6], Pb[:, u, t, :],
                              gwb[:, t, bass.ds(2 * p, 2), :].rearrange("p e i -> p (e i)"),
                              start=t == 0, stop=t == T - 1, skip_group_check=True)
                last.then_inc(s_gsp, 1)

            def units(b, half, c):
                return [w[:, b, 0:U].rearrange("p (a k m) -> p a k m", a=2, k=K)[:, :, c, :] for w in (whi, wlo)]

            def up(p, u, i):
                pe.wait_ge(s_ulo, 2 * (2 * p + i) + 2)
                cols = slice(i * W, i * W + P)
                split_product(ps[:, 2 + u, :], lambda k: ([xg[:, u, h_, k, cols] for h_ in range(2)], units(i, 0, k)),
                              K, start=i == 0, stop=i == 1).then_inc(s_uused, 1)

            def down(p, i):
                pe.wait_ge(s_2lo, 2 * p + i + 1)
                cols = slice(i * W, i * W + P)
                split_product(ps[:, 4, :], lambda m: ([hiT[:, h_, m, cols] for h_ in range(2)],
                                                      [w[:, i, U + m * D:U + (m + 1) * D] for w in (whi, wlo)]),
                              MC, start=i == 0, stop=i == 1).then_inc(s_used, 1)

            def combine(p, u, start):
                pe.wait_ge(s_yl, p + 1)
                pe.wait_ge(s_PT, p + 1)
                for t in range(T):
                    for h_ in range(2):
                        last = mm(ps[:, 6 + t, :], PT[:, u, t, :], yy[:, h_, :], start=start and h_ == 0, stop=True,
                                  skip_group_check=True)
                last.then_inc(s_comb, 1)

            def round_(r, last=False):
                for j in range(PR):
                    p = r * PR + j
                    u = j % 2
                    first = isinstance(p, int) and p == 0
                    more = not (last and j == PR - 1)
                    pe.wait_ge(s_xgl, p + 1)
                    up(p, u, 0)
                    up(p, u, 1)
                    if more:
                        gather(p + 1, 1 - u)
                    pe.wait_ge(s_hid, p + 1)
                    if more:
                        weights(p + 1, 1 - u)
                    for m in range(MC):
                        last_t = tr(ps[:, 1, m * P:(m + 1) * P], hid[:, m::MC], ident[:, :])
                    last_t.then_inc(s_T, 1)
                    if not first:
                        pe.wait_ge(s_PT, p)
                    for t in range(T):
                        last_t = mm(ps[:, 5, t * P:(t + 1) * P], Pb[:, u, t, :], identb[:, :], start=True, stop=True)
                    last_t.then_inc(s_PTp, 1)
                    if not first:
                        combine(p - 1, 1 - u, isinstance(p, int) and p == 1)
                    pe.wait_ge(s_Tl, p + 1)
                    down(p, 0)
                    down(p, 1)

            pe.wait_ge(s_hb, 1)
            gather(0, 0)
            pe.wait_ge(s_route, 1)
            weights(0, 0)
            pe.wait_ge(s_const, 2)
            pe.wait_ge(s_sel, 2)
            round_(0)
            with pe.Fori(1, EDGE_ROUND) as r:
                round_(r)
            pe.wait_ge(s_eq, 1)
            pe.wait_ge(s_ovd, 1)
            pe.wait_ge(s_PT, PR * EDGE_ROUND)
            for c in range(EC):
                last = mm(ps[:, 5, c * B:(c + 1) * B], keyrow[:, c, :], coef[:, c, :], start=True, stop=True)
            for c in range(EC):
                last = mm(ps[:, 5, EC * B + c:EC * B + c + 1], eqb[:, c, :], onesb[:, :], start=True, stop=True)
            o = EC * (B + 1)
            mm(ps[:, 5, o:o + 2 * NOVMAX], ones[:, :], ov_d[:, :], start=True, stop=True).then_inc(s_csps, 1)
            pe.wait_ge(s_cellsum, 1)
            pe.wait_ge(o_done, 1)
            with pe.Fori(EDGE_ROUND, ROUNDS - 1) as r:
                round_(r)
            round_(ROUNDS - 1, last=True)
            combine(NP - 1, (NP - 1) % 2, False)

            pe.wait_ge(s_ovtab, 1)
            nov = pe.value_load(ov_i[0:1, NOVMAX:NOVMAX + 1], min_val=0, max_val=NOVMAX - 1)
            with pe.If(nov > 0):
                with pe.Fori(0, nov) as v:
                    one = bass.ds(pe.value_load(ov_i[0:1, bass.ds(v, 1)], min_val=0, max_val=E - 1), 1)
                    pe.wait_ge(o_P, v + 1)
                    for t in range(T):
                        mm(ps[0:W, 5, t * P:(t + 1) * P], Pb[:, 0, t, 0:W], identb[:, :], start=True, stop=True)
                    for t in range(T):
                        mm(ps[0:W, 1, MC * P:MC * P + 3], Pb[:, 0, t, 0:W], gwb[:, t, one, :].rearrange("p e i -> p (e i)"),
                           start=t == 0, stop=t == T - 1, skip_group_check=True)
                    for k in range(K):
                        for i in range(3):
                            for t in range(T):
                                last = mm(ps[:, 0, k * W:(k + 1) * W], hb[:, i, t, k::K], Pb[:, 0, t, 0:W],
                                          start=i == 0 and t == 0, stop=i == 2 and t == T - 1)
                    last.then_inc(o_xgp, 1)
                    pe.wait_ge(o_w, 48 * (v + 1))
                    pe.wait_ge(o_xg, v + 1)
                    w13 = extra[:, 0:U].rearrange("p (a k m) -> p a k m", a=2, k=K)
                    for k in range(K):
                        last = mm(ps[0:W, 2, :], xw[:, k, :], w13[:, :, k, :], start=k == 0, stop=k == K - 1)
                    last.then_inc(o_up, 1)
                    pe.wait_ge(o_hh, v + 1)
                    for m in range(MC):
                        last = tr(ps[:, 1, m * P:(m + 1) * P], hid[:, m::MC], ident[:, :])
                    last.then_inc(o_T, 1)
                    pe.wait_ge(o_Tc, v + 1)
                    for m in range(MC):
                        last = mm(ps[0:W, 4, :], hw[:, m, :], extra[:, U + m * D:U + (m + 1) * D],
                                  start=m == 0, stop=m == MC - 1)
                    last.then_inc(o_down, 1)
                    pe.wait_ge(o_y, v + 1)
                    for t in range(T):
                        last = mm(ps[:, 6 + t, :], PTw[0:W, t * P:(t + 1) * P], yw[0:W, :], start=False, stop=True,
                                  skip_group_check=True)
                    last.then_inc(o_done, 1)

            def unit_parts(e, k):
                return [w[:, e % 2, k * D:(k + 1) * D] for w in (whi, wlo)]

            pe.wait_ge(s_h2, 1)
            pe.wait_ge(s_atab, 16)

            def links_product(b):
                if b >= 2:
                    pe.wait_ge(s_zlo, b - 1)
                for k in range(K):
                    for st in range(T):
                        last = mm(ps[:, 2 * (b % 2) + k // 2, (k % 2) * N:(k % 2 + 1) * N], h[:, st, k::K],
                                  atab[:, st, :, b], start=st == 0, stop=st == T - 1)
                last.then_inc(s_zp, 1)

            links_product(0)
            for b in range(B):
                if b + 1 < B:
                    links_product(b + 1)
                pe.wait_ge(s_zlo, b + 1)
                pe.wait_ge(s_ulo, 2 * (E + b) + 2)
                for t in range(T):
                    last = split_product(ps[:, 4 + t, :],
                                         lambda k: ([zz[:, b % 2, h_, k, t * P:(t + 1) * P] for h_ in range(2)], unit_parts(b, k)),
                                         K, start=b == 0, stop=b == B - 1)
                last.then_inc(s_uused, 1)

            pe.wait_ge(s_h3, 1)
            transpose_h(4, s_h3T)
            pe.wait_ge(s_mb, 1)
            for b in range(NBIN):
                for t in range(T):
                    last = mm(ps[:, b // 2, (b % 2) * N + t * P:(b % 2) * N + (t + 1) * P], ones[:, :],
                              areg[:, (b * T + t) * P:(b * T + t + 1) * P], start=True, stop=True)
                last.then_inc(s_mrow, 1)
            for b in range(NBIN):
                pe.wait_ge(s_hm, b + 1)
                pe.wait_ge(s_hml, b + 1)
                pe.wait_ge(s_ulo, 2 * (E + B + b) + 2)
                for t in range(T):
                    last = split_product(ps[:, 6 + t, :],
                                         lambda k: ([zz[:, b % 2, h_, k, t * P:(t + 1) * P] for h_ in range(2)], unit_parts(b, k)),
                                         K, start=b == 0, stop=b == NBIN - 1)
                last.then_inc(s_uused, 1)



_INS = ["x", "src", "dst", "edge_type_32", "edge_weight1", "L0_gnn_weight", "L0_gnn_bias", "L0_ffn_gate_w",
        "L0_ffn_gate_b", "L0_ffn_w1", "L0_ffn_w3", "L0_ffn_w2", "L1_gnn_bases", "L1_gnn_w_comp",
        "L1_gnn_h_bias", "L1_ffn_W"]


def kernel(**inputs):
    import numpy as _np
    import concourse.bacc as _bacc
    from concourse import mybir as _mybir
    from concourse.bass_utils import run_bass_kernel_spmd as _run

    nc = _bacc.Bacc("TRN2", target_bir_lowering=False, num_devices=1)
    arrays, args = {}, []
    for name in _INS:
        a = _np.ascontiguousarray(inputs[name])
        arrays[f"in_{name}_dram"] = a
        args.append(nc.dram_tensor(f"in_{name}_dram", a.shape, _mybir.dt.from_np(a.dtype), kind="ExternalInput").ap())
    n, d = arrays["in_x_dram"].shape
    res = nc.dram_tensor("out_0_dram", (n, d), _mybir.dt.float32, kind="ExternalOutput").ap()
    build(nc, *args, res)
    r = _run(nc, [arrays], core_ids=[0])
    return r.results[0]["out_0_dram"]
```

```python
import concourse.bass as bass
from concourse import mybir
from contextlib import ExitStack


def build(nc, x, src, dst, etype, ew, w0, bias0, gate_w, gate_b, w1, w3, w2, bases, w_comp, bias1, wf, out):
    fp32, bf16, i32, u32 = mybir.dt.float32, mybir.dt.bfloat16, mybir.dt.int32, mybir.dt.uint32
    f32r = mybir.dt.float32r
    ALU = mybir.AluOpType
    ACT = mybir.ActivationFunctionType
    AX = mybir.AxisListType.X

    P = 128
    N, D = x.shape
    T = N // P
    K = D // P
    EDGES = src.shape[0]
    EC = EDGES // P
    E, _, M = w1.shape
    MC = M // P
    R, B = w_comp.shape
    NBIN = wf.shape[0]
    G, TOPG, TOPK, SCALE = 8, 4, 8, 2.5
    GE = E // G
    EPS = 1e-5
    BINS = [-1.5, -1.0, -0.5, 0.0, 0.5, 1.0, 1.5]
    W = 64
    NRING = 4
    PR = 4
    ROUNDS = E // 2 // PR
    EARLY = 1
    EDGE_ROUND = 1
    U = K * D
    NP = E // 2
    NOVMAX = 32
    NEG, TAKEN = -1.0e30, -3.0e30
    CELLS = N * N
    ROWS = CELLS + P

    table = nc.dram_tensor("cell_table", [ROWS, B], fp32, kind="Internal").ap()

    ctx = ExitStack()
    with ctx:
        def sb(name, shape, dt=fp32):
            return ctx.enter_context(nc.sbuf_tensor(name, shape, dt))

        def sem(name):
            return ctx.enter_context(nc.semaphore(name))

        raw = sb("raw", [P, NRING, U])
        raw2 = sb("raw2", [P, NRING, M * D // P])
        whi = sb("whi", [P, 2, U + M * D // P], f32r)
        wlo = sb("wlo", [P, 2, U + M * D // P], f32r)
        fr = sb("split_arena", [P, 6144], f32r)
        extra = sb("extra", [P, EDGES])
        areg = sb("areg", [P, EDGES])
        pa = sb("pair_arena", [P, 5121 + 1024])
        xcur = sb("xcur", [P, T, D])
        h = sb("h", [P, T, D])
        bias1_sb = sb("bias1_sb", [P, D])
        ident = sb("ident", [P, P])
        before = sb("before", [P, P])
        onesb = sb("onesb", [P, 1], bf16)
        ones = sb("ones", [P, P])
        iota_n = sb("iota_n", [P, N], bf16)
        iota_w = sb("iota_w", [P, W])
        identb = sb("identb", [P, P], bf16)
        pidx = sb("pidx", [P, 1])
        gwb = sb("gw_thirds", [P, T, E, 3], bf16)
        gw_r = sb("gw_rest", [P, T, E])
        gs = sb("slot_weight", [P, 1])
        osel = sb("osel", [P, E])
        ov_d = sb("ov_d", [P, 2 * NOVMAX])
        spare = sb("spare", [P, 1])
        src_i = sb("src_i", [P, EC], i32)
        dst_i = sb("dst_i", [P, EC], i32)
        srcf = sb("srcf", [P, EC])
        dstf = sb("dstf", [P, EC])
        key = sb("key", [P, EC])
        ew_sb = sb("ew_sb", [P, EC])
        wc_sb = sb("wc_sb", [R, B])
        wcb = sb("wcomp_thirds", [R, 3, B], bf16)
        coef = sb("coef", [P, EC, B])
        csum = coef
        dup = sb("dup", [P, EC])
        isdup = sb("isdup", [P, EC])
        idxf = sb("idxf", [P, EC])
        idx = sb("idx", [P, EC], u32)
        idx_now = sb("idx_now", [P, 1], u32)
        csum_now = sb("csum_now", [P, B])
        waiter = sb("waiter", [P, 1])
        gateb_sb = sb("gateb_sb", [P, E])
        gT = sb("gT", [P, K, E])
        sel = sb("sel", [P, T, E])
        gw = sb("gw", [P, T, E])
        rankm = sb("rankm", [P, T, E])
        gsc = sb("gsc", [P, T, 16])
        v8 = sb("v8", [P, T, 8])
        grep = sb("grep", [P, T, 16])
        gmask = sb("gmask", [P, T, G])
        gpen = sb("gpen", [P, T, G])
        den = sb("den", [P, T])
        stats = sb("stats", [P, T, 6])
        mv = sb("mv", [P, T, 2])
        rstd = sb("rstd", [P, T])
        nw_v = sb("newton_v", [P, T])
        nw_i = sb("newton_i", [P, T], i32)
        nw_t = sb("newton_t", [P, T])
        deg = sb("deg", [P, T])
        dinv = sb("dinv", [P, T])
        hscale = sb("hscale", [P, T])
        cnt = sb("cnt", [P, E])
        ovc = sb("ovc", [P, E])
        oincl = sb("oincl", [P, E])
        ov_e = sb("ov_e", [P, 1])
        ov_m = sb("ov_m", [P, 1])
        ov_k = sb("ov_k", [P, NOVMAX])
        ov_i = sb("ov_i", [P, NOVMAX + 1], i32)
        bins = sb("bins", [P, NBIN + 1])
        above = sb("above", [P, T, NBIN + 1])
        binm = sb("binm", [P, T, NBIN], bf16)

        NH = EC // 2
        oneh = extra[:, 0:NH * N].bitcast(bf16)
        S1 = oneh[:, 0:NH * N].rearrange("p (c n) -> p c n", n=N)
        D1 = oneh[:, NH * N:2 * NH * N].rearrange("p (c n) -> p c n", n=N)
        eqb = extra[:, EDGES // 2:EDGES].bitcast(bf16).rearrange("p (c q) -> p c q", q=P)
        rel_v = raw[:, 1:4, :].rearrange("p a b -> p (a b)")[0:R, 0:EDGES]
        rel_i = rel_v.bitcast(i32)
        relh = rel_v.bitcast(bf16)[:, 0:EDGES]
        relh_c = relh.rearrange("r (p c) -> r c p", c=EC)
        keyrow = areg[:, :].rearrange("p (c q) -> p c q", q=P)
        eq = extra[:, 0:EDGES // 2].bitcast(bf16).rearrange("p (c q) -> p c q", q=P)
        atab = areg[:, 0:T * N * B].rearrange("p (t d b) -> p t d b", t=T, b=B)
        zero = pa[:, 0:ROWS * B // P // 8]
        hT = pa[:, 1537:2561].rearrange("p (k n) -> p k n", k=K)
        adj = pa[:, 2561:3073].rearrange("p (t n) -> p t n", t=T)
        links = pa[:, 513:1025].rearrange("p (t n) -> p t n", t=T)
        gate_sb = pa[0:E, 5121:5121 + D]
        y0 = pa[:, 5121:5121 + T * D].rearrange("p (t o) -> p t o", t=T)
        s = pa[:, 2561:2689].rearrange("p (t e) -> p t e", t=T)
        rep = pa[:, 2689:2817].rearrange("p (t e) -> p t e", t=T)
        m8 = pa[:, 2817:2945].rearrange("p (g i) -> p g i", i=8)
        scores = pa[:, 2945:3073].rearrange("p (t e) -> p t e", t=T)
        w0_sb = pa[:, 3073:5121].rearrange("p (k o) -> p k o", k=K)
        bias0_sb = pa[:, 1025:1537]
        Pb = pa[:, 0:256].bitcast(bf16).rearrange("p (u t s) -> p u t s", u=2, t=T)
        sg = pa[:, 256:512]
        hid = pa[:, 512:768]
        coef3 = pa[:, 1280:1280 + 3 * EC * B // 2].bitcast(bf16).rearrange("p (c i b) -> p c i b", c=EC, i=3)
        act13 = pa[:, 768:1280]
        hb = pa[:, 3073:4609].bitcast(bf16).rearrange("p (i t d) -> p i t d", i=3, t=T)
        h_r = extra[:, 0:T * D].rearrange("p (t d) -> p t d", t=T)
        xw = pa[:, 1792:2048].rearrange("p (k s) -> p k s", k=K)
        hw = pa[:, 2048:2176].rearrange("p (m s) -> p m s", m=MC)
        PTw = pa[:, 2304:2560]
        yw = pa[:, 2560:3072]
        xg = fr[:, 0:2048].rearrange("p (u k q s) -> p u k q s", u=2, k=K, q=4)
        hiT = fr[:, 3072:3840].rearrange("p (h m s) -> p h m s", h=2, m=MC)
        PT = fr[:, 3840:4352].rearrange("p (u t s) -> p u t s", u=2, t=T)
        yy = fr[:, 4352:5376].rearrange("p (h d) -> p h d", h=2)
        zz = fr[:, 0:4096].rearrange("p (u h k n) -> p u h k n", u=2, h=2, k=K)
        mrow = extra[:, 0:NBIN * N].rearrange("p (b n) -> p b n", b=NBIN)
        h2s = fr[:, 4096:6144].rearrange("p (h t d) -> p h t d", h=2, t=T)

        def cells(w, b):
            return w[:, b % 2, U:U + T * N].rearrange("p (t d) -> p t d", t=T)

        hT3 = fr[:, 4096:6144].rearrange("p (h k n) -> p h k n", h=2, k=K)

        def own_slots(blocks):
            return blocks.rearrange("p a (j s) -> p a j s", j=3)[:, :, 0::2, :]

        ps = ctx.enter_context(nc.psum_tensor("ps", [P, 8, 512], fp32))

        s_x, s_w0, s_edges, s_ew, s_wc, s_rel = (sem(n) for n in (
            "x_loaded", "w0_loaded", "edges_loaded", "ew_loaded", "wcomp_loaded", "relations_loaded"))
        s_gate, s_gateb, s_b0, s_b1 = (sem(n) for n in ("gate_loaded", "gateb_loaded", "bias0_loaded", "bias1_loaded"))
        s_unit = [sem(f"unit{i}_loaded") for i in range(NRING)]
        s_two = [sem(f"w2_{i}_loaded") for i in range(NRING)]
        s_zeroset, s_zeroed, s_cellsum, s_scat, s_atab = (sem(n) for n in (
            "zero_set", "table_zeroed", "cell_sums_made", "scattered", "table_loaded"))
        s_const, s_dve, s_pool = sem("constants_made"), sem("dve_chain"), sem("pool_chain")
        s_key, s_onehot, s_keyrow, s_keyrow_sb, s_eq, s_relh = (sem(n) for n in (
            "key_made", "onehots_made", "keyrow_done", "keyrow_copied", "equalities_made", "relation_onehot_made"))
        s_coefps, s_coef, s_csps = sem("coef_product"), sem("coef_made"), sem("cellsum_product")
        s_adj, s_T0, s_T0sb, s_o0, s_h1, s_hT, s_hTsb = (sem(n) for n in (
            "adj_made", "adj_h_product", "adj_h_copied", "gcn_product", "h1_made", "hT_done", "hT_copied"))
        s_gT, s_gTsb, s_logit, s_score, s_sel, s_rank, s_route, s_ovtab = (sem(n) for n in (
            "gateT_done", "gateT_copied", "logits_done", "scores_made", "selected", "ranks_done", "routed", "overflow_listed"))
        s_P, s_xgp, s_xgh, s_xgl, s_PTp, s_PT = (sem(n) for n in (
            "onehot_made", "gather_done", "gathered_hi", "gathered_lo", "PT_product", "PT_copied"))
        s_uhi, s_ulo, s_uused, s_2hi, s_2lo, s_used = (sem(n) for n in (
            "unit_hi", "unit_lo", "units_used", "w2_hi", "w2_lo", "experts_used"))
        s_sg, s_hid, s_T, s_Th, s_Tl, s_gsp, s_gs = (sem(n) for n in (
            "silu_made", "hidden_made", "hidden_transposed", "hiddenT_hi", "hiddenT_lo", "slot_weight_product", "slot_weight"))
        s_yh, s_yl, s_comb, s_padded, s_h1st, s_rest, s_hb, s_ovd = (sem(n) for n in (
            "y_hi", "y_lo", "combined", "padding_zeroed", "thirds_act", "rests_pool", "h_thirds_made", "overflow_diag"))
        s_wcb = sem("wcomp_thirds_made")
        s_mrow_sb, s_hml, s_h0 = sem("mask_rows_copied"), sem("masked_lo_made"), sem("h0_made")
        s_now, s_2last = sem("chunk_in_place"), sem("last_w2_lo")
        s_alo_first, s_mrow_first, s_hml_first = (sem(n) for n in (
            "first_cells_lo", "first_mask_rows_in_sbuf", "first_masked_lo"))
        s_ahi, s_alo, s_h2hi, s_h2lo, s_rel_out, s_bin_out = (sem(n) for n in (
            "cells_hi", "cells_lo", "h2_hi", "h2_lo", "relational_sum_done", "binned_sum_done"))
        s_cross, s_sum = sem("second_rows_moved"), sem("parts_added")
        s_ohread, s_y0, s_y0sb, s_lk, s_lkT, s_y0d = (sem(n) for n in (
            "onehots_read", "xw_product", "xw_copied", "links_copied", "links_transposed", "xw_scaled"))
        o_w, o_P, o_xgp, o_xg, o_gs, o_PT, o_up, o_silu, o_hh, o_T, o_Tc, o_down, o_y, o_done = (
            sem("over_" + n) for n in ("loaded", "onehot", "gather", "xg_copied", "slot_weight", "PT_copied", "up",
                                       "silu", "hidden", "transposed", "hiddenT_copied", "down", "y_copied", "done"))
        s_h2, s_zp, s_zhi, s_zlo, s_h3, s_h3T, s_h3Tsb = (sem(n) for n in (
            "h2_made", "ah_product", "ah_hi", "ah_lo", "h3_made",
            "h3T_done", "h3T_copied"))
        s_mb, s_hm, s_mrow, s_fin, s_out = (sem(n) for n in (
            "mask_rows_done", "masked_made", "mask_row_done", "result_made", "result_stored"))

        block = ctx.enter_context(nc.Block())

        @block.sync
        def _(sp):
            sp.dma_start(xcur[:, :, :], x.rearrange("(t p) d -> p t d", p=P)).then_inc(s_x, 16)
            sp.dma_start(w0_sb, w0.rearrange("(p k) o -> p k o", k=K)).then_inc(s_w0, 16)

            def load_unit(slot, e):
                one = bass.ds(e, 1)
                sp.dma_start(raw[:, slot, 0:U // 2], w1[one].rearrange("a (p k) m -> p (a k m)", k=K)).then_inc(s_unit[slot], 16)
                sp.dma_start(raw[:, slot, U // 2:U], w3[one].rearrange("a (p k) m -> p (a k m)", k=K)).then_inc(s_unit[slot], 16)

            def load_two(slot, e):
                sp.dma_start(raw2[:, slot, :], w2[bass.ds(e, 1)].rearrange("a (p k) m -> p (a k m)", k=MC)).then_inc(s_two[slot], 16)

            def load_units(q, slot, free=None):
                for i in range(2):
                    if free is not None:
                        sp.wait_ge(s_ulo, 2 * free + 2 * i + 2)
                    load_unit(slot + i, 2 * q + i)

            def load_twos(q, slot, free=None):
                for i in range(2):
                    if free is not None:
                        sp.wait_ge(s_2lo, free + i + 1)
                    load_two(slot + i, 2 * q + i)

            load_unit(0, 0)
            load_twos(0, 0)
            load_twos(1, 2)
            sp.wait_ge(s_coefps, 1)
            for slot in range(1, NRING):
                load_unit(slot, slot)
            load_units(2, 0, free=0)
            with sp.Fori(1, NP // 2 - 1) as r:
                load_units(2 * r + 1, 2, free=4 * r - 2)
                load_twos(2 * r, 0, free=4 * r - 4)
                load_units(2 * r + 2, 0, free=4 * r)
                load_twos(2 * r + 1, 2, free=4 * r - 2)
            load_units(NP - 1, 2, free=E - 6)
            load_twos(NP - 2, 0, free=E - 8)
            load_twos(NP - 1, 2, free=E - 6)

            sp.wait_ge(s_ovtab, 1)
            nov = sp.value_load(ov_i[0:1, NOVMAX:NOVMAX + 1], min_val=0, max_val=NOVMAX - 1)
            with sp.If(nov > 0):
                with sp.Fori(0, nov) as v:
                    one = bass.ds(sp.value_load(ov_i[0:1, bass.ds(v, 1)], min_val=0, max_val=E - 1), 1)
                    sp.wait_ge(o_done, v + 1)
                    sp.dma_start(extra[:, 0:1024], w1[one].rearrange("a (p k) m -> p (a k m)", k=K)).then_inc(o_w, 16)
                    sp.dma_start(extra[:, 1024:2048], w3[one].rearrange("a (p k) m -> p (a k m)", k=K)).then_inc(o_w, 16)
                    sp.dma_start(extra[:, 2048:3072], w2[one].rearrange("a (p k) m -> p (a k m)", k=MC)).then_inc(o_w, 16)
            for b in range(B + NBIN):
                e = E + b
                of = bases[b] if b < B else wf[b - B]
                sp.wait_ge(s_ulo, 2 * (e - NRING) + 2)
                for half in range(2):
                    cols = slice(half * U // 2, (half + 1) * U // 2)
                    sp.dma_start(raw[:, e % NRING, cols],
                                 of.rearrange("(p k) o -> p (k o)", k=K)[:, cols]).then_inc(s_unit[e % NRING], 16)
            for t in range(T):
                sp.wait_ge(s_fin, t + 1)
                sp.dma_start(out[t * P:(t + 1) * P, :], xcur[:, t, :]).then_inc(s_out, 16)
            sp.wait_ge(s_out, 16 * T)

        @block.gpsimd
        def _(pool):
            gp = nc.gpsimd
            chain = [0]

            def link(ins):
                chain[0] += 1
                ins.then_inc(s_pool, 1)
                pool.wait_ge(s_pool, chain[0])

            gp.iota(iota_n[:, :], [[1, N]], base=0, channel_multiplier=0, allow_small_or_imprecise_dtypes=True)
            gp.iota(iota_w[:, :], [[1, W]], base=0, channel_multiplier=0, allow_small_or_imprecise_dtypes=True)
            gp.iota(spare[:, :], [[1, 1]], base=CELLS, channel_multiplier=1, allow_small_or_imprecise_dtypes=True)
            gp.iota(pidx[:, :], [[1, 1]], base=0, channel_multiplier=1, allow_small_or_imprecise_dtypes=True)
            gp.memset(gsc[:, :, :], NEG)
            for i, edge in enumerate(BINS):
                gp.memset(bins[:, i + 1:i + 2], edge)
            link(gp.memset(ones[:, :], 1.0))
            gp.memset(onesb[:, :], 1.0)
            gp.affine_select(out=ident[:, :], in_=ones[:, :], compare_op=ALU.is_equal, fill=0.0, base=0,
                             pattern=[[-1, P]], channel_multiplier=1)
            gp.affine_select(out=before[:, :], in_=ones[:, :], compare_op=ALU.is_gt, fill=0.0, base=0,
                             pattern=[[1, P]], channel_multiplier=-1).then_inc(s_const, 1)
            pool.wait_ge(s_const, 1)
            gp.tensor_copy(identb[:, :], ident[:, :]).then_inc(s_const, 1)
            gp.memset(zero, 0.0).then_inc(s_zeroset, 1)
            gp.memset(fr[:, 0:3840].bitcast(fp32), 0.0).then_inc(s_padded, 1)
            pool.wait_ge(s_rel, 16)
            pool.wait_ge(s_const, 1)
            gp.tensor_scalar(relh, rel_i, pidx[0:R, 0:1], None, ALU.is_equal).then_inc(s_relh, 1)
            pool.wait_ge(s_ohread, EC)
            pool.wait_ge(s_h1, 1)
            pool.wait_ge(s_h1st, 1)
            gp.tensor_tensor(h_r, h[:, :, :], hb[:, 0], ALU.subtract).then_inc(s_rest, 1)
            pool.wait_ge(s_h1st, 2)
            gp.tensor_tensor(h_r, h_r, hb[:, 1], ALU.subtract).then_inc(s_rest, 1)
            pool.wait_ge(s_hb, 1)
            for c in range(EC):
                if c % 4 == 0:
                    pool.wait_ge(s_keyrow_sb, c // 4 + 1)
                last = gp.tensor_scalar(eq[:, c, :], keyrow[:, c, :], key[:, c:c + 1], None, ALU.is_equal)
            link(last)
            gp.tensor_tensor(eqb, eq, before[:, :].unsqueeze(1).to_broadcast([P, EC, P]),
                             ALU.mult).then_inc(s_eq, 1)

            def two_lo(e, b, slot):
                pool.wait_ge(s_2hi, e + 1)
                gp.tensor_tensor(wlo[:, b, U:], raw2[:, slot, :], whi[:, b, U:].bitcast(fp32), ALU.subtract).then_inc(s_2lo, 1)

            for e in range(4, 8):
                two_lo(e, e % 2, e % NRING)
            pool.wait_ge(s_zeroed, 128)
            pool.wait_ge(s_cellsum, 1)
            link(gp.tensor_scalar(isdup[:, :], dup[:, :], 0.0, None, ALU.is_gt))
            link(gp.tensor_scalar(idxf[:, :], key[:, :], spare[:, 0:1], None, ALU.subtract))
            link(gp.tensor_tensor(idxf[:, :], idxf[:, :], isdup[:, :], ALU.mult))
            link(gp.tensor_tensor(idxf[:, :], key[:, :], idxf[:, :], ALU.subtract))
            link(gp.tensor_copy(idx[:, :], idxf[:, :]))
            def scatter(c, one):
                if not (isinstance(c, int) and c == 0):
                    pool.wait_ge(s_scat, 16 * c)
                gp.tensor_copy(idx_now[:, :], idx[:, one])
                gp.tensor_copy(csum_now[:, :], csum[:, one, :].rearrange("p c b -> p (c b)")).then_inc(s_now, 1)
                pool.wait_ge(s_now, c + 1)
                gp.tensor_tensor(waiter[:, :], spare[:, :], spare[:, :], ALU.add)
                gp.indirect_dma_start(out=table, out_offset=bass.IndirectOffsetOnAxis(ap=idx_now[:, :], axis=0),
                                      in_=csum_now[:, :], in_offset=None, compute_op=ALU.add).then_inc(s_scat, 16)

            for c in range(EARLY):
                scatter(c, slice(c, c + 1))
            with pool.Fori(EDGE_ROUND, ROUNDS - 1) as r:
                for j in range(PR):
                    c = EARLY + (r - EDGE_ROUND) * PR + j
                    two_lo(2 * (r * PR + j), 0, 2 * (j % 2))
                    two_lo(2 * (r * PR + j) + 1, 1, 2 * (j % 2) + 1)
                    scatter(c, bass.ds(c, 1))
            c = EARLY + NP - PR - PR * EDGE_ROUND
            for p in range(NP - PR, NP - 1):
                two_lo(2 * p, 0, 2 * (p % 2))
                scatter(c, slice(c, c + 1))
                c += 1
                two_lo(2 * p + 1, 1, 2 * (p % 2) + 1)
                scatter(c, slice(c, c + 1))
                c += 1
            for c in range(c, EC):
                scatter(c, slice(c, c + 1))
            pool.wait_ge(s_scat, 16 * EC)
            pool.dma_start(areg[:, 0:T * N * B].rearrange("p (t r) -> p t r", t=T),
                           table[0:CELLS, :].rearrange("(t p d) b -> p t (d b)", t=T, p=P)).then_inc(s_atab, 16)

            pool.wait_ge(s_ahi, 1)
            pool.wait_ge(s_atab, 16)
            gp.tensor_tensor(cells(wlo, 0), atab[:, :, :, 0], cells(whi, 0).bitcast(fp32), ALU.subtract).then_inc(s_alo_first, 1)

            pool.wait_ge(s_h3Tsb, 2)
            pool.wait_ge(s_mrow_first, 1)
            for b in range(1, NBIN):
                if b >= 2:
                    pool.wait_ge(s_mrow_sb, b // 2)
                if b >= 2:
                    pool.wait_ge(s_uused, E + B + b - 1)
                gp.tensor_tensor(zz[:, b % 2, 1], hT3[:, 1].bitcast(fp32),
                                 mrow[:, b, :].unsqueeze(1).to_broadcast([P, K, N]), ALU.mult).then_inc(s_hml, 1)

        @block.scalar
        def _(act):
            sc = nc.scalar
            ints = "(p c) -> p c"
            act.dma_start(src_i[:, :], src.rearrange(ints, c=EC)).then_inc(s_edges, 16)
            act.dma_start(dst_i[:, :], dst.rearrange(ints, c=EC)).then_inc(s_edges, 16)
            act.dma_start(rel_i, etype.rearrange("(a e) -> a e", a=1).broadcast_to([R, EDGES])).then_inc(s_rel, 16)
            act.dma_start(wc_sb[:, :], w_comp).then_inc(s_wc, 16)
            act.dma_start(ew_sb[:, :], ew.rearrange("(p c) a -> p (c a)", c=EC)).then_inc(s_ew, 16)
            act.dma_start(gate_sb, gate_w).then_inc(s_gate, 16)
            act.dma_start(gateb_sb[:, :], gate_b.rearrange("(a e) -> a e", a=1).broadcast_to([P, E])).then_inc(s_gateb, 16)
            act.dma_start(bias0_sb, bias0.rearrange("(a e) -> a e", a=1).broadcast_to([P, D])).then_inc(s_b0, 16)
            act.dma_start(bias1_sb[:, :], bias1.rearrange("(a e) -> a e", a=1).broadcast_to([P, D])).then_inc(s_b1, 16)
            act.wait_ge(s_const, 1)
            sc.activation(den[:, 0:1], ones[:, 0:1], ACT.Sigmoid)
            act.wait_ge(s_T0, 1)
            sc.copy(hT[:, :, :], ps[:, 6:8, :].rearrange("p a (k n) -> p (a k) n", k=2)).then_inc(s_T0sb, 1)
            act.wait_ge(s_gT, 1)
            sc.copy(gT[:, :, :], ps[:, 4, 0:K * E].rearrange("p (k e) -> p k e", k=K)).then_inc(s_gTsb, 1)
            for t in range(T):
                act.wait_ge(s_y0, t + 1)
                sc.copy(y0[:, t, :], ps[:, t, :]).then_inc(s_y0sb, 1)
            act.wait_ge(s_zeroset, 1)
            tz = table.rearrange("(p r) b -> p (r b)", p=P)
            q = ROWS * B // P // 8
            for i in range(8):
                act.dma_start(tz[:, i * q:(i + 1) * q], zero).then_inc(s_zeroed, 16)
            for e in range(2):
                act.wait_ge(s_unit[e], 32)
                for half in range(2):
                    c = slice(half * U // 2, (half + 1) * U // 2)
                    sc.copy(whi[:, e, c], raw[:, e, c]).then_inc(s_uhi, 1)
            for g in range((EC + 3) // 4):
                n = min(4, EC - 4 * g)
                act.wait_ge(s_keyrow, g + 1)
                sc.copy(areg[:, g * 512:g * 512 + n * P], ps[:, g % 2, 0:n * P]).then_inc(s_keyrow_sb, 1)
            act.wait_ge(s_h1, 1)
            sc.copy(hb[:, 0], h[:, :, :]).then_inc(s_h1st, 1)
            act.wait_ge(s_hT, 1)
            sc.copy(hT[:, 0:2, :], ps[:, 2, :].rearrange("p (k n) -> p k n", k=2)).then_inc(s_hTsb, 1)
            act.wait_ge(s_logit, 1)
            sc.activation(scores[:, :, :], ps[:, 4, 0:T * E].rearrange("p (t e) -> p t e", t=T),
                          ACT.Sigmoid).then_inc(s_score, 1)
            act.wait_ge(s_rest, 1)
            sc.copy(hb[:, 1], h_r).then_inc(s_h1st, 1)
            act.wait_ge(s_rest, 2)
            sc.copy(hb[:, 2], h_r).then_inc(s_hb, 1)

            def early(p, n):
                return isinstance(p, int) and p < n

            def times(e, slot):
                return e // NRING + 1 if isinstance(e, int) else (e - slot) // NRING + 1

            def unit_hi(e, b, slot, fill, half):
                if half == 0:
                    act.wait_ge(s_unit[slot], 32 * (fill + 1))
                    if not early(e, 2):
                        act.wait_ge(s_uused, e - 1)
                c = slice(half * U // 2, (half + 1) * U // 2)
                sc.copy(whi[:, b, c], raw[:, slot, c]).then_inc(s_uhi, 1)

            def two_hi(e, b, slot, fill):
                act.wait_ge(s_two[slot], 16 * (fill + 1))
                if not early(e, 2):
                    act.wait_ge(s_used, e - 1)
                sc.copy(whi[:, b, U:], raw2[:, slot, :]).then_inc(s_2hi, 1)

            def gathered_hi(p, u):
                act.wait_ge(s_xgp, p + 1)
                sc.copy(xg[:, u, :, 0::3, :], ps[:, 0, :].rearrange("p (k i s) -> p k i s", k=K, i=2)).then_inc(s_xgh, 1)

            def y_hi(p):
                act.wait_ge(s_used, 2 * p + 2)
                sc.copy(yy[:, 0, :], ps[:, 4, :]).then_inc(s_yh, 1)

            def pair(p, j, r, last=False):
                u = j % 2
                at, nxt = 2 * u, 2 * (1 - u)
                fill = r * (PR // 2) + j // 2
                nfill = fill + u
                def cross(i):
                    act.wait_ge(s_uused, 2 * p + i + 1)
                    sc.copy(act13[i * W:(i + 1) * W, :], ps[(1 - i) * W:(2 - i) * W, 2 + i, :]).then_inc(s_cross, 1)

                cross(0)
                if not last:
                    unit_hi(2 * p + 2, 0, nxt, nfill, 0)
                    unit_hi(2 * p + 2, 0, nxt, nfill, 1)
                cross(1)
                if not last:
                    unit_hi(2 * p + 3, 1, nxt + 1, nfill, 0)
                    gathered_hi(p + 1, 1 - u)
                act.wait_ge(s_sum, 2 * p + 2)
                sc.activation(sg, act13[:, 0:M], ACT.Silu).then_inc(s_sg, 1)
                if not last:
                    unit_hi(2 * p + 3, 1, nxt + 1, nfill, 1)
                two_hi(2 * p, 0, at, fill)
                if not early(p, 1):
                    y_hi(p - 1)
                act.wait_ge(s_T, p + 1)
                sc.copy(own_slots(hiT[:, 0]), ps[:, 1, 0:MC * P].rearrange("p (m i s) -> p m i s", m=MC, i=2)).then_inc(s_Th, 1)
                act.wait_ge(s_PTp, p + 1)
                sc.copy(PT[:, u], ps[:, 5, 0:T * P].rearrange("p (t s) -> p t s", t=T)).then_inc(s_PT, 1)
                two_hi(2 * p + 1, 1, at + 1, fill)

            def round_(r, last=False):
                for j in range(PR):
                    pair(r * PR + j, j, r, last and j == PR - 1)

            def cells_hi(b):
                if b >= 2:
                    act.wait_ge(s_zp, b - 1)
                sc.copy(cells(whi, b), atab[:, :, :, b]).then_inc(s_ahi, 1)

            act.wait_ge(s_padded, 1)
            gathered_hi(0, 0)
            sc.activation(sg[:, 0:1], ones[:, 0:1], ACT.Silu)
            round_(0)
            with act.Fori(1, ROUNDS - 1) as r:
                round_(r)
            round_(ROUNDS - 1, last=True)

            def unit_hi_late(e):
                for half in range(2):
                    unit_hi(e, e % 2, e % NRING, e // NRING, half)

            unit_hi_late(E)
            y_hi(NP - 1)
            unit_hi_late(E + 1)

            act.wait_ge(s_ovtab, 1)
            nov = act.value_load(ov_i[0:1, NOVMAX:NOVMAX + 1], min_val=0, max_val=NOVMAX - 1)
            act.wait_ge(s_comb, NP)
            with act.If(nov > 0):
                with act.Fori(0, nov) as v:
                    act.wait_ge(o_xgp, v + 1)
                    sc.copy(xw, ps[:, 0, 0:K * W].rearrange("p (k s) -> p k s", k=K)).then_inc(o_xg, 1)
                    sc.copy(PTw[0:W, :], ps[0:W, 5, 0:T * P]).then_inc(o_PT, 1)
                    act.wait_ge(o_up, v + 1)
                    sc.activation(sg[0:W, :], ps[0:W, 2, 0:M], ACT.Silu).then_inc(o_silu, 1)
                    act.wait_ge(o_T, v + 1)
                    sc.copy(hw, ps[:, 1, 0:MC * P].rearrange("p (m s) -> p m s", m=MC)[:, :, 0:W]).then_inc(o_Tc, 1)

            def split_next(b):
                if b + 2 < B + NBIN:
                    unit_hi_late(E + b + 2)

            act.wait_ge(s_atab, 16)
            cells_hi(0)
            cells_hi(1)
            for t in range(T):
                act.wait_ge(s_h2, t + 1)
                sc.copy(h2s[:, 0, t], h[:, t, :]).then_inc(s_h2hi, 1)

            def links_hi(b):
                act.wait_ge(s_zp, b + 1)
                if b >= 2:
                    act.wait_ge(s_uused, E + b - 1)
                sc.copy(zz[:, b % 2, 0], ps[:, 2 * (b % 2):2 * (b % 2) + 2, :].rearrange("p a (k n) -> p (a k) n", k=2)).then_inc(s_zhi, 1)

            links_hi(0)
            for b in range(B):
                if b + 1 < B:
                    links_hi(b + 1)
                if b + 2 < B:
                    cells_hi(b + 2)
                split_next(b)
            act.wait_ge(s_h3T, 1)
            sc.copy(hT3[:, 0], ps[:, 4:6, :].rearrange("p a (k n) -> p (a k) n", k=2)).then_inc(s_h3Tsb, 1)
            for g in range(1, NBIN // 2):
                act.wait_ge(s_mrow, 2 * g + 2)
                sc.copy(mrow[:, 2 * g:2 * g + 2, :], ps[:, g, :].rearrange("p (b n) -> p b n", b=2)).then_inc(s_mrow_sb, 1)
            for b in range(B, B + NBIN):
                split_next(b)

        @block.vector
        def _(dve):
            v_ = nc.vector
            chain = [0]

            def link(ins):
                chain[0] += 1
                ins.then_inc(s_dve, 1)
                dve.wait_ge(s_dve, chain[0])

            def unit_lo(e, b, slot, half):
                c = slice(half * U // 2, (half + 1) * U // 2)
                dve.wait_ge(s_uhi, 2 * e + half + 1)
                v_.tensor_tensor(wlo[:, b, c], raw[:, slot, c], whi[:, b, c].bitcast(fp32), ALU.subtract).then_inc(s_ulo, 1)

            def rsqrt(out_, in_, add):
                link(v_.tensor_scalar(nw_v[:, :], in_, add, None, ALU.add))
                link(v_.tensor_scalar(nw_i[:, :], nw_v[:, :].bitcast(i32), 1, None, ALU.logical_shift_right))
                link(v_.tensor_scalar(out_.bitcast(i32), nw_i[:, :], -1.0, float(0x5F3759DF), ALU.mult, ALU.add))
                for _ in range(3):
                    link(v_.scalar_tensor_tensor(out=nw_t[:, :], in0=out_, scalar=-0.5, in1=nw_v[:, :],
                                                 op0=ALU.mult, op1=ALU.mult))
                    link(v_.tensor_tensor(nw_t[:, :], nw_t[:, :], out_, ALU.mult))
                    link(v_.scalar_tensor_tensor(out=out_, in0=nw_t[:, :], scalar=1.5, in1=out_,
                                                 op0=ALU.add, op1=ALU.mult))

            def norm_stats(begun=False):
                if not begun:
                    for t in range(T):
                        link(v_.bn_stats(stats[:, t, :], xcur[:, t, :]))
                for t in range(T):
                    link(v_.bn_aggr(mv[:, t, :], stats[:, t, :]))
                rsqrt(rstd[:, :], mv[:, :, 1], EPS)

            dve.wait_ge(s_x, 16)
            norm_stats()
            for t in range(T):
                last = v_.tensor_scalar(h[:, t, :], xcur[:, t, :], mv[:, t, 0:1], rstd[:, t:t + 1],
                                        ALU.subtract, ALU.mult)
            last.then_inc(s_h0, 1)
            dve.wait_ge(s_edges, 32)
            v_.tensor_copy(dstf[:, :], dst_i[:, :])
            link(v_.tensor_copy(srcf[:, :], src_i[:, :]))
            v_.scalar_tensor_tensor(out=key[:, :], in0=srcf[:, :], scalar=float(N), in1=dstf[:, :],
                                    op0=ALU.mult, op1=ALU.add).then_inc(s_key, 1)
            dve.wait_ge(s_const, 1)
            def onehots(c, one, j, first=False):
                if not first:
                    dve.wait_ge(s_ohread, c - NH + 1)
                v_.tensor_scalar(S1[:, j, :], iota_n[:, :], srcf[:, one], None, ALU.is_equal)
                v_.tensor_scalar(D1[:, j, :], iota_n[:, :], dstf[:, one], None, ALU.is_equal).then_inc(s_onehot, 1)

            for j in range(NH):
                onehots(j, slice(j, j + 1), j, first=True)
            for j in range(NH):
                onehots(NH + j, slice(NH + j, NH + j + 1), j)

            dve.wait_ge(s_wc, 16)
            link(v_.tensor_copy(wcb[:, 0, :], wc_sb[:, :]))
            link(v_.tensor_tensor(wc_sb[:, :], wc_sb[:, :], wcb[:, 0, :], ALU.subtract))
            link(v_.tensor_copy(wcb[:, 1, :], wc_sb[:, :]))
            link(v_.tensor_tensor(wc_sb[:, :], wc_sb[:, :], wcb[:, 1, :], ALU.subtract))
            v_.tensor_copy(wcb[:, 2, :], wc_sb[:, :]).then_inc(s_wcb, 1)
            dve.wait_ge(s_b0, 16)
            for t in range(T):
                link(v_.tensor_tensor(xcur[:, t, :], xcur[:, t, :], bias0_sb, ALU.add))
            dve.wait_ge(s_ohread, EC)
            v_.tensor_copy(links[:, :, :], ps[:, 2:4, 0:N]).then_inc(s_lk, 1)
            dve.wait_ge(s_lk, 1)
            dve.wait_ge(s_lkT, 1)
            link(v_.tensor_tensor(links[:, :, :], links[:, :, :], ps[:, 6, :].rearrange("p (t n) -> p t n", t=T), ALU.add))
            for t in range(T):
                link(v_.tensor_scalar(adj[:, t, :], links[:, t, :], 1.0, 0.0, ALU.min, ALU.add,
                                      accum_out=deg[:, t:t + 1]))
            for t in range(T):
                blk = adj[:, t, t * P:(t + 1) * P]
                last = v_.tensor_tensor(blk, blk, ident[:, :], ALU.add)
            last.then_inc(s_adj, 1)
            rsqrt(dinv[:, :], deg[:, :], 1.0)
            dve.wait_ge(s_y0sb, T)
            for t in range(T):
                v_.tensor_scalar(y0[:, t, :], y0[:, t, :], dinv[:, t:t + 1], None, ALU.mult).then_inc(s_y0d, 1)
            unit_lo(0, 0, 0, 0)
            unit_lo(0, 0, 0, 1)
            for t in range(T):
                dve.wait_ge(s_o0, t + 1)
                link(v_.scalar_tensor_tensor(out=xcur[:, t, :], in0=ps[:, 6 + t, :], scalar=dinv[:, t:t + 1],
                                             in1=xcur[:, t, :], op0=ALU.mult, op1=ALU.add))
            norm_stats()
            for t in range(T):
                last = v_.tensor_scalar(h[:, t, :], xcur[:, t, :], mv[:, t, 0:1], rstd[:, t:t + 1],
                                        ALU.subtract, ALU.mult)
            last.then_inc(s_h1, 1)
            dve.wait_ge(s_hT, 1)
            v_.tensor_copy(hT[:, 2:4, :], ps[:, 3, :].rearrange("p (k n) -> p k n", k=2)).then_inc(s_hTsb, 1)
            unit_lo(1, 1, 1, 0)
            dve.wait_ge(s_coefps, 1)
            dve.wait_ge(s_ew, 16)
            v_.tensor_tensor(coef[:, :, :], ps[:, 5, 0:EC * B].rearrange("p (c b) -> p c b", b=B),
                             ew_sb[:, :].unsqueeze(2).to_broadcast([P, EC, B]), ALU.mult).then_inc(s_coef, 1)

            dve.wait_ge(s_score, 1)
            dve.wait_ge(s_gateb, 16)
            for t in range(T):
                link(v_.tensor_tensor(s[:, t, :], scores[:, t, :], gateb_sb[:, :], ALU.add))
            for t in range(T):
                for g in range(G):
                    last = v_.max(m8[:, t * G + g, :], s[:, t, g * GE:(g + 1) * GE])
            link(last)
            link(v_.tensor_tensor(gsc[:, :, 0:G], m8[:, :, 0].rearrange("p (t g) -> p t g", t=T),
                                  m8[:, :, 1].rearrange("p (t g) -> p t g", t=T), ALU.add))
            for t in range(T):
                link(v_.max(v8[:, t, :], gsc[:, t, 0:G]))
            link(v_.memset(v8[:, :, TOPG:8], NEG))
            for t in range(T):
                link(v_.match_replace(out=grep[:, t, :], in_to_replace=v8[:, t, :], in_values=gsc[:, t, :],
                                      imm_value=TAKEN))
            link(v_.tensor_scalar(gmask[:, :, :], grep[:, :, 0:G], 2 * NEG, None, ALU.is_lt))
            link(v_.tensor_scalar(gpen[:, :, :], gmask[:, :, :], 1.0, -NEG, ALU.subtract, ALU.mult))
            sv = s[:, :, :].rearrange("p t (g e) -> p (t g) e", g=G)
            gmv = gmask[:, :, :].rearrange("p t g -> p (t g)").unsqueeze(2).to_broadcast([P, T * G, GE])
            gpv = gpen[:, :, :].rearrange("p t g -> p (t g)").unsqueeze(2).to_broadcast([P, T * G, GE])
            link(v_.tensor_tensor(sv, sv, gmv, ALU.mult))
            link(v_.tensor_tensor(sv, sv, gpv, ALU.add))
            for t in range(T):
                link(v_.max(v8[:, t, :], s[:, t, :]))
                link(v_.match_replace(out=rep[:, t, :], in_to_replace=v8[:, t, :], in_values=s[:, t, :],
                                      imm_value=TAKEN))
            v_.tensor_scalar(sel[:, :, :], rep[:, :, :], 2 * NEG, None, ALU.is_lt).then_inc(s_sel, 1)
            dve.wait_ge(s_sel, 1)
            link(v_.tensor_tensor(gw[:, :, :], scores[:, :, :], sel[:, :, :], ALU.mult))
            link(v_.tensor_reduce(den[:, :], gw[:, :, :], AX, ALU.add))
            link(v_.reciprocal(den[:, :], den[:, :]))
            for t in range(T):
                link(v_.tensor_scalar(gw[:, t, :], gw[:, t, :], den[:, t:t + 1], SCALE, ALU.mult, ALU.mult))
            dve.wait_ge(s_rank, 1)
            link(v_.scalar_tensor_tensor(out=rankm[:, :, :], in0=ps[:, 5, 0:T * E].rearrange("p (t e) -> p t e", t=T),
                                         scalar=1.0, in1=sel[:, :, :], op0=ALU.add, op1=ALU.mult))
            link(v_.tensor_scalar(rankm[:, :, :], rankm[:, :, :], -1.0, None, ALU.add))

            def early(p, n):
                return isinstance(p, int) and p < n

            iota_b = iota_w[:, :].unsqueeze(1).to_broadcast([P, 2, W])

            def make_onehots(p, u):
                if not early(p, 2):
                    dve.wait_ge(s_PTp, p - 1)
                for t in range(T):
                    ranks = rankm[:, t, bass.ds(2 * p, 2)].unsqueeze(2).to_broadcast([P, 2, W])
                    last = v_.tensor_tensor(Pb[:, u, t].rearrange("p (i s) -> p i s", i=2), iota_b, ranks, ALU.is_equal)
                last.then_inc(s_P, 1)

            dve.wait_ge(s_zeroed, 128)
            make_onehots(0, 0)
            make_onehots(1, 1)
            unit_lo(1, 1, 1, 1)
            link(v_.tensor_copy(gwb[:, :, :, 0], gw[:, :, :]))
            link(v_.tensor_tensor(gw_r[:, :, :], gw[:, :, :], gwb[:, :, :, 0], ALU.subtract))
            link(v_.tensor_copy(gwb[:, :, :, 1], gw_r[:, :, :]))
            link(v_.tensor_tensor(gw_r[:, :, :], gw_r[:, :, :], gwb[:, :, :, 1], ALU.subtract))
            v_.tensor_copy(gwb[:, :, :, 2], gw_r[:, :, :]).then_inc(s_route, 1)
            v_.tensor_copy(cnt[:, :], ps[:, 5, T * E:T * E + E]).then_inc(s_sel, 1)

            def two_lo(e, b, slot, done):
                dve.wait_ge(s_2hi, e + 1)
                v_.tensor_tensor(wlo[:, b, U:], raw2[:, slot, :], whi[:, b, U:].bitcast(fp32), ALU.subtract).then_inc(done, 1)

            def gathered_lo(p, u):
                dve.wait_ge(s_xgh, p + 1)
                v_.tensor_tensor(xg[:, u, :, 1:3, :], ps[:, 0, :].rearrange("p (k i s) -> p k i s", k=K, i=2),
                                 xg[:, u, :, 0::3, :].bitcast(fp32), ALU.subtract).then_inc(s_xgl, 1)

            def slot_weights(p):
                dve.wait_ge(s_gsp, p + 1)
                for i in range(2):
                    rows = slice(i * W, (i + 1) * W)
                    last = v_.tensor_reduce(gs[rows, :], ps[rows, 1, MC * P + 3 * i:MC * P + 3 * i + 3], AX, ALU.add)
                last.then_inc(s_gs, 1)

            def y_lo(p):
                dve.wait_ge(s_yh, p + 1)
                v_.tensor_tensor(yy[:, 1, :], ps[:, 4, :], yy[:, 0, :].bitcast(fp32), ALU.subtract).then_inc(s_yl, 1)

            def edge_sums_out():
                dve.wait_ge(s_csps, 1)
                v_.tensor_copy(dup[:, :], ps[:, 5, EC * B:EC * (B + 1)])
                v_.tensor_copy(csum[:, :, :], ps[:, 5, 0:EC * B].rearrange("p (c b) -> p c b", b=B)).then_inc(s_cellsum, 1)
                o = EC * (B + 1)
                v_.tensor_copy(ov_i[:, 0:NOVMAX], ps[:, 5, o:o + NOVMAX])
                v_.tensor_copy(ov_k[:, :], ps[:, 5, o + NOVMAX:o + 2 * NOVMAX]).then_inc(o_done, 1)
                v_.tensor_copy(ov_i[:, NOVMAX:NOVMAX + 1], oincl[:, E - 1:E]).then_inc(s_ovtab, 1)

            def pair(p, j, last=False, twos=False):
                u = j % 2
                at, nxt = 2 * u, 2 * (1 - u)

                def add_parts(i):
                    dve.wait_ge(s_cross, 2 * p + i + 1)
                    rows = slice(i * W, (i + 1) * W)
                    v_.tensor_tensor(act13[rows, :], act13[rows, :], ps[rows, 2 + i, :], ALU.add).then_inc(s_sum, 1)

                add_parts(0)
                if not last:
                    unit_lo(2 * p + 2, 0, nxt, 0)
                if early(p, 1):
                    add_parts(1)
                if not last:
                    unit_lo(2 * p + 2, 0, nxt, 1)
                if not early(p, 1):
                    add_parts(1)
                dve.wait_ge(s_gs, p + 1)
                dve.wait_ge(s_sg, p + 1)
                v_.scalar_tensor_tensor(out=hid, in0=act13[:, M:2 * M], scalar=gs[:, 0:1], in1=sg,
                                        op0=ALU.mult, op1=ALU.mult).then_inc(s_hid, 1)
                if not last:
                    gathered_lo(p + 1, 1 - u)
                    unit_lo(2 * p + 3, 1, nxt + 1, 0)
                if twos:
                    two_lo(2 * p, 0, at, s_2last if last else s_2lo)
                if isinstance(p, int) and p == PR * EDGE_ROUND - 1:
                    edge_sums_out()
                if not early(p, 1):
                    y_lo(p - 1)
                dve.wait_ge(s_Th, p + 1)
                v_.tensor_tensor(own_slots(hiT[:, 1]), ps[:, 1, 0:MC * P].rearrange("p (m i s) -> p m i s", m=MC, i=2),
                                 own_slots(hiT[:, 0]).bitcast(fp32), ALU.subtract).then_inc(s_Tl, 1)
                if not last:
                    unit_lo(2 * p + 3, 1, nxt + 1, 1)
                    slot_weights(p + 1)
                if twos:
                    two_lo(2 * p + 1, 1, at + 1, s_2last if last else s_2lo)

            def round_(r, last=False):
                for j in range(PR):
                    p = r * PR + j
                    pair(p, j, last and j == PR - 1, twos=early(p, 2) or (last and j == PR - 1))
                    if not (last and j >= PR - 2):
                        make_onehots(p + 2, j % 2)

            def list_windows():
                dve.wait_ge(s_sel, 2)
                link(v_.tensor_scalar(ovc[:, :], cnt[:, :], float(W), None, ALU.is_gt))
                for q in range(2, N // W):
                    link(v_.scalar_tensor_tensor(out=ovc[:, :], in0=cnt[:, :], scalar=float(W * q), in1=ovc[:, :],
                                                 op0=ALU.is_gt, op1=ALU.add))
                link(v_.tensor_tensor_scan(out=oincl[:, :], data0=ones[:, 0:E], data1=ovc[:, :], initial=0.0,
                                           op0=ALU.mult, op1=ALU.add))
                link(v_.tensor_scalar(osel[:, :], oincl[:, :], pidx[:, 0:1], None, ALU.is_le))
                link(v_.tensor_reduce(ov_e[:, :], osel[:, :], AX, ALU.add))
                link(v_.tensor_tensor(osel[:, :], osel[:, :], ovc[:, :], ALU.mult))
                link(v_.tensor_reduce(ov_m[:, :], osel[:, :], AX, ALU.add))
                link(v_.tensor_tensor(ov_m[:, :], pidx[:, :], ov_m[:, :], ALU.subtract))
                link(v_.tensor_scalar(ov_m[:, :], ov_m[:, :], 1.0, float(W), ALU.add, ALU.mult))
                v_.tensor_scalar(ov_d[:, 0:NOVMAX], ident[:, 0:NOVMAX], ov_e[:, 0:1], None, ALU.mult)
                v_.tensor_scalar(ov_d[:, NOVMAX:], ident[:, 0:NOVMAX], ov_m[:, 0:1], None, ALU.mult).then_inc(s_ovd, 1)
                dve.wait_ge(s_coef, 1)
                link(v_.tensor_copy(coef3[:, :, 0, :], coef[:, :, :]))
                link(v_.tensor_tensor(coef[:, :, :], coef[:, :, :], coef3[:, :, 0, :], ALU.subtract))
                link(v_.tensor_copy(coef3[:, :, 1, :], coef[:, :, :]))
                link(v_.tensor_tensor(coef[:, :, :], coef[:, :, :], coef3[:, :, 1, :], ALU.subtract))
                v_.tensor_copy(coef3[:, :, 2, :], coef[:, :, :]).then_inc(s_ovd, 1)

            slot_weights(0)
            gathered_lo(0, 0)
            list_windows()
            round_(0)
            with dve.Fori(EDGE_ROUND, ROUNDS - 1) as r:
                round_(r)
            round_(ROUNDS - 1, last=True)

            def unit_lo_late(e):
                for half in range(2):
                    unit_lo(e, e % 2, e % NRING, half)

            def cells_lo(b):
                dve.wait_ge(s_ahi, b + 1)
                v_.tensor_tensor(cells(wlo, b), atab[:, :, :, b], cells(whi, b).bitcast(fp32), ALU.subtract).then_inc(s_alo, 1)

            unit_lo_late(E)
            y_lo(NP - 1)
            unit_lo_late(E + 1)

            dve.wait_ge(s_ovtab, 1)
            nov = dve.value_load(ov_i[0:1, NOVMAX:NOVMAX + 1], min_val=0, max_val=NOVMAX - 1)
            dve.wait_ge(s_comb, NP)
            with dve.If(nov > 0):
                with dve.Fori(0, nov) as v:
                    e = dve.value_load(ov_i[0:1, bass.ds(v, 1)], min_val=0, max_val=E - 1)
                    for t in range(T):
                        last = v_.scalar_tensor_tensor(
                            out=Pb[:, 0, t, 0:W], in0=rankm[:, t, bass.ds(e, 1)].to_broadcast([P, W]),
                            scalar=ov_k[:, bass.ds(v, 1)], in1=iota_w[:, :], op0=ALU.subtract, op1=ALU.is_equal)
                    last.then_inc(o_P, 1)
                    dve.wait_ge(o_xgp, v + 1)
                    v_.tensor_reduce(gs[0:W, :], ps[0:W, 1, MC * P:MC * P + 3], AX, ALU.add).then_inc(o_gs, 1)
                    dve.wait_ge(o_gs, v + 1)
                    dve.wait_ge(o_silu, v + 1)
                    v_.scalar_tensor_tensor(out=hid[0:W, :], in0=ps[0:W, 2, M:2 * M], scalar=gs[0:W, 0:1], in1=sg[0:W, :],
                                            op0=ALU.mult, op1=ALU.mult).then_inc(o_hh, 1)
                    dve.wait_ge(o_down, v + 1)
                    v_.tensor_copy(yw[0:W, :], ps[0:W, 4, :]).then_inc(o_y, 1)
                    dve.wait_ge(o_done, v + 2)

            dve.wait_ge(s_comb, NP)
            for t in range(T):
                link(v_.tensor_tensor(xcur[:, t, :], xcur[:, t, :], ps[:, 6 + t, :], ALU.add))
            norm_stats()
            for t in range(T):
                v_.tensor_scalar(h[:, t, :], xcur[:, t, :], mv[:, t, 0:1], rstd[:, t:t + 1],
                                 ALU.subtract, ALU.mult).then_inc(s_h2, 1)
            for t in range(T):
                dve.wait_ge(s_h2hi, t + 1)
                v_.tensor_tensor(h2s[:, 1, t], h[:, t, :], h2s[:, 0, t].bitcast(fp32), ALU.subtract).then_inc(s_h2lo, 1)
            cells_lo(1)
            dve.wait_ge(s_b1, 16)
            for t in range(T):
                link(v_.tensor_tensor(xcur[:, t, :], xcur[:, t, :], bias1_sb[:, :], ALU.add))
            link(v_.memset(above[:, :, 0:1], 1.0))
            link(v_.memset(above[:, :, NBIN:NBIN + 1], 0.0))
            def split_next(b):
                if b + 2 < B + NBIN:
                    unit_lo_late(E + b + 2)

            def links_lo(b):
                dve.wait_ge(s_zhi, b + 1)
                v_.tensor_tensor(zz[:, b % 2, 1], ps[:, 2 * (b % 2):2 * (b % 2) + 2, :].rearrange("p a (k n) -> p (a k) n", k=2),
                                 zz[:, b % 2, 0].bitcast(fp32), ALU.subtract).then_inc(s_zlo, 1)

            links_lo(0)
            for b in range(B):
                if b + 1 < B:
                    links_lo(b + 1)
                if b + 2 < B:
                    cells_lo(b + 2)
                if b + 1 < B:
                    split_next(b)
            for t in range(T):
                dve.wait_ge(s_rel_out, t + 1)
                link(v_.tensor_tensor(xcur[:, t, :], xcur[:, t, :], ps[:, 4 + t, :], ALU.add))
                link(v_.bn_stats(stats[:, t, :], xcur[:, t, :]))
            norm_stats(begun=True)
            for t in range(T):
                v_.tensor_scalar(h[:, t, :], xcur[:, t, :], mv[:, t, 0:1], rstd[:, t:t + 1],
                                 ALU.subtract, ALU.mult).then_inc(s_h3, 1)
            dve.wait_ge(s_h3, T)
            for t in range(T):
                link(v_.tensor_scalar(above[:, t, 1:NBIN], bins[:, 1:NBIN], h[:, t, 0:1], None, ALU.is_lt))
            v_.tensor_tensor(binm[:, :, :], above[:, :, 0:NBIN], above[:, :, 1:NBIN + 1], ALU.subtract).then_inc(s_mb, 1)
            dve.wait_ge(s_mrow, 2)
            v_.tensor_copy(mrow[:, 0:2, :], ps[:, 0, :].rearrange("p (b n) -> p b n", b=2)).then_inc(s_mrow_first, 1)

            def masked(b, part, done):
                if b >= 2:
                    dve.wait_ge(s_mrow_sb, b // 2)
                    dve.wait_ge(s_uused, E + B + b - 1)
                v_.tensor_tensor(zz[:, b % 2, part], hT3[:, part].bitcast(fp32),
                                 mrow[:, b, :].unsqueeze(1).to_broadcast([P, K, N]), ALU.mult).then_inc(done, 1)

            dve.wait_ge(s_mrow_first, 1)
            dve.wait_ge(s_h3Tsb, 1)
            masked(0, 0, s_hm)
            v_.tensor_tensor(hT3[:, 1], ps[:, 4:6, :].rearrange("p a (k n) -> p (a k) n", k=2),
                             hT3[:, 0].bitcast(fp32), ALU.subtract).then_inc(s_h3Tsb, 1)
            dve.wait_ge(s_h3Tsb, 2)
            masked(0, 1, s_hml_first)
            split_next(B - 1)
            for b in range(NBIN):
                if b + 1 < NBIN:
                    masked(b + 1, 0, s_hm)
                split_next(B + b)
            for t in range(T):
                dve.wait_ge(s_bin_out, t + 1)
                v_.tensor_tensor(xcur[:, t, :], xcur[:, t, :], ps[:, 6 + t, :], ALU.add).then_inc(s_fin, 1)

        @block.tensor
        def _(pe):
            mm = nc.tensor.matmul
            tr = nc.tensor.transpose

            def transpose_h(bank, done, ready=None):
                for t in range(T):
                    if ready is not None:
                        pe.wait_ge(ready, t + 1)
                    for k in range(K):
                        o = (k % 2) * N + t * P
                        last = tr(ps[:, bank + k // 2, o:o + P], h[:, t, k::K], ident[:, :])
                last.then_inc(done, 1)

            pe.wait_ge(s_const, 1)
            pe.wait_ge(s_h0, 1)
            transpose_h(6, s_T0)
            def count(c):
                pe.wait_ge(s_onehot, c + 1)
                for t in range(T):
                    last = mm(ps[:, 2 + t, 0:N], S1[:, c % NH, t * P:(t + 1) * P], D1[:, c % NH, :],
                              start=c == 0, stop=c == EC - 1)
                last.then_inc(s_ohread, 1)

            for c in range(NH):
                count(c)
            pe.wait_ge(s_T0sb, 1)
            pe.wait_ge(s_w0, 16)
            for t in range(T):
                for k in range(K):
                    last = mm(ps[:, t, :], hT[:, k, t * P:(t + 1) * P], w0_sb[:, k, :],
                              start=k == 0, stop=k == K - 1)
                last.then_inc(s_y0, 1)
            pe.wait_ge(s_gate, 16)
            for k in range(K):
                last = tr(ps[:, 4, k * E:(k + 1) * E], gate_sb[:, k::K], ident[0:E, 0:E])
            last.then_inc(s_gT, 1)
            for c in range(NH, EC):
                count(c)
            pe.wait_ge(s_lk, 1)
            for t in range(T):
                for st in range(T):
                    last = tr(ps[:, 6, t * N + st * P:t * N + (st + 1) * P], links[:, st, t * P:(t + 1) * P], ident[:, :])
            last.then_inc(s_lkT, 1)
            pe.wait_ge(s_relh, 1)
            pe.wait_ge(s_wcb, 1)
            for c in range(EC):
                for i in range(3):
                    last = mm(ps[:, 5, c * B:(c + 1) * B], relh_c[:, c, :], wcb[:, i, :], start=i == 0, stop=i == 2)
            last.then_inc(s_coefps, 1)

            def key_rows(g):
                if g >= 2:
                    pe.wait_ge(s_keyrow_sb, g - 1)
                for c in range(4 * g, min(4 * g + 4, EC)):
                    last = mm(ps[:, g % 2, (c % 4) * P:(c % 4 + 1) * P], key[:, c:c + 1].to_broadcast([P, P]),
                              ident[:, :], start=True, stop=True)
                last.then_inc(s_keyrow, 1)

            pe.wait_ge(s_y0sb, T)
            key_rows(0)
            key_rows(1)
            pe.wait_ge(s_adj, 1)
            for t in range(T):
                for st in range(T):
                    pe.wait_ge(s_y0d, st + 1)
                    last = mm(ps[:, 6 + t, :], adj[:, st, t * P:(t + 1) * P], y0[:, st, :],
                              start=st == 0, stop=st == T - 1)
                last.then_inc(s_o0, 1)
            for g in range(2, (EC + 3) // 4):
                key_rows(g)
            pe.wait_ge(s_h1, 1)
            transpose_h(2, s_hT)
            pe.wait_ge(s_hTsb, 2)
            pe.wait_ge(s_gTsb, 1)
            for t in range(T):
                for k in range(K):
                    last = mm(ps[:, 4, t * E:(t + 1) * E], hT[:, k, t * P:(t + 1) * P], gT[:, k, :],
                              start=k == 0, stop=k == K - 1)
            last.then_inc(s_logit, 1)
            def keep_clock_up(n):
                for _ in range(n):
                    mm(ps[:, 0, :], identb[:, :], hb[:, 0, 0, :], start=True, stop=True)

            pe.wait_ge(s_keyrow_sb, (EC + 3) // 4)
            pe.wait_ge(s_h1st, 1)
            keep_clock_up(24)
            pe.wait_ge(s_sel, 1)
            pe.wait_ge(s_coef, 1)
            mm(ps[:, 5, 0:E], before[:, :], sel[:, 0, :], start=True, stop=True)
            mm(ps[:, 5, E:2 * E], before[:, :], sel[:, 1, :], start=True, stop=False)
            mm(ps[:, 5, E:2 * E], ones[:, :], sel[:, 0, :], start=False, stop=True)
            mm(ps[:, 5, 2 * E:3 * E], ones[:, :], sel[:, 0, :], start=True, stop=False)
            mm(ps[:, 5, 2 * E:3 * E], ones[:, :], sel[:, 1, :], start=False, stop=True).then_inc(s_rank, 1)

            def split_product(out_, pairs, n, start=True, stop=True):
                for k in range(n):
                    (xh, xl), (wh, wl) = pairs(k)
                    mm(out_, xh, wh, start=start and k == 0, stop=False, skip_group_check=True)
                    mm(out_, xh, wl, start=False, stop=False, skip_group_check=True)
                    last = mm(out_, xl, wh, start=False, stop=stop and k == n - 1, skip_group_check=True)
                return last

            def gather(p, u):
                pe.wait_ge(s_P, p + 1)
                for k in range(K):
                    for i in range(3):
                        for t in range(T):
                            last = mm(ps[:, 0, k * P:(k + 1) * P], hb[:, i, t, k::K], Pb[:, u, t, :],
                                      start=i == 0 and t == 0, stop=i == 2 and t == T - 1)
                last.then_inc(s_xgp, 1)

            def weights(p, u):
                for t in range(T):
                    last = mm(ps[:, 1, MC * P:MC * P + 6], Pb[:, u, t, :],
                              gwb[:, t, bass.ds(2 * p, 2), :].rearrange("p e i -> p (e i)"),
                              start=t == 0, stop=t == T - 1, skip_group_check=True)
                last.then_inc(s_gsp, 1)

            def units(b, half, c):
                return [w[:, b, 0:U].rearrange("p (a k m) -> p a k m", a=2, k=K)[:, :, c, :] for w in (whi, wlo)]

            def up(p, u, i):
                pe.wait_ge(s_ulo, 2 * (2 * p + i) + 2)
                for k in range(K):
                    tokens = xg[:, u, k, 2 * i:2 * i + 2, :].rearrange("p q s -> p (q s)")
                    for part, w in enumerate(units(i, 0, k)):
                        last = mm(ps[:, 2 + i, :], tokens, w, start=k == 0 and part == 0, stop=k == K - 1 and part == 1)
                last.then_inc(s_uused, 1)

            def down(p, i):
                if isinstance(p, int) and p == NP - 1:
                    pe.wait_ge(s_2last, i + 1)
                else:
                    pe.wait_ge(s_2lo, 2 * p + i + 1)
                cols = slice(i * W, i * W + P)
                split_product(ps[:, 4, :], lambda m: ([hiT[:, h_, m, cols] for h_ in range(2)],
                                                      [w[:, i, U + m * D:U + (m + 1) * D] for w in (whi, wlo)]),
                              MC, start=i == 0, stop=i == 1).then_inc(s_used, 1)

            def combine(p, u, start):
                pe.wait_ge(s_yl, p + 1)
                pe.wait_ge(s_PT, p + 1)
                for t in range(T):
                    for h_ in range(2):
                        last = mm(ps[:, 6 + t, :], PT[:, u, t, :], yy[:, h_, :], start=start and h_ == 0, stop=True,
                                  skip_group_check=True)
                last.then_inc(s_comb, 1)

            def edge_sums():
                pe.wait_ge(s_eq, 1)
                pe.wait_ge(s_ovd, 2)
                pe.wait_ge(s_PT, PR * EDGE_ROUND - 1)
                for c in range(EC):
                    for i in range(3):
                        last = mm(ps[:, 5, c * B:(c + 1) * B], eq[:, c, :], coef3[:, c, i, :], start=i == 0, stop=i == 2)
                for c in range(EC):
                    last = mm(ps[:, 5, EC * B + c:EC * B + c + 1], eqb[:, c, :], onesb[:, :], start=True, stop=True)
                o = EC * (B + 1)
                mm(ps[:, 5, o:o + 2 * NOVMAX], ones[:, :], ov_d[:, :], start=True, stop=True).then_inc(s_csps, 1)

            def round_(r, last=False):
                for j in range(PR):
                    p = r * PR + j
                    u = j % 2
                    edges_now = isinstance(p, int) and p == PR * EDGE_ROUND - 1
                    first = isinstance(p, int) and p == 0
                    more = not (last and j == PR - 1)
                    pe.wait_ge(s_xgl, p + 1)
                    up(p, u, 0)
                    if not (isinstance(p, int) and p < 2):
                        combine(p - 2, u, isinstance(p, int) and p == 2)
                    up(p, u, 1)
                    if more:
                        gather(p + 1, 1 - u)
                    if edges_now:
                        edge_sums()
                    if not first:
                        pe.wait_ge(s_Tl, p)
                        down(p - 1, 0)
                        down(p - 1, 1)
                    pe.wait_ge(s_hid, p + 1)
                    if more:
                        weights(p + 1, 1 - u)
                    for m in range(MC):
                        last_t = tr(ps[:, 1, m * P:(m + 1) * P], hid[:, m::MC], ident[:, :])
                    last_t.then_inc(s_T, 1)
                    if not first:
                        pe.wait_ge(s_PT, p)
                    if edges_now:
                        pe.wait_ge(s_cellsum, 1)
                        pe.wait_ge(o_done, 1)
                    for t in range(T):
                        last_t = mm(ps[:, 5, t * P:(t + 1) * P], Pb[:, u, t, :], identb[:, :], start=True, stop=True)
                    last_t.then_inc(s_PTp, 1)

            pe.wait_ge(s_hb, 1)
            gather(0, 0)
            pe.wait_ge(s_route, 1)
            weights(0, 0)
            pe.wait_ge(s_const, 2)
            pe.wait_ge(s_sel, 2)
            round_(0)
            with pe.Fori(EDGE_ROUND, ROUNDS - 1) as r:
                round_(r)
            round_(ROUNDS - 1, last=True)
            combine(NP - 2, NP % 2, False)
            pe.wait_ge(s_Tl, NP)
            down(NP - 1, 0)
            down(NP - 1, 1)
            combine(NP - 1, (NP - 1) % 2, False)

            pe.wait_ge(s_ovtab, 1)
            nov = pe.value_load(ov_i[0:1, NOVMAX:NOVMAX + 1], min_val=0, max_val=NOVMAX - 1)
            with pe.If(nov > 0):
                with pe.Fori(0, nov) as v:
                    one = bass.ds(pe.value_load(ov_i[0:1, bass.ds(v, 1)], min_val=0, max_val=E - 1), 1)
                    pe.wait_ge(o_P, v + 1)
                    for t in range(T):
                        mm(ps[0:W, 5, t * P:(t + 1) * P], Pb[:, 0, t, 0:W], identb[:, :], start=True, stop=True)
                    for t in range(T):
                        mm(ps[0:W, 1, MC * P:MC * P + 3], Pb[:, 0, t, 0:W], gwb[:, t, one, :].rearrange("p e i -> p (e i)"),
                           start=t == 0, stop=t == T - 1, skip_group_check=True)
                    for k in range(K):
                        for i in range(3):
                            for t in range(T):
                                last = mm(ps[:, 0, k * W:(k + 1) * W], hb[:, i, t, k::K], Pb[:, 0, t, 0:W],
                                          start=i == 0 and t == 0, stop=i == 2 and t == T - 1)
                    last.then_inc(o_xgp, 1)
                    pe.wait_ge(o_w, 48 * (v + 1))
                    pe.wait_ge(o_xg, v + 1)
                    w13 = extra[:, 0:U].rearrange("p (a k m) -> p a k m", a=2, k=K)
                    for k in range(K):
                        last = mm(ps[0:W, 2, :], xw[:, k, :], w13[:, :, k, :], start=k == 0, stop=k == K - 1)
                    last.then_inc(o_up, 1)
                    pe.wait_ge(o_hh, v + 1)
                    for m in range(MC):
                        last = tr(ps[:, 1, m * P:(m + 1) * P], hid[:, m::MC], ident[:, :])
                    last.then_inc(o_T, 1)
                    pe.wait_ge(o_Tc, v + 1)
                    for m in range(MC):
                        last = mm(ps[0:W, 4, :], hw[:, m, :], extra[:, U + m * D:U + (m + 1) * D],
                                  start=m == 0, stop=m == MC - 1)
                    last.then_inc(o_down, 1)
                    pe.wait_ge(o_y, v + 1)
                    for t in range(T):
                        last = mm(ps[:, 6 + t, :], PTw[0:W, t * P:(t + 1) * P], yw[0:W, :], start=False, stop=True,
                                  skip_group_check=True)
                    last.then_inc(o_done, 1)

            def unit_parts(e, k):
                return [w[:, e % 2, k * D:(k + 1) * D] for w in (whi, wlo)]

            keep_clock_up(30)

            def z_place(b, k):
                return ps[:, 2 * (b % 2) + k // 2, (k % 2) * N:(k % 2 + 1) * N]

            def first_links_product():
                pe.wait_ge(s_ahi, 1)
                pe.wait_ge(s_alo_first, 1)
                for st in range(T):
                    pe.wait_ge(s_h2hi, st + 1)
                    for k in range(K):
                        for w in (whi, wlo):
                            mm(z_place(0, k), h2s[:, 0, st, k::K], cells(w, 0)[:, st, :], start=st == 0 and w is whi and k % 2 == 0,
                               stop=False, skip_group_check=True)
                for st in range(T):
                    pe.wait_ge(s_h2lo, st + 1)
                    for k in range(K):
                        last = mm(z_place(0, k), h2s[:, 1, st, k::K], cells(whi, 0)[:, st, :], start=False,
                                  stop=st == T - 1, skip_group_check=True)
                last.then_inc(s_zp, 1)

            def links_product(b):
                if b >= 1:
                    pe.wait_ge(s_alo, b)
                if b >= 2:
                    pe.wait_ge(s_zlo, b - 1)
                for k in range(K):
                    last = split_product(z_place(b, k), lambda st: ([h2s[:, h_, st, k::K] for h_ in range(2)],
                                                                    [cells(w, b)[:, st, :] for w in (whi, wlo)]), T)
                last.then_inc(s_zp, 1)

            first_links_product()
            for b in range(B):
                if b + 1 < B:
                    links_product(b + 1)
                pe.wait_ge(s_zlo, b + 1)
                pe.wait_ge(s_ulo, 2 * (E + b) + 2)
                for t in range(T):
                    last = split_product(ps[:, 4 + t, :],
                                         lambda k: ([zz[:, b % 2, h_, k, t * P:(t + 1) * P] for h_ in range(2)], unit_parts(b, k)),
                                         K, start=b == 0, stop=b == B - 1)
                    if b == B - 1:
                        last.then_inc(s_rel_out, 1)
                if b < B - 1:
                    last.then_inc(s_uused, 1)
                else:
                    mm(ps[:, 0, 0:1], identb[:, :], onesb[:, :], start=True, stop=True).then_inc(s_uused, 1)

            keep_clock_up(20)
            transpose_h(4, s_h3T, ready=s_h3)
            pe.wait_ge(s_mb, 1)
            for b in range(NBIN):
                for t in range(T):
                    last = mm(ps[:, b // 2, (b % 2) * N + t * P:(b % 2) * N + (t + 1) * P],
                              binm[:, t, b:b + 1].to_broadcast([P, P]), identb[:, :], start=True, stop=True)
                last.then_inc(s_mrow, 1)
            pe.wait_ge(s_hm, 1)
            pe.wait_ge(s_ulo, 2 * (E + B) + 2)
            for t in range(T):
                for k in range(K):
                    for i, w in enumerate(unit_parts(0, k)):
                        mm(ps[:, 6 + t, :], zz[:, 0, 0, k, t * P:(t + 1) * P], w, start=k == 0 and i == 0, stop=False,
                           skip_group_check=True)
            pe.wait_ge(s_hml_first, 1)
            for t in range(T):
                for k in range(K):
                    last = mm(ps[:, 6 + t, :], zz[:, 0, 1, k, t * P:(t + 1) * P], unit_parts(0, k)[0], start=False,
                              stop=False, skip_group_check=True)
            last.then_inc(s_uused, 1)
            for b in range(1, NBIN):
                pe.wait_ge(s_hm, b + 1)
                pe.wait_ge(s_hml, b)
                pe.wait_ge(s_ulo, 2 * (E + B + b) + 2)
                for t in range(T):
                    last = split_product(ps[:, 6 + t, :],
                                         lambda k: ([zz[:, b % 2, h_, k, t * P:(t + 1) * P] for h_ in range(2)], unit_parts(b, k)),
                                         K, start=False, stop=b == NBIN - 1)
                    if b == NBIN - 1:
                        last.then_inc(s_bin_out, 1)
                if b < NBIN - 1:
                    last.then_inc(s_uused, 1)



_INS = ["x", "src", "dst", "edge_type_32", "edge_weight1", "L0_gnn_weight", "L0_gnn_bias", "L0_ffn_gate_w",
        "L0_ffn_gate_b", "L0_ffn_w1", "L0_ffn_w3", "L0_ffn_w2", "L1_gnn_bases", "L1_gnn_w_comp",
        "L1_gnn_h_bias", "L1_ffn_W"]


def kernel(**inputs):
    import numpy as _np
    import concourse.bacc as _bacc
    from concourse import mybir as _mybir
    from concourse.bass_utils import run_bass_kernel_spmd as _run

    nc = _bacc.Bacc("TRN2", target_bir_lowering=False, num_devices=1)
    arrays, args = {}, []
    for name in _INS:
        a = _np.ascontiguousarray(inputs[name])
        arrays[f"in_{name}_dram"] = a
        args.append(nc.dram_tensor(f"in_{name}_dram", a.shape, _mybir.dt.from_np(a.dtype), kind="ExternalInput").ap())
    n, d = arrays["in_x_dram"].shape
    res = nc.dram_tensor("out_0_dram", (n, d), _mybir.dt.float32, kind="ExternalOutput").ap()
    build(nc, *args, res)
    r = _run(nc, [arrays], core_ids=[0])
    return r.results[0]["out_0_dram"]
```
